# Optimizing a Trainium2 kernel written in Bass

```python
import numpy as np
import jax
import jax.numpy as jnp

def _softmax(x, axis=-1):
    return jax.nn.softmax(x, axis=axis)
def _gelu(x):
    return jax.nn.gelu(x, approximate=True)
def _silu(x):
    return jax.nn.silu(x)
def _sigmoid(x):
    return jax.nn.sigmoid(x)
def _layernorm(x, axis=-1, eps=1e-5):
    m = jnp.mean(x, axis=axis, keepdims=True)
    v = jnp.var(x, axis=axis, keepdims=True)
    return (x - m) / jnp.sqrt(v + eps)
def _scatter_add(tgt, idx, src, axis=0):
    return tgt.at[idx].add(src)
def _segment_sum(src, seg, n):
    return jax.ops.segment_sum(src, seg, n)

kernel_name = 'mk_conv_seq_d4_conv_nchw192_85d34d'

def setup_inputs(seed: int = 0):
    np.random.seed(seed)
    _w = jnp.asarray
    def _rec_inputs():
        import jax
        import jax.numpy as jnp
        _gk = jax.random.key(seed)
        x = -0.0006872 + 1.001 * jax.random.normal(jax.random.fold_in(_gk, 1), (4, 192, 56, 56), jnp.float32)
        return x
    x = _rec_inputs()
    def _L0_conv_setup():
        import jax, jax.numpy as jnp
        import numpy as np
        DIM = 192
        HEADS = 6
        HD = DIM // HEADS
        WIN = 7
        K = WIN * WIN
        B, H, W = (4, 56, 56)
        EPS = 1e-05
        PAD = WIN // 2

        def _conv1x1(x, w, b):
            return jnp.einsum('bchw,oc->bohw', x, w) + b[None, :, None, None]
        key = jax.random.key(seed)
        ks = jax.random.split(key, 8)

        def n(k, shape, scale=0.02):
            return jax.random.normal(k, shape, dtype=jnp.float32) * scale
        return {'x': jax.random.normal(ks[0], (B, DIM, H, W), dtype=jnp.float32), 'bn_gamma': jnp.ones((DIM,), jnp.float32), 'bn_beta': jnp.zeros((DIM,), jnp.float32), 'qkv_w': n(ks[1], (3 * DIM, DIM)), 'qkv_b': jnp.zeros((3 * DIM,), jnp.float32), 'dm_w': n(ks[2], (K, 2 * HD, WIN, WIN)), 'dm_b': jnp.zeros((K,), jnp.float32), 'rel_bias': n(ks[3], (K, HEADS)), 'proj_w': n(ks[4], (DIM, DIM)), 'proj_b': jnp.zeros((DIM,), jnp.float32), 'c1_w': n(ks[5], (4 * DIM, DIM)), 'c1_b': jnp.zeros((4 * DIM,), jnp.float32), 'c2_w': n(ks[6], (DIM, 4 * DIM)), 'c2_b': jnp.zeros((DIM,), jnp.float32)}
    _L0_conv_all = _L0_conv_setup()
    _L0_conv_in = {k: v for k, v in _L0_conv_all.items() if k in ('bn_gamma', 'bn_beta', 'qkv_w', 'qkv_b', 'dm_w', 'dm_b', 'rel_bias', 'proj_w', 'proj_b', 'c1_w', 'c1_b', 'c2_w', 'c2_b', )}
    del _L0_conv_all

    def _L1_conv_setup():
        import jax, jax.numpy as jnp
        import numpy as np
        C = 192
        DCT = 7
        EPS = 1e-05
        LOW_X = [0, 0, 1, 1, 0, 2, 2, 1, 2, 0, 3, 4, 0, 1, 3, 0, 1, 2, 3, 4, 5, 0, 1, 2, 3, 4, 5, 6, 1, 2, 3, 4]
        LOW_Y = [0, 1, 0, 1, 2, 0, 1, 2, 2, 3, 0, 0, 4, 3, 1, 5, 4, 3, 2, 1, 0, 6, 5, 4, 3, 2, 1, 0, 6, 5, 4, 3]

        def _dct_basis():
            t = jnp.arange(DCT, dtype=jnp.float32)
            fx = jnp.array(LOW_X, dtype=jnp.float32)
            fy = jnp.array(LOW_Y, dtype=jnp.float32)

            def bf(freq):
                r = jnp.cos(jnp.pi * freq[:, None] * (t[None, :] + 0.5) / DCT) / jnp.sqrt(jnp.float32(DCT))
                return jnp.where(freq[:, None] == 0, r, r * jnp.sqrt(jnp.float32(2.0)))
            bx, by = (bf(fx), bf(fy))
            return bx[:, :, None] * by[:, None, :]
        key = jax.random.key(seed)
        ks = jax.random.split(key, 16)
        n, h, w = (64, 56, 56)
        return {'x': jax.random.normal(ks[0], (n, C, h, w), jnp.float32), 'wg1': jax.random.normal(ks[1], (32, C), jnp.float32) * (2.0 / C) ** 0.5, 'bn2_g': jax.random.uniform(ks[2], (32,), jnp.float32, 0.8, 1.2), 'bn2_b': jax.random.normal(ks[3], (32,), jnp.float32) * 0.1, 'bn2_m': jax.random.normal(ks[4], (32,), jnp.float32) * 0.1, 'bn2_v': jax.random.uniform(ks[5], (32,), jnp.float32, 0.5, 1.5), 'wg2': jax.random.normal(ks[6], (32, 32), jnp.float32) * (2.0 / 32) ** 0.5, 'bg2': jax.random.normal(ks[7], (32,), jnp.float32) * 0.1, 'beta': jax.random.uniform(ks[8], (1,), jnp.float32, 0.05, 0.25), 'w1d': jax.random.normal(ks[9], (C, C, 3), jnp.float32) * (2.0 / (3 * C)) ** 0.5, 'b1d': jax.random.normal(ks[10], (C,), jnp.float32) * 0.1, 'bn1_g': jax.random.uniform(ks[11], (C,), jnp.float32, 0.8, 1.2), 'bn1_b': jax.random.normal(ks[12], (C,), jnp.float32) * 0.1, 'bn1_m': jax.random.normal(ks[13], (C,), jnp.float32) * 0.1, 'bn1_v': jax.random.uniform(ks[14], (C,), jnp.float32, 0.5, 1.5)}
    _L1_conv_all = _L1_conv_setup()
    _L1_conv_in = {k: v for k, v in _L1_conv_all.items() if k in ('wg1', 'bn2_g', 'bn2_b', 'bn2_m', 'bn2_v', 'wg2', 'bg2', 'beta', 'w1d', 'b1d', 'bn1_g', 'bn1_b', 'bn1_m', 'bn1_v', )}
    del _L1_conv_all

    def _L2_conv_setup():
        import jax, jax.numpy as jnp
        import numpy as np
        DIM = 192
        HEADS = 6
        WS = 8
        OVERLAP = 2
        PAD = 3
        STRIDE = WS - OVERLAP
        HID = DIM * 4
        _coords = np.stack(np.meshgrid(np.arange(WS), np.arange(WS), indexing='ij'), 0).reshape(2, -1)
        _rel = (_coords[:, :, None] - _coords[:, None, :]).transpose(1, 2, 0).astype(np.int64)
        _rel[..., 0] += WS - 1
        _rel[..., 1] += WS - 1
        _rel[..., 0] *= 2 * WS - 1
        REL_IDX = jnp.asarray(_rel.sum(-1).reshape(-1))

        def _ln_c(x, g, b):
            mu = jnp.mean(x, axis=1, keepdims=True)
            var = jnp.mean((x - mu) ** 2, axis=1, keepdims=True)
            return (x - mu) * jax.lax.rsqrt(var + 1e-05) * g[:, None, None] + b[:, None, None]

        def _conv1x1(x, w, b):
            return jnp.einsum('bchw,oc->bohw', x, w) + b[:, None, None]

        def _dwconv3(x, w, b):
            y = jax.lax.conv_general_dilated(x, w, (1, 1), ((1, 1), (1, 1)), feature_group_count=x.shape[1], dimension_numbers=('NCHW', 'OIHW', 'NCHW'))
            return y + b[:, None, None]

        def _unfold(x, k, s, p):
            B, C, H, W = x.shape
            xp = jnp.pad(x, ((0, 0), (0, 0), (p, p), (p, p)))
            Lh = (H + 2 * p - k) // s + 1
            Lw = (W + 2 * p - k) // s + 1
            ih = (jnp.arange(Lh) * s)[:, None] + jnp.arange(k)
            iw = (jnp.arange(Lw) * s)[:, None] + jnp.arange(k)
            t = xp[:, :, ih, :][:, :, :, :, iw]
            t = t.transpose(0, 1, 3, 5, 2, 4)
            return t.reshape(B, C * k * k, Lh * Lw)

        def _fold(cols, h, w, k, s, p):
            B = cols.shape[0]
            Lh = (h + 2 * p - k) // s + 1
            Lw = (w + 2 * p - k) // s + 1
            C = cols.shape[1] // (k * k)
            t = cols.reshape(B, C, k, k, Lh, Lw).transpose(0, 1, 4, 2, 5, 3)
            ih = (jnp.arange(Lh) * s)[:, None] + jnp.arange(k)
            iw = (jnp.arange(Lw) * s)[:, None] + jnp.arange(k)
            out = jnp.zeros((B, C, h + 2 * p, w + 2 * p), cols.dtype)
            out = out.at[:, :, ih[:, :, None, None], iw[None, None, :, :]].add(t)
            return out[:, :, p:p + h, p:p + w]

        def _reverse(win, h, w):
            B, L, nH, ws2, ch = win.shape
            cols = win.transpose(0, 2, 4, 3, 1).reshape(B, nH * ch * ws2, L)
            return _fold(cols, h, w, WS, STRIDE, PAD)

        def _hft(x, w, b):
            B, C, h, ww = x.shape
            a = 3.0 * x
            for s in (2, 4, 8):
                pool = x.reshape(B, C, h // s, s, ww // s, s).mean(axis=(3, 5))
                a = a - jnp.repeat(jnp.repeat(pool, s, axis=2), s, axis=3)
            return jax.nn.sigmoid(_dwconv3(a, w, b)) * x

        def _forward(x, n1g, n1b, qkv_w, qkv_b, temp, rpb, proj_w, proj_b, hft_w, hft_b, n2g, n2b, fc1_w, fc1_b, sgn_g, sgn_b, sg_w, sg_b, fc2_w, fc2_b):
            B, C, H, W = x.shape
            ch = C // HEADS
            y = _conv1x1(_ln_c(x, n1g, n1b), qkv_w, qkv_b)
            cols = _unfold(y, WS, STRIDE, PAD)
            L = cols.shape[-1]
            win = cols.reshape(B, 3 * HEADS, ch, WS * WS, L).transpose(0, 4, 1, 3, 2)
            q = win[:, :, :HEADS] * temp[None, None]
            k = win[:, :, HEADS:2 * HEADS]
            v = win[:, :, 2 * HEADS:]
            attn = jnp.einsum('blhic,blhjc->blhij', q, k)
            bias = rpb[REL_IDX].reshape(WS * WS, WS * WS, HEADS).transpose(2, 0, 1)
            attn = attn + bias[None, None]
            e = jnp.exp(attn - jnp.max(attn, axis=-1, keepdims=True))
            s = jnp.sum(e, axis=-1, keepdims=True)
            s_img = _reverse(s, H, W)
            o = jnp.einsum('blhij,blhjc->blhic', e, v)
            o_img = _reverse(o, H, W).reshape(B, HEADS, ch, H, W)
            out = (o_img / s_img[:, :, None]).reshape(B, C, H, W)
            out = _hft(_conv1x1(out, proj_w, proj_b), hft_w, hft_b)
            x1 = x + out
            z = jax.nn.gelu(_conv1x1(_ln_c(x1, n2g, n2b), fc1_w, fc1_b), approximate=False)
            z1, z2 = jnp.split(z, 2, axis=1)
            z = z1 * _dwconv3(_ln_c(z2, sgn_g, sgn_b), sg_w, sg_b)
            return x1 + _conv1x1(z, fc2_w, fc2_b)
        key = jax.random.key(seed)
        ks = jax.random.split(key, 8)
        B, Hi, Wi = (4, 128, 128)
        f = jnp.float32
        return {'x': jax.random.normal(ks[0], (B, DIM, Hi, Wi), f), 'n1g': jnp.ones((DIM,), f), 'n1b': jnp.zeros((DIM,), f), 'qkv_w': jax.random.normal(ks[1], (3 * DIM, DIM), f) * 0.02, 'qkv_b': jnp.zeros((3 * DIM,), f), 'temp': jnp.ones((HEADS, 1, 1), f), 'rpb': jax.random.normal(ks[2], ((2 * WS - 1) ** 2, HEADS), f) * 0.02, 'proj_w': jax.random.normal(ks[3], (DIM, DIM), f) * 0.02, 'proj_b': jnp.zeros((DIM,), f), 'hft_w': jax.random.normal(ks[4], (DIM, 1, 3, 3), f) * 0.02, 'hft_b': jnp.zeros((DIM,), f), 'n2g': jnp.ones((DIM,), f), 'n2b': jnp.zeros((DIM,), f), 'fc1_w': jax.random.normal(ks[5], (HID, DIM), f) * 0.02, 'fc1_b': jnp.zeros((HID,), f), 'sgn_g': jnp.ones((HID // 2,), f), 'sgn_b': jnp.zeros((HID // 2,), f), 'sg_w': jax.random.normal(ks[6], (HID // 2, 1, 3, 3), f) * 0.02, 'sg_b': jnp.zeros((HID // 2,), f), 'fc2_w': jax.random.normal(ks[7], (DIM, HID // 2), f) * 0.02, 'fc2_b': jnp.zeros((DIM,), f)}
    _L2_conv_all = _L2_conv_setup()
    _L2_conv_in = {k: v for k, v in _L2_conv_all.items() if k in ('n1g', 'n1b', 'qkv_w', 'qkv_b', 'temp', 'rpb', 'proj_w', 'proj_b', 'hft_w', 'hft_b', 'n2g', 'n2b', 'fc1_w', 'fc1_b', 'sgn_g', 'sgn_b', 'sg_w', 'sg_b', 'fc2_w', 'fc2_b', )}
    del _L2_conv_all

    def _L3_conv_setup():
        import jax, jax.numpy as jnp
        import numpy as np
        B, C, H, W = (8, 192, 64, 64)
        D_INNER = 192
        N_STATE = 4
        DT_RANK = 12
        K_DIRS = 4

        def _ln_cf(x, w, b, eps=1e-05):
            mu = x.mean(1, keepdims=True)
            var = ((x - mu) ** 2).mean(1, keepdims=True)
            return (x - mu) / jnp.sqrt(var + eps) * w[None, :, None, None] + b[None, :, None, None]

        def _selective_scan(u, dt, A, Bv, Cv):

            def step(h, inp):
                dt_t, u_t, B_t, C_t = inp
                dA = jnp.exp(dt_t[..., None] * A)
                h = dA * h + dt_t[..., None] * B_t[:, :, None, :] * u_t[..., None]
                y = jnp.einsum('bkdn,bkn->bkd', h, C_t)
                return (h, y)
            h0 = jnp.zeros(u.shape[:3] + (A.shape[-1],), u.dtype)
            xs = (jnp.moveaxis(dt, -1, 0), jnp.moveaxis(u, -1, 0), jnp.moveaxis(Bv, -1, 0), jnp.moveaxis(Cv, -1, 0))
            _, ys = jax.lax.scan(step, h0, xs)
            return jnp.moveaxis(ys, 0, -1)
        key = jax.random.key(seed)
        ks = jax.random.split(key, 8)
        s = 0.02
        return {'x': jax.random.normal(ks[0], (B, C, H, W), jnp.float32), 'ln_w': jnp.ones((C,), jnp.float32), 'ln_b': jnp.zeros((C,), jnp.float32), 'in_proj_w': jax.random.normal(ks[1], (2 * D_INNER, C), jnp.float32) * s, 'conv_w': jax.random.normal(ks[2], (D_INNER, 1, 3, 3), jnp.float32) * s, 'conv_b': jnp.zeros((D_INNER,), jnp.float32), 'x_proj_w': jax.random.normal(ks[3], (K_DIRS, DT_RANK + 2 * N_STATE, D_INNER), jnp.float32) * s, 'dt_proj_w': jax.random.normal(ks[4], (K_DIRS, D_INNER, DT_RANK), jnp.float32) * s, 'dt_proj_b': jnp.full((K_DIRS, D_INNER), -4.6, jnp.float32), 'A_log': jnp.log(jnp.broadcast_to(jnp.arange(1, N_STATE + 1, dtype=jnp.float32), (K_DIRS, D_INNER, N_STATE))), 'Ds': jnp.ones((K_DIRS, D_INNER), jnp.float32), 'out_norm_w': jnp.ones((D_INNER,), jnp.float32), 'out_norm_b': jnp.zeros((D_INNER,), jnp.float32), 'out_proj_w': jax.random.normal(ks[5], (C, D_INNER), jnp.float32) * s}
    _L3_conv_all = _L3_conv_setup()
    _L3_conv_in = {k: v for k, v in _L3_conv_all.items() if k in ('ln_w', 'ln_b', 'in_proj_w', 'conv_w', 'conv_b', 'x_proj_w', 'dt_proj_w', 'dt_proj_b', 'A_log', 'Ds', 'out_norm_w', 'out_norm_b', 'out_proj_w', )}
    del _L3_conv_all

    return {
        "x": x,
        "L0_conv_bn_gamma": _L0_conv_in["bn_gamma"],
        "L0_conv_bn_beta": _L0_conv_in["bn_beta"],
        "L0_conv_qkv_w": _L0_conv_in["qkv_w"],
        "L0_conv_qkv_b": _L0_conv_in["qkv_b"],
        "L0_conv_dm_w": _L0_conv_in["dm_w"],
        "L0_conv_dm_b": _L0_conv_in["dm_b"],
        "L0_conv_rel_bias": _L0_conv_in["rel_bias"],
        "L0_conv_proj_w": _L0_conv_in["proj_w"],
        "L0_conv_proj_b": _L0_conv_in["proj_b"],
        "L0_conv_c1_w": _L0_conv_in["c1_w"],
        "L0_conv_c1_b": _L0_conv_in["c1_b"],
        "L0_conv_c2_w": _L0_conv_in["c2_w"],
        "L0_conv_c2_b": _L0_conv_in["c2_b"],
        "L1_conv_wg1": _L1_conv_in["wg1"],
        "L1_conv_bn2_g": _L1_conv_in["bn2_g"],
        "L1_conv_bn2_b": _L1_conv_in["bn2_b"],
        "L1_conv_bn2_m": _L1_conv_in["bn2_m"],
        "L1_conv_bn2_v": _L1_conv_in["bn2_v"],
        "L1_conv_wg2": _L1_conv_in["wg2"],
        "L1_conv_bg2": _L1_conv_in["bg2"],
        "L1_conv_beta": _L1_conv_in["beta"],
        "L1_conv_w1d": _L1_conv_in["w1d"],
        "L1_conv_b1d": _L1_conv_in["b1d"],
        "L1_conv_bn1_g": _L1_conv_in["bn1_g"],
        "L1_conv_bn1_b": _L1_conv_in["bn1_b"],
        "L1_conv_bn1_m": _L1_conv_in["bn1_m"],
        "L1_conv_bn1_v": _L1_conv_in["bn1_v"],
        "L2_conv_n1g": _L2_conv_in["n1g"],
        "L2_conv_n1b": _L2_conv_in["n1b"],
        "L2_conv_qkv_w": _L2_conv_in["qkv_w"],
        "L2_conv_qkv_b": _L2_conv_in["qkv_b"],
        "L2_conv_temp": _L2_conv_in["temp"],
        "L2_conv_rpb": _L2_conv_in["rpb"],
        "L2_conv_proj_w": _L2_conv_in["proj_w"],
        "L2_conv_proj_b": _L2_conv_in["proj_b"],
        "L2_conv_hft_w": _L2_conv_in["hft_w"],
        "L2_conv_hft_b": _L2_conv_in["hft_b"],
        "L2_conv_n2g": _L2_conv_in["n2g"],
        "L2_conv_n2b": _L2_conv_in["n2b"],
        "L2_conv_fc1_w": _L2_conv_in["fc1_w"],
        "L2_conv_fc1_b": _L2_conv_in["fc1_b"],
        "L2_conv_sgn_g": _L2_conv_in["sgn_g"],
        "L2_conv_sgn_b": _L2_conv_in["sgn_b"],
        "L2_conv_sg_w": _L2_conv_in["sg_w"],
        "L2_conv_sg_b": _L2_conv_in["sg_b"],
        "L2_conv_fc2_w": _L2_conv_in["fc2_w"],
        "L2_conv_fc2_b": _L2_conv_in["fc2_b"],
        "L3_conv_ln_w": _L3_conv_in["ln_w"],
        "L3_conv_ln_b": _L3_conv_in["ln_b"],
        "L3_conv_in_proj_w": _L3_conv_in["in_proj_w"],
        "L3_conv_conv_w": _L3_conv_in["conv_w"],
        "L3_conv_conv_b": _L3_conv_in["conv_b"],
        "L3_conv_x_proj_w": _L3_conv_in["x_proj_w"],
        "L3_conv_dt_proj_w": _L3_conv_in["dt_proj_w"],
        "L3_conv_dt_proj_b": _L3_conv_in["dt_proj_b"],
        "L3_conv_A_log": _L3_conv_in["A_log"],
        "L3_conv_Ds": _L3_conv_in["Ds"],
        "L3_conv_out_norm_w": _L3_conv_in["out_norm_w"],
        "L3_conv_out_norm_b": _L3_conv_in["out_norm_b"],
        "L3_conv_out_proj_w": _L3_conv_in["out_proj_w"],
    }

def reference(x, L0_conv_bn_gamma, L0_conv_bn_beta, L0_conv_qkv_w, L0_conv_qkv_b, L0_conv_dm_w, L0_conv_dm_b, L0_conv_rel_bias, L0_conv_proj_w, L0_conv_proj_b, L0_conv_c1_w, L0_conv_c1_b, L0_conv_c2_w, L0_conv_c2_b, L1_conv_wg1, L1_conv_bn2_g, L1_conv_bn2_b, L1_conv_bn2_m, L1_conv_bn2_v, L1_conv_wg2, L1_conv_bg2, L1_conv_beta, L1_conv_w1d, L1_conv_b1d, L1_conv_bn1_g, L1_conv_bn1_b, L1_conv_bn1_m, L1_conv_bn1_v, L2_conv_n1g, L2_conv_n1b, L2_conv_qkv_w, L2_conv_qkv_b, L2_conv_temp, L2_conv_rpb, L2_conv_proj_w, L2_conv_proj_b, L2_conv_hft_w, L2_conv_hft_b, L2_conv_n2g, L2_conv_n2b, L2_conv_fc1_w, L2_conv_fc1_b, L2_conv_sgn_g, L2_conv_sgn_b, L2_conv_sg_w, L2_conv_sg_b, L2_conv_fc2_w, L2_conv_fc2_b, L3_conv_ln_w, L3_conv_ln_b, L3_conv_in_proj_w, L3_conv_conv_w, L3_conv_conv_b, L3_conv_x_proj_w, L3_conv_dt_proj_w, L3_conv_dt_proj_b, L3_conv_A_log, L3_conv_Ds, L3_conv_out_norm_w, L3_conv_out_norm_b, L3_conv_out_proj_w):
    import jax
    import jax.numpy as jnp
    def _L0_conv_ref(x, bn_gamma, bn_beta, qkv_w, qkv_b, dm_w, dm_b, rel_bias, proj_w, proj_b, c1_w, c1_b, c2_w, c2_b):
        import jax, jax.numpy as jnp
        import numpy as np
        DIM = 192
        HEADS = 6
        HD = DIM // HEADS
        WIN = 7
        K = WIN * WIN
        B, H, W = (4, 56, 56)
        EPS = 1e-05
        PAD = WIN // 2

        def _conv1x1(x, w, b):
            return jnp.einsum('bchw,oc->bohw', x, w) + b[None, :, None, None]
        Bx, C, Hx, Wx = x.shape
        shortcut = x
        mean = jnp.mean(x, axis=(0, 2, 3), keepdims=True)
        var = jnp.var(x, axis=(0, 2, 3), keepdims=True)
        xn = (x - mean) * jax.lax.rsqrt(var + EPS)
        xn = xn * bn_gamma[None, :, None, None] + bn_beta[None, :, None, None]
        qkv = _conv1x1(xn, qkv_w, qkv_b).reshape(Bx, 3, HEADS, HD, Hx, Wx)
        q, k, v = (qkv[:, 0], qkv[:, 1], qkv[:, 2])
        scale = HD ** (-0.5)
        qk = jnp.concatenate([(q * scale).reshape(Bx * HEADS, HD, Hx, Wx), k.reshape(Bx * HEADS, HD, Hx, Wx)], axis=1)
        attn = jax.lax.conv_general_dilated(qk, dm_w, (1, 1), [(PAD, PAD), (PAD, PAD)], dimension_numbers=('NCHW', 'OIHW', 'NCHW')) + dm_b[None, :, None, None]
        attn = attn.reshape(Bx, HEADS, K, Hx, Wx)
        attn = attn + rel_bias.T[None, :, :, None, None]
        attn = jax.nn.softmax(attn, axis=2)
        patches = jax.lax.conv_general_dilated_patches(v.reshape(Bx * HEADS, HD, Hx, Wx), (WIN, WIN), (1, 1), [(PAD, PAD), (PAD, PAD)], dimension_numbers=('NCHW', 'OIHW', 'NCHW'))
        patches = patches.reshape(Bx, HEADS, HD, K, Hx, Wx)
        out = jnp.einsum('bnckhw,bnkhw->bnchw', patches, attn).reshape(Bx, C, Hx, Wx)
        out = _conv1x1(out, proj_w, proj_b)
        x1 = shortcut + out
        h = _conv1x1(x1, c1_w, c1_b)
        h = jax.nn.gelu(h, approximate=False)
        h = _conv1x1(h, c2_w, c2_b)
        return x1 + h

    def _L1_conv_ref(x, wg1, bn2_g, bn2_b, bn2_m, bn2_v, wg2, bg2, beta, w1d, b1d, bn1_g, bn1_b, bn1_m, bn1_v):
        import jax, jax.numpy as jnp
        import numpy as np
        C = 192
        DCT = 7
        EPS = 1e-05
        LOW_X = [0, 0, 1, 1, 0, 2, 2, 1, 2, 0, 3, 4, 0, 1, 3, 0, 1, 2, 3, 4, 5, 0, 1, 2, 3, 4, 5, 6, 1, 2, 3, 4]
        LOW_Y = [0, 1, 0, 1, 2, 0, 1, 2, 2, 3, 0, 0, 4, 3, 1, 5, 4, 3, 2, 1, 0, 6, 5, 4, 3, 2, 1, 0, 6, 5, 4, 3]

        def _dct_basis():
            t = jnp.arange(DCT, dtype=jnp.float32)
            fx = jnp.array(LOW_X, dtype=jnp.float32)
            fy = jnp.array(LOW_Y, dtype=jnp.float32)

            def bf(freq):
                r = jnp.cos(jnp.pi * freq[:, None] * (t[None, :] + 0.5) / DCT) / jnp.sqrt(jnp.float32(DCT))
                return jnp.where(freq[:, None] == 0, r, r * jnp.sqrt(jnp.float32(2.0)))
            bx, by = (bf(fx), bf(fy))
            return bx[:, :, None] * by[:, None, :]
        n, c, h, w = x.shape
        g = jnp.einsum('nchw,oc->nohw', x, wg1)
        g = (g - bn2_m[None, :, None, None]) * (bn2_g / jnp.sqrt(bn2_v + EPS))[None, :, None, None] + bn2_b[None, :, None, None]
        g = jax.nn.relu(g).mean(axis=(2, 3))
        xg = g @ wg2.T + bg2
        xg = jax.nn.relu(jnp.tanh(xg)) + beta
        xg0 = jax.lax.stop_gradient(xg[0])
        s = xg0.sum()
        p_mid = jnp.round(xg0[:31] / s * c)
        param = jnp.concatenate([jnp.zeros(1, jnp.float32), p_mid, (jnp.float32(c) - p_mid.sum())[None]])
        ch = jnp.arange(c, dtype=jnp.float32)
        basis = _dct_basis()
        filt = jnp.zeros((c, DCT, DCT), jnp.float32)
        for i in range(32):
            m = (ch >= param[i]) & (ch < param[i + 1])
            filt = jnp.where(m[:, None, None], basis[i], filt)
        xp = x.reshape(n, c, DCT, h // DCT, DCT, w // DCT).mean(axis=(3, 5))
        y = jnp.sum(xp * filt[None], axis=(2, 3))
        y = y @ w1d[:, :, 1].T + b1d
        y = (y - bn1_m) * (bn1_g / jnp.sqrt(bn1_v + EPS)) + bn1_b
        y = jax.nn.relu(y)
        return x * y[:, :, None, None] + x

    def _L2_conv_ref(x, n1g, n1b, qkv_w, qkv_b, temp, rpb, proj_w, proj_b, hft_w, hft_b, n2g, n2b, fc1_w, fc1_b, sgn_g, sgn_b, sg_w, sg_b, fc2_w, fc2_b):
        import jax, jax.numpy as jnp
        import numpy as np
        DIM = 192
        HEADS = 6
        WS = 8
        OVERLAP = 2
        PAD = 3
        STRIDE = WS - OVERLAP
        HID = DIM * 4
        _coords = np.stack(np.meshgrid(np.arange(WS), np.arange(WS), indexing='ij'), 0).reshape(2, -1)
        _rel = (_coords[:, :, None] - _coords[:, None, :]).transpose(1, 2, 0).astype(np.int64)
        _rel[..., 0] += WS - 1
        _rel[..., 1] += WS - 1
        _rel[..., 0] *= 2 * WS - 1
        REL_IDX = jnp.asarray(_rel.sum(-1).reshape(-1))

        def _ln_c(x, g, b):
            mu = jnp.mean(x, axis=1, keepdims=True)
            var = jnp.mean((x - mu) ** 2, axis=1, keepdims=True)
            return (x - mu) * jax.lax.rsqrt(var + 1e-05) * g[:, None, None] + b[:, None, None]

        def _conv1x1(x, w, b):
            return jnp.einsum('bchw,oc->bohw', x, w) + b[:, None, None]

        def _dwconv3(x, w, b):
            y = jax.lax.conv_general_dilated(x, w, (1, 1), ((1, 1), (1, 1)), feature_group_count=x.shape[1], dimension_numbers=('NCHW', 'OIHW', 'NCHW'))
            return y + b[:, None, None]

        def _unfold(x, k, s, p):
            B, C, H, W = x.shape
            xp = jnp.pad(x, ((0, 0), (0, 0), (p, p), (p, p)))
            Lh = (H + 2 * p - k) // s + 1
            Lw = (W + 2 * p - k) // s + 1
            ih = (jnp.arange(Lh) * s)[:, None] + jnp.arange(k)
            iw = (jnp.arange(Lw) * s)[:, None] + jnp.arange(k)
            t = xp[:, :, ih, :][:, :, :, :, iw]
            t = t.transpose(0, 1, 3, 5, 2, 4)
            return t.reshape(B, C * k * k, Lh * Lw)

        def _fold(cols, h, w, k, s, p):
            B = cols.shape[0]
            Lh = (h + 2 * p - k) // s + 1
            Lw = (w + 2 * p - k) // s + 1
            C = cols.shape[1] // (k * k)
            t = cols.reshape(B, C, k, k, Lh, Lw).transpose(0, 1, 4, 2, 5, 3)
            ih = (jnp.arange(Lh) * s)[:, None] + jnp.arange(k)
            iw = (jnp.arange(Lw) * s)[:, None] + jnp.arange(k)
            out = jnp.zeros((B, C, h + 2 * p, w + 2 * p), cols.dtype)
            out = out.at[:, :, ih[:, :, None, None], iw[None, None, :, :]].add(t)
            return out[:, :, p:p + h, p:p + w]

        def _reverse(win, h, w):
            B, L, nH, ws2, ch = win.shape
            cols = win.transpose(0, 2, 4, 3, 1).reshape(B, nH * ch * ws2, L)
            return _fold(cols, h, w, WS, STRIDE, PAD)

        def _hft(x, w, b):
            B, C, h, ww = x.shape
            a = 3.0 * x
            for s in (2, 4, 8):
                pool = x.reshape(B, C, h // s, s, ww // s, s).mean(axis=(3, 5))
                a = a - jnp.repeat(jnp.repeat(pool, s, axis=2), s, axis=3)
            return jax.nn.sigmoid(_dwconv3(a, w, b)) * x

        def _forward(x, n1g, n1b, qkv_w, qkv_b, temp, rpb, proj_w, proj_b, hft_w, hft_b, n2g, n2b, fc1_w, fc1_b, sgn_g, sgn_b, sg_w, sg_b, fc2_w, fc2_b):
            B, C, H, W = x.shape
            ch = C // HEADS
            y = _conv1x1(_ln_c(x, n1g, n1b), qkv_w, qkv_b)
            cols = _unfold(y, WS, STRIDE, PAD)
            L = cols.shape[-1]
            win = cols.reshape(B, 3 * HEADS, ch, WS * WS, L).transpose(0, 4, 1, 3, 2)
            q = win[:, :, :HEADS] * temp[None, None]
            k = win[:, :, HEADS:2 * HEADS]
            v = win[:, :, 2 * HEADS:]
            attn = jnp.einsum('blhic,blhjc->blhij', q, k)
            bias = rpb[REL_IDX].reshape(WS * WS, WS * WS, HEADS).transpose(2, 0, 1)
            attn = attn + bias[None, None]
            e = jnp.exp(attn - jnp.max(attn, axis=-1, keepdims=True))
            s = jnp.sum(e, axis=-1, keepdims=True)
            s_img = _reverse(s, H, W)
            o = jnp.einsum('blhij,blhjc->blhic', e, v)
            o_img = _reverse(o, H, W).reshape(B, HEADS, ch, H, W)
            out = (o_img / s_img[:, :, None]).reshape(B, C, H, W)
            out = _hft(_conv1x1(out, proj_w, proj_b), hft_w, hft_b)
            x1 = x + out
            z = jax.nn.gelu(_conv1x1(_ln_c(x1, n2g, n2b), fc1_w, fc1_b), approximate=False)
            z1, z2 = jnp.split(z, 2, axis=1)
            z = z1 * _dwconv3(_ln_c(z2, sgn_g, sgn_b), sg_w, sg_b)
            return x1 + _conv1x1(z, fc2_w, fc2_b)
        return _forward(x, n1g, n1b, qkv_w, qkv_b, temp, rpb, proj_w, proj_b, hft_w, hft_b, n2g, n2b, fc1_w, fc1_b, sgn_g, sgn_b, sg_w, sg_b, fc2_w, fc2_b)

    def _L3_conv_ref(x, ln_w, ln_b, in_proj_w, conv_w, conv_b, x_proj_w, dt_proj_w, dt_proj_b, A_log, Ds, out_norm_w, out_norm_b, out_proj_w):
        import jax, jax.numpy as jnp
        import numpy as np
        B, C, H, W = (8, 192, 64, 64)
        D_INNER = 192
        N_STATE = 4
        DT_RANK = 12
        K_DIRS = 4

        def _ln_cf(x, w, b, eps=1e-05):
            mu = x.mean(1, keepdims=True)
            var = ((x - mu) ** 2).mean(1, keepdims=True)
            return (x - mu) / jnp.sqrt(var + eps) * w[None, :, None, None] + b[None, :, None, None]

        def _selective_scan(u, dt, A, Bv, Cv):

            def step(h, inp):
                dt_t, u_t, B_t, C_t = inp
                dA = jnp.exp(dt_t[..., None] * A)
                h = dA * h + dt_t[..., None] * B_t[:, :, None, :] * u_t[..., None]
                y = jnp.einsum('bkdn,bkn->bkd', h, C_t)
                return (h, y)
            h0 = jnp.zeros(u.shape[:3] + (A.shape[-1],), u.dtype)
            xs = (jnp.moveaxis(dt, -1, 0), jnp.moveaxis(u, -1, 0), jnp.moveaxis(Bv, -1, 0), jnp.moveaxis(Cv, -1, 0))
            _, ys = jax.lax.scan(step, h0, xs)
            return jnp.moveaxis(ys, 0, -1)
        R = dt_proj_w.shape[-1]
        N = A_log.shape[-1]
        xn = _ln_cf(x, ln_w, ln_b)
        xz = jnp.einsum('dc,bchw->bdhw', in_proj_w, xn)
        xc, z = jnp.split(xz, 2, axis=1)
        xc = jax.lax.conv_general_dilated(xc, conv_w, (1, 1), 'SAME', feature_group_count=xc.shape[1])
        xc = jax.nn.silu(xc + conv_b[None, :, None, None])
        Bsz, D, Hh, Ww = xc.shape
        L = Hh * Ww
        x_hw = xc.reshape(Bsz, D, L)
        x_wh = xc.transpose(0, 1, 3, 2).reshape(Bsz, D, L)
        xs = jnp.stack([x_hw, x_wh, x_hw[..., ::-1], x_wh[..., ::-1]], axis=1)
        x_dbl = jnp.einsum('kcd,bkdl->bkcl', x_proj_w, xs)
        dts, Bv, Cv = jnp.split(x_dbl, [R, R + N], axis=2)
        dt = jnp.einsum('kdr,bkrl->bkdl', dt_proj_w, dts) + dt_proj_b[None, :, :, None]
        dt = jax.nn.softplus(dt)
        A = -jnp.exp(A_log)
        ys = _selective_scan(xs, dt, A, Bv, Cv) + Ds[None, :, :, None] * xs
        y = ys[:, 0] + ys[:, 2, :, ::-1] + ys[:, 1].reshape(Bsz, D, Ww, Hh).transpose(0, 1, 3, 2).reshape(Bsz, D, L) + ys[:, 3, :, ::-1].reshape(Bsz, D, Ww, Hh).transpose(0, 1, 3, 2).reshape(Bsz, D, L)
        y = y.reshape(Bsz, D, Hh, Ww)
        y = _ln_cf(y, out_norm_w, out_norm_b)
        y = y * jax.nn.silu(z)
        out = jnp.einsum('cd,bdhw->bchw', out_proj_w, y)
        return x + out

    def _gn(v, G=32, eps=1e-5):
        B_, C_, H_, W_ = v.shape
        g = v.reshape(B_, G, C_ // G, H_, W_)
        m = jnp.mean(g, axis=(2, 3, 4), keepdims=True)
        s = jnp.var(g, axis=(2, 3, 4), keepdims=True)
        return ((g - m) / jnp.sqrt(s + eps)).reshape(v.shape)

    def _ln_c(v, eps=1e-6):
        m = jnp.mean(v, axis=1, keepdims=True)
        s = jnp.var(v, axis=1, keepdims=True)
        return (v - m) / jnp.sqrt(s + eps)

    def _ln_t(v, eps=1e-5):
        m = jnp.mean(v, axis=-1, keepdims=True)
        s = jnp.var(v, axis=-1, keepdims=True)
        return (v - m) / jnp.sqrt(s + eps)

    def _to_tokens(v):
        B_, C_, H_, W_ = v.shape
        return v.reshape(B_, C_, H_ * W_).transpose(0, 2, 1)
    def _from_tokens(t, like):
        B_, C_, H_, W_ = like.shape
        return t.transpose(0, 2, 1).reshape(B_, C_, H_, W_)

    x = _L0_conv_ref(x, L0_conv_bn_gamma, L0_conv_bn_beta, L0_conv_qkv_w, L0_conv_qkv_b, L0_conv_dm_w, L0_conv_dm_b, L0_conv_rel_bias, L0_conv_proj_w, L0_conv_proj_b, L0_conv_c1_w, L0_conv_c1_b, L0_conv_c2_w, L0_conv_c2_b)
    x = _L1_conv_ref(x, L1_conv_wg1, L1_conv_bn2_g, L1_conv_bn2_b, L1_conv_bn2_m, L1_conv_bn2_v, L1_conv_wg2, L1_conv_bg2, L1_conv_beta, L1_conv_w1d, L1_conv_b1d, L1_conv_bn1_g, L1_conv_bn1_b, L1_conv_bn1_m, L1_conv_bn1_v)
    x = _L2_conv_ref(x, L2_conv_n1g, L2_conv_n1b, L2_conv_qkv_w, L2_conv_qkv_b, L2_conv_temp, L2_conv_rpb, L2_conv_proj_w, L2_conv_proj_b, L2_conv_hft_w, L2_conv_hft_b, L2_conv_n2g, L2_conv_n2b, L2_conv_fc1_w, L2_conv_fc1_b, L2_conv_sgn_g, L2_conv_sgn_b, L2_conv_sg_w, L2_conv_sg_b, L2_conv_fc2_w, L2_conv_fc2_b)
    x = _L3_conv_ref(x, L3_conv_ln_w, L3_conv_ln_b, L3_conv_in_proj_w, L3_conv_conv_w, L3_conv_conv_b, L3_conv_x_proj_w, L3_conv_dt_proj_w, L3_conv_dt_proj_b, L3_conv_A_log, L3_conv_Ds, L3_conv_out_norm_w, L3_conv_out_norm_b, L3_conv_out_proj_w)
    return x


_drawn_inputs = setup_inputs


def setup_inputs(seed=0):
    import zlib

    import numpy as np

    out = dict(_drawn_inputs(seed))
    spreads = {'L0_conv_bn_gamma': (1.0, 0.6),
     'L0_conv_bn_beta': (0.0, 0.8),
     'L0_conv_qkv_b': (0.0, 0.274),
     'L0_conv_dm_b': (0.0, 0.8),
     'L0_conv_proj_b': (0.0, 0.1),
     'L0_conv_c1_b': (0.0, 0.1),
     'L0_conv_c2_b': (0.0, 0.1),
     'L2_conv_n1g': (1.0, 0.6),
     'L2_conv_n1b': (0.0, 0.8),
     'L2_conv_qkv_b': (0.0, 0.658),
     'L2_conv_temp': (1.0, 0.6),
     'L2_conv_proj_b': (0.0, 0.1),
     'L2_conv_hft_b': (0.0, 0.8),
     'L2_conv_n2g': (1.0, 0.6),
     'L2_conv_n2b': (0.0, 0.8),
     'L2_conv_fc1_b': (0.0, 0.8),
     'L2_conv_sgn_g': (1.0, 0.6),
     'L2_conv_sgn_b': (0.0, 0.8),
     'L2_conv_sg_b': (0.0, 0.8),
     'L2_conv_fc2_b': (0.0, 0.1),
     'L3_conv_ln_w': (1.0, 0.6),
     'L3_conv_ln_b': (0.0, 0.8),
     'L3_conv_conv_b': (0.0, 0.1),
     'L3_conv_dt_proj_b': (-4.599999904632568, 0.6),
     'L3_conv_Ds': (1.0, 0.6),
     'L3_conv_out_norm_w': (1.0, 0.6),
     'L3_conv_out_norm_b': (0.0, 0.8)}
    factors = {'L0_conv_qkv_w': 4.19,
     'L0_conv_dm_w': 8.0,
     'L0_conv_rel_bias': 8.0,
     'L1_conv_wg1': 5.452,
     'L1_conv_bn2_g': 6.619,
     'L1_conv_bn2_b': 8.0,
     'L1_conv_bn2_m': 4.476,
     'L1_conv_bn2_v': 4.825,
     'L1_conv_wg2': 3.084,
     'L1_conv_bg2': 8.0,
     'L1_conv_bn1_g': 3.839,
     'L1_conv_bn1_v': 3.213,
     'L2_conv_qkv_w': 7.833,
     'L2_conv_rpb': 8.0,
     'L2_conv_proj_w': 4.275,
     'L2_conv_hft_w': 8.0,
     'L2_conv_fc1_w': 8.0,
     'L2_conv_sg_w': 8.0,
     'L2_conv_fc2_w': 8.0,
     'L3_conv_conv_w': 8.0,
     'L3_conv_x_proj_w': 8.0,
     'L3_conv_dt_proj_w': 8.0,
     'L3_conv_A_log': 8.0}
    for name, (base, spread) in spreads.items():
        noise = np.random.default_rng([zlib.crc32(name.encode()), seed]).standard_normal(out[name].shape)
        drawn = base * np.exp(spread * noise) if base else spread * noise
        out[name] = jnp.asarray(drawn.astype(out[name].dtype))
    for name, factor in factors.items():
        out[name] = (out[name] * factor).astype(out[name].dtype)
    return out
```

```python
from contextlib import ExitStack, contextmanager
import concourse.bass as bass
from concourse import mybir
F32 = mybir.dt.float32
BF16 = mybir.dt.bfloat16
ALU = mybir.AluOpType
ACT = mybir.ActivationFunctionType
AX = mybir.AxisListType
B, C, H, W = 4, 192, 56, 56
N = H * W
G = 96
NCH = 7
CH = 8 * W
PW = 62
PN = PW * PW
HD = 32
EPS = 1e-5

NU = 6
TAPS = 49
K1 = 10
NS = 5
NT = 14
MB = 28
G_TAPS = [k for k in range(TAPS) if k % 5 in (0, 2, 4)]
D_TAPS = [k for k in range(TAPS) if k % 5 in (1, 3)]
NSTEP = NCH * TAPS
SLOTS = 17 * MB
AGG_SLOT = [12 + a * (SLOTS - 14) // NSTEP for a in range(NSTEP)]
NGA = (len(G_TAPS) - 1) * NCH
NDA = (len(D_TAPS) - 1) * NCH
GR, DR = 6, 2
F = 4 * C
DCT = 7
LOW_X = [0, 0, 1, 1, 0, 2, 2, 1, 2, 0, 3, 4, 0, 1, 3, 0, 1, 2, 3, 4, 5, 0, 1, 2, 3, 4, 5, 6, 1, 2, 3, 4]
LOW_Y = [0, 1, 0, 1, 2, 0, 1, 2, 2, 3, 0, 0, 4, 3, 1, 5, 4, 3, 2, 1, 0, 6, 5, 4, 3, 2, 1, 0, 6, 5, 4, 3]
NF = 32
ROUND = 1.5 * 2.0 ** 23
HEADS = 6
WS = 8
STEP = 6
NR = 10
SN = WS * PW
ON = STEP * PW
NP = NR // 2
HID = 4 * C
AW = W + 2
R3 = 3
PLACE = [0, 1, 2, 0, 1, 2, 3]
USES = [PLACE.count(i) for i in range(4)]
LAG = 5
AW = W + 2
R3 = 3
KD, NST, RANK = 4, 4, 12
NBC = 2 * KD * NST
NSEC = 3 * KD
NIT = NSEC * NST
RP = 7
PIECES = [[(0, 0, 0, 128)], [(0, 128, 0, 64), (1, 0, 64, 64)], [(1, 64, 0, 128)]]


@contextmanager
def stage_semaphores(nc):
    held = []

    def sem(name):
        held.append(nc.alloc_semaphore(name))
        return held[-1]
    yield sem
    nc.clear_and_free_semaphores(held)
    nc.all_engine_barrier()


def batchnorm_qkv(nc, x, gamma, beta, qkv_wT, qkv_b, qkvp):
    with ExitStack() as ctx:
        sb = lambda name, shape, dt=F32: ctx.enter_context(nc.sbuf_tensor(name, shape, dt))
        sem = ctx.enter_context(stage_semaphores(nc))
        xs = sb("a_x", [G, 2, B, N])
        wt = sb("a_wt", [G, 2, 3 * C])
        wf = sb("a_wf", [G, 2, 3 * C])
        par = sb("a_par", [G, 2, 2])
        qb = sb("a_qb", [G, 6])
        stats = sb("a_stats", [G, 2, B * NCH, 6])
        mv = sb("a_mv", [G, 2, 2])
        std = sb("a_std", [G, 2])
        sc = sb("a_sc", [G, 2])
        sh = sb("a_sh", [G, 2])
        bias = sb("a_bias", [G, 6])
        zero = sb("a_zero", [G, B * 2, 3 * PW])
        out = [sb(f"a_out{i}", [G, 6, 8, PW]) for i in range(2)]
        ps = [ctx.enter_context(nc.psum_tensor(f"a_ps{i}", [G, 512], F32)) for i in range(4)]
        psb = ctx.enter_context(nc.psum_tensor("a_psb", [G, 512], F32))
        x_loaded = [sem(f"a_x_loaded{b}") for b in range(B)]
        par_loaded = sem("a_par_loaded")
        zero_set = sem("a_zero_set")
        border_stored = sem("a_border_stored")
        stats_done = sem("a_stats_done")
        norm_step = sem("a_norm_step")
        std_done = sem("a_std_done")
        bias_summed = sem("a_bias_summed")
        folded = sem("a_folded")
        product = sem("a_product")
        evacuated_even = sem("a_evacuated_even")
        evacuated_odd = sem("a_evacuated_odd")
        stored = [sem(f"a_stored{i}") for i in range(2)]
        block = ctx.enter_context(nc.Block())
        xv = x.rearrange("b (g p) h w -> b p g (h w)", g=2)
        qv = qkvp.rearrange("t (b g p) h w -> t b p g (h w)", b=B, g=2)

        @block.sync
        def _(sp):
            for b in range(B):
                sp.dma_start(xs[:, :, b, :], xv[b]).then_inc(x_loaded[b], 16)
            sp.dma_start(wt[:, :, :], qkv_wT.rearrange("(g p) o -> p g o", g=2)).then_inc(par_loaded, 16)
            with nc.allow_non_contiguous_dma(reason="per-channel vectors"):
                sp.dma_start(par[:, :, 0], gamma.rearrange("(g p) -> p g", g=2)).then_inc(par_loaded, 16)
                sp.dma_start(par[:, :, 1], beta.rearrange("(g p) -> p g", g=2)).then_inc(par_loaded, 16)
                sp.dma_start(qb[:, :], qkv_b.rearrange("(m p) -> p m", p=G)).then_inc(par_loaded, 16)
            sp.wait_ge(zero_set, 1)
            for t in range(3):
                for r in (0, PW - 3):
                    dst = qkvp[t].rearrange("(n p) h w -> p n (h w)", p=G)[:, :, r * PW:(r + 3) * PW]
                    sp.dma_start(dst, zero[:, :, :]).then_inc(border_stored, 16)
            with sp.Fori(0, B) as b:
                for c in range(NCH):
                    o = c % 2
                    sp.wait_ge(evacuated_even, 3 * NCH * b + 3 * (c + 1))
                    sp.wait_ge(evacuated_odd, 3 * NCH * b + 3 * (c + 1))
                    for t in range(3):
                        sp.dma_start(qv[t, b, :, :, (3 + 8 * c) * PW:(11 + 8 * c) * PW],
                                     out[o][:, 2 * t:2 * t + 2, :, :].rearrange("p g h w -> p g (h w)")
                                     ).then_inc(stored[o], 16)
            sp.wait_ge(stored[0], 16 * 3 * 4 * B)
            sp.wait_ge(stored[1], 16 * 3 * 3 * B)
            sp.wait_ge(border_stored, 16 * 6)

        @block.gpsimd
        def _(pool):
            pool.memset(zero[:, :, :], 0.0).then_inc(zero_set, 1)
            pool.memset(out[0][:, :, :, :], 0.0).then_inc(zero_set, 1)
            pool.memset(out[1][:, :, :, :], 0.0).then_inc(zero_set, 1)

        @block.vector
        def _(v):
            for b in range(B):
                v.wait_ge(x_loaded[b], 16)
                for g in range(2):
                    for c in range(NCH):
                        last = v.bn_stats(stats[:, g, b * NCH + c, :], xs[:, g, b, c * CH:(c + 1) * CH])
            last.then_inc(stats_done, 1)
            v.wait_ge(stats_done, 1)
            for g in range(2):
                v.bn_aggr(mv[:, g, :], stats[:, g, :, :]).then_inc(norm_step, 1)
            v.wait_ge(par_loaded, 64)
            v.wait_ge(std_done, 1)
            v.reciprocal(sc[:, :], std[:, :]).then_inc(norm_step, 1)
            v.wait_ge(norm_step, 3)
            v.tensor_tensor(sc[:, :], sc[:, :], par[:, :, 0], ALU.mult).then_inc(norm_step, 1)
            v.wait_ge(norm_step, 4)
            v.tensor_tensor(sh[:, :], mv[:, :, 0], sc[:, :], ALU.mult).then_inc(norm_step, 1)
            v.wait_ge(norm_step, 5)
            v.tensor_tensor(sh[:, :], par[:, :, 1], sh[:, :], ALU.subtract).then_inc(norm_step, 1)
            for g in range(2):
                v.tensor_scalar(wf[:, g, 0:C], wt[:, g, 0:C], sc[:, g:g + 1], HD ** -0.5, ALU.mult, ALU.mult)
                v.tensor_scalar(wf[:, g, C:], wt[:, g, C:], sc[:, g:g + 1], None, ALU.mult).then_inc(folded, 1)
            v.wait_ge(bias_summed, 1)
            v.tensor_tensor(bias[:, :], psb[:, 0:6], qb[:, :], ALU.add).then_inc(norm_step, 1)
            v.wait_ge(norm_step, 7)
            v.tensor_scalar(bias[:, 0:2], bias[:, 0:2], HD ** -0.5, None, ALU.mult).then_inc(folded, 1)
            v.wait_ge(folded, 3)
            v.wait_ge(zero_set, 3)
            with v.Fori(0, B) as b:
                for c in range(NCH):
                    o = c % 2
                    v.wait_ge(stored[o], 16 * 3 * ((3 if o else 4) * b + c // 2))
                    for m in (1, 3, 5):
                        v.wait_ge(product, 6 * NCH * b + 6 * c + m + 1)
                        v.tensor_scalar(out[o][:, m, :, 3:3 + W],
                                        ps[(6 * c + m) % 4][:, 0:CH].rearrange("p (h w) -> p h w", w=W),
                                        bias[:, m:m + 1], None, ALU.add).then_inc(evacuated_odd, 1)

        @block.scalar
        def _(a):
            a.wait_ge(norm_step, 2)
            a.activation(std[:, :], mv[:, :, 1], ACT.Sqrt, bias=EPS).then_inc(std_done, 1)
            a.wait_ge(folded, 3)
            a.wait_ge(zero_set, 3)
            with a.Fori(0, B) as b:
                for c in range(NCH):
                    o = c % 2
                    a.wait_ge(stored[o], 16 * 3 * ((3 if o else 4) * b + c // 2))
                    for m in (0, 2, 4):
                        a.wait_ge(product, 6 * NCH * b + 6 * c + m + 1)
                        a.activation(out[o][:, m, :, 3:3 + W],
                                     ps[(6 * c + m) % 4][:, 0:CH].rearrange("p (h w) -> p h w", w=W),
                                     ACT.Identity, bias=bias[:, m:m + 1]).then_inc(evacuated_even, 1)

        @block.tensor
        def _(pe):
            pe.wait_ge(norm_step, 6)
            for m in range(6):
                for g in range(2):
                    last = pe.matmul(psb[:, m:m + 1], wt[:, g, m * G:(m + 1) * G], sh[:, g:g + 1],
                                     start=(g == 0), stop=(g == 1))
            last.then_inc(bias_summed, 1)
            pe.wait_ge(folded, 2)
            with pe.Fori(0, B) as b:
                for c in range(NCH):
                    for m in range(6):
                        n = 6 * c + m
                        k = 3 * NCH * b + (n - 4) // 2 + 1
                        if n >= 4:
                            pe.wait_ge(evacuated_odd if m % 2 else evacuated_even, k)
                        else:
                            pe.wait_ge(evacuated_odd if m % 2 else evacuated_even, 3 * NCH * b)
                        for g in range(2):
                            last = pe.matmul(ps[n % 4][:, 0:CH], wf[:, g, m * G:(m + 1) * G],
                                             xs[:, g, b, c * CH:(c + 1) * CH], start=(g == 0), stop=(g == 1))
                        last.then_inc(product, 1)


def window_attention(nc, qkvp, dm_wT, dm_b, rel_bias, sel, ident, att):
    with ExitStack() as ctx:
        sb = lambda name, shape, dt=F32: ctx.enter_context(nc.sbuf_tensor(name, shape, dt))
        pt = lambda name, dt=F32, n=512: ctx.enter_context(nc.psum_tensor(name, [128, n], dt))
        sem = ctx.enter_context(stage_semaphores(nc))
        wdm = sb("b_wdm", [128, 4, 7, 128])
        rel = sb("b_rel", [128, 6])
        dmb = sb("b_dmb", [128, 1])
        mapb = sb("b_mapb", [128, 4, 6])
        curb = sb("b_curb", [128, 4])
        selt = sb("b_sel", [120, K1, 128], BF16)
        idf = sb("b_idf", [128, 128])
        idb = sb("b_idb", [128, 128], BF16)
        qk = [sb(f"b_qk{i}", [128, 61, PW]) for i in range(2)]
        vv = sb("b_v", [128, PW, PW])
        lg = [sb(f"b_lg{i}", [128, 28, W]) for i in range(2)]
        mx = sb("b_mx", [112, 28])
        rs = sb("b_rs", [112, 28])
        rr = sb("b_rr", [112, 28])
        pr = sb("b_pr", [112, 28, TAPS])
        res = sb("b_res", [112, 28, TAPS])
        px = sb("b_px", [112, 28, NS, 4, 3, K1], BF16)
        at = sb("b_at", [120, NS, N], BF16)
        prodg = sb("b_prodg", [128, GR, CH])
        prodd = sb("b_prodd", [128, DR, CH])
        accg = sb("b_accg", [128, N])
        accd = sb("b_accd", [128, N])
        pc = [pt(f"b_pc{i}") for i in range(2)]
        pbc = [pt(f"b_pbc{i}") for i in range(2)]
        ptr = [pt(f"b_ptr{i}") for i in range(2)]
        pbt = [pt(f"b_pbt{i}", BF16, 1024) for i in range(2)]
        const_loaded = sem("b_const_loaded")
        cleared = sem("b_cleared")
        bias_ready = sem("b_bias_ready")
        bias_set = sem("b_bias_set")
        idb_ready = sem("b_idb_ready")
        qk_loaded = [sem(f"b_qk_loaded{i}") for i in range(2)]
        v_loaded = sem("b_v_loaded")
        conv_done = sem("b_conv_done")
        conv_evac = sem("b_conv_evac")
        turned = sem("b_turned")
        max_found = sem("b_max_found")
        centred = sem("b_centred")
        exp_done = sem("b_exp_done")
        sum_step = sem("b_sum_step")
        prob_ready = sem("b_prob_ready")
        hi_ready = sem("b_hi_ready")
        rest_ready = sem("b_rest_ready")
        mid_ready = sem("b_mid_ready")
        lo_ready = sem("b_lo_ready")
        back_turned = sem("b_back_turned")
        back_evac = sem("b_back_evac")
        spread = sem("b_spread")
        weighted = sem("b_weighted")
        dadded = sem("b_dadded")
        gadded = sem("b_gadded")
        combined = sem("b_combined")
        stored = sem("b_stored")
        block = ctx.enter_context(nc.Block())
        qv = qkvp.rearrange("t (n r) h w -> t n r (h w)", r=HD)
        vvd = qkvp[2].rearrange("(u r) h w -> u r (h w)", r=128)
        av = att.rearrange("(u r) n -> u r n", r=128)

        def run(eng, part):
            part(None, 0)
            with eng.Fori(0, NU - 1) as u:
                part(u, u + 1)
            part(NU - 1, None)

        @block.sync
        def _(sp):
            sp.wait_ge(cleared, 2)
            with nc.allow_non_contiguous_dma(reason="weights, once"):
                for s, r, p0, d0, n in ((0, 0, 0, 0, 4), (1, 1, 0, 0, 4), (1, 0, 0, 1, 3), (0, 1, 1, 1, 3)):
                    for i in range(n):
                        sp.dma_start(wdm[64 * s:64 * s + 64, p0 + i, :, 64 * r:64 * r + TAPS],
                                     dm_wT[:, d0 + 2 * i, :, :]).then_inc(const_loaded, 16)
                for r in range(2):
                    sp.dma_start(rel[64 * r:64 * r + TAPS, :], rel_bias).then_inc(const_loaded, 16)
                    sp.dma_start(dmb[64 * r:64 * r + TAPS, :], dm_b.rearrange("(k o) -> k o", o=1)).then_inc(const_loaded, 16)
            sp.dma_start(selt[:, :, :], sel).then_inc(const_loaded, 16)
            sp.dma_start(idf[:, :], ident).then_inc(const_loaded, 16)

            def part(ua, uc):
                if ua is not None:
                    sp.wait_ge(weighted, NSTEP * ua)
                    sp.dma_start(vv[:, :, :].rearrange("p h w -> p (h w)"), vvd[ua]).then_inc(v_loaded, 16)
                for j in range(4):
                    if uc is not None:
                        o = j % 2
                        hidx = 4 * uc + j
                        if ua is not None or j >= 2:
                            sp.wait_ge(conv_done, 16 * uc + 4 * (j - 1))
                        for t in range(2):
                            for s in range(2):
                                sp.dma_start(qk[o][64 * s + 32 * t:64 * s + 32 * t + 32, :, :].rearrange("p h w -> p (h w)"),
                                             qv[t, hidx, :, s * PW:(s + 61) * PW]).then_inc(qk_loaded[o], 16)
                    if ua is not None:
                        for c in ((), (0,), (1, 2), (3, 4, 5, 6))[j]:
                            sp.wait_ge(combined, NCH * ua + c + 1)
                            sp.dma_start(av[ua, :, c * CH:(c + 1) * CH], accg[:, c * CH:(c + 1) * CH]).then_inc(stored, 16)
            run(sp, part)
            sp.wait_ge(stored, 16 * NCH * NU)

        @block.tensor
        def _(pe):
            pe.wait_ge(const_loaded, 16 * 20)
            pe.wait_ge(idb_ready, 1)

            def part(ua, uc):
                step = 0
                for slot in range(SLOTS):
                    n, m = divmod(slot, MB)
                    if uc is not None and n < 16:
                        j, cc = divmod(n, 4)
                        if m == 0:
                            if cc == 0:
                                pe.wait_ge(qk_loaded[j % 2], 64 * (2 * uc + j // 2 + 1))
                            if ua is not None or n >= 2:
                                pe.wait_ge(conv_evac, 16 * uc + n - 1)
                        p, dx = divmod(m, 7)
                        y0 = 14 * cc + 2 * p
                        mm = pe.matmul(pc[n % 2][0:113, 0:392], wdm[:, p, dx, 0:113],
                                       qk[j % 2][:, y0:y0 + 13:2, dx:dx + W], start=(m == 0), stop=(m == MB - 1))
                        if m == MB - 1:
                            mm.then_inc(conv_done, 1)
                    if uc is not None and n >= 4 and n % 4 == 0 and m in (8, 10, 16, 22):
                        j = n // 4 - 1
                        tg = (8, 10, 16, 22).index(m)
                        if tg == 0:
                            pe.wait_ge(conv_evac, 16 * uc + 4 * (j + 1))
                        if ua is not None or 4 * j + tg >= 2:
                            pe.wait_ge(centred, 16 * uc + 4 * j + tg - 1)
                        for t in range(4 * tg, min(4 * tg + 4, NT)):
                            o = (t - 4 * tg) * 128
                            mm = pe.transpose(ptr[tg % 2][0:112, o:o + 113],
                                              lg[j % 2][0:113, 2 * t:2 * t + 2, :].rearrange("p a b -> p (a b)"), idf[0:113, 0:113])
                        mm.then_inc(turned, 1)
                    if ua is not None and n < 4 and m in (1, 5, 9, 13, 17, 21):
                        c, gg = divmod(6 * n + (m - 1) // 4, 3)
                        if c < NCH:
                            q = 3 * c + gg
                            if q == 0:
                                pe.wait_ge(lo_ready, 4 * ua + 4)
                                pe.wait_ge(mid_ready, 4 * ua + 4)
                            pe.wait_ge(back_evac, 21 * ua + (q - 1 if q >= 2 else 0))
                            for s in range(2 * gg, min(2 * gg + 2, NS)):
                                for t2 in range(2):
                                    for r in range(2):
                                        o = (s - 2 * gg) * CH + (4 * t2 + r) * W
                                        mm = pe.transpose(
                                            pbt[q % 2][0:120, o:o + 3 * W].rearrange("p (a b) -> p a b", b=W)[:, 0:3:2, :],
                                            px[:, 2 * (2 * c + t2) + r, s, :, :, :].rearrange("p a b c -> p (a b c)"),
                                            idb[0:112, 0:112])
                            mm.then_inc(back_turned, 1)
                    while ua is not None and step < NSTEP and AGG_SLOT[step] == slot:
                        c, k = divmod(step, TAPS)
                        if k == 0:
                            pe.wait_ge(back_evac, 21 * ua + 3 * c + 3)
                        pe.wait_ge(weighted, NSTEP * ua + (step - 1 if step >= 2 else 0))
                        pe.matmul(pbc[step % 2][:, 0:CH], selt[:, k % K1, :], at[:, k // K1, c * CH:(c + 1) * CH],
                                  start=True, stop=True).then_inc(spread, 1)
                        step += 1
            run(pe, part)

        @block.scalar
        def _(a):
            a.wait_ge(bias_ready, 1)

            def part(ua, uc):
                if uc is not None:
                    a.activation(curb[:, :], mapb[:, :, :].rearrange("p a b -> p (a b)")[:, bass.ds(4 * uc, 4)],
                                 ACT.Copy).then_inc(bias_set, 1)
                    a.wait_ge(bias_set, uc + 1)
                for slot in range(SLOTS):
                    n, m = divmod(slot, MB)
                    if ua is not None and n < 4 and m in (3, 7, 11, 15, 19, 23):
                        c, gg = divmod(6 * n + (m - 3) // 4, 3)
                        if c < NCH:
                            q = 3 * c + gg
                            ns = min(2, NS - 2 * gg)
                            if q == 0:
                                a.wait_ge(spread, NSTEP * ua)
                            a.wait_ge(back_turned, 21 * ua + q + 1)
                            a.activation(at[:, 2 * gg:2 * gg + ns, c * CH:(c + 1) * CH],
                                         pbt[q % 2][0:120, 0:ns * CH].rearrange("p (s n) -> p s n", s=ns),
                                         ACT.Copy).then_inc(back_evac, 1)
                    if uc is not None and n < 16 and m == MB - 1:
                        j, cc = divmod(n, 4)
                        a.wait_ge(conv_done, 16 * uc + n + 1)
                        if cc == 0 and (ua is not None or j >= 2):
                            a.wait_ge(turned, 16 * uc + 4 * (j - 1))
                        a.activation(lg[j % 2][0:113, 7 * cc:7 * cc + 7, :],
                                     pc[n % 2][0:113, 0:392].rearrange("p (a b) -> p a b", b=W), ACT.Identity,
                                     bias=curb[0:113, j:j + 1]).then_inc(conv_evac, 1)
                    if uc is not None and n >= 4:
                        j = n // 4 - 1
                        hidx = 4 * uc + j
                        stage = {(0, 27): "exp", (1, 6): "hi", (1, 14): "mid"}.get((n % 4, m)) if n < 16 else \
                            {24: "exp", 26: "hi", 27: "mid"}.get(m)
                        if stage == "exp":
                            a.wait_ge(centred, 4 * hidx + 4)
                            a.activation(pr[:, :, :], pr[:, :, :], ACT.Exp).then_inc(exp_done, 1)
                        if stage in ("hi", "mid"):
                            part_i = 0 if stage == "hi" else 1
                            src = pr if stage == "hi" else res
                            a.wait_ge(prob_ready if stage == "hi" else rest_ready, hidx + 1)
                            if stage == "hi" and ua is not None:
                                a.wait_ge(back_turned, 21 * uc)
                            a.activation(px[:, :, 0:4, j, part_i, :], src[:, :, 0:40].rearrange("p r (s k) -> p r s k", s=4), ACT.Copy)
                            a.activation(px[:, :, 4, j, part_i, 0:9], src[:, :, 40:49], ACT.Copy)\
                                .then_inc(hi_ready if stage == "hi" else mid_ready, 1)
            run(a, part)

        @block.vector
        def _(v):
            v.memset(wdm[:, :, :, :], 0.0).then_inc(cleared, 1)
            v.memset(rel[:, :], 0.0)
            v.memset(dmb[:, :], 0.0).then_inc(cleared, 1)
            v.memset(px[:, :, :, :, :, :], 0.0).then_inc(cleared, 1)
            v.wait_ge(const_loaded, 16 * 20)
            v.wait_ge(cleared, 3)
            for i in range(4):
                last = v.tensor_scalar(mapb[:, i, :], rel[:, :], dmb[:, 0:1], None, ALU.add)
            last.then_inc(bias_ready, 1)
            v.tensor_copy(idb[:, :], idf[:, :]).then_inc(idb_ready, 1)

            def part(ua, uc):
                step = 0
                pend = None

                def flush():
                    nonlocal pend
                    if pend is not None:
                        stp, i, c = pend
                        v.wait_ge(weighted, NSTEP * ua + stp + 1)
                        v.wait_ge(dadded, NDA * ua + c * (len(D_TAPS) - 1) + i - 1)
                        sl = accd[:, c * CH:(c + 1) * CH]
                        v.tensor_tensor(sl, sl, prodd[:, i % DR, :], ALU.add).then_inc(dadded, 1)
                        pend = None
                for slot in range(SLOTS):
                    n, m = divmod(slot, MB)
                    while ua is not None and step < NSTEP and AGG_SLOT[step] == slot:
                        c, k = divmod(step, TAPS)
                        if step == 0:
                            v.wait_ge(v_loaded, 16 * (ua + 1))
                        v.wait_ge(spread, NSTEP * ua + step + 1)
                        if k in G_TAPS:
                            i = G_TAPS.index(k)
                            if i == 0:
                                out = accg[:, c * CH:(c + 1) * CH]
                                if c == 0:
                                    v.wait_ge(stored, 16 * NCH * ua)
                            else:
                                out = prodg[:, (c * 28 + i - 1) % GR, :]
                                e = c * 28 + i - 1 - GR
                                v.wait_ge(gadded, NGA * ua + (e + 1 if e >= 0 else 0))
                        else:
                            i = D_TAPS.index(k)
                            if i == 0 and c == 0:
                                v.wait_ge(combined, NCH * ua)
                            out = accd[:, c * CH:(c + 1) * CH] if i == 0 else prodd[:, i % DR, :]
                        dy, dx = divmod(k, 7)
                        v.tensor_tensor(out.rearrange("p (h w) -> p h w", w=W),
                                        pbc[step % 2][:, 0:CH].rearrange("p (h w) -> p h w", w=W),
                                        vv[:, 8 * c + dy:8 * c + dy + 8, dx:dx + W], ALU.mult).then_inc(weighted, 1)
                        flush()
                        if k in D_TAPS and D_TAPS.index(k):
                            pend = (step, D_TAPS.index(k), c)
                        if k == TAPS - 1:
                            flush()
                        step += 1
                    if uc is not None and n >= 4:
                        j = n // 4 - 1
                        hidx = 4 * uc + j
                        if n % 4 == 0 and m in (14, 16, 20, 24 if n < 16 else 23):
                            tg = {14: 0, 16: 1, 20: 2}.get(m, 3)
                            nt = min(4, NT - 4 * tg)
                            v.wait_ge(turned, 4 * hidx + tg + 1)
                            src = ptr[tg % 2][0:112, :].rearrange("p (t r k) -> p t r k", t=4, r=2)[:, 0:nt, :, 0:TAPS]
                            mt = mx[:, 8 * tg:8 * tg + 2 * nt]
                            v.tensor_reduce(mt.rearrange("p (t r) -> p t r", r=2), src, AX.X, ALU.max).then_inc(max_found, 1)
                            v.wait_ge(max_found, 4 * hidx + tg + 1)
                            if tg == 0 and (ua is not None or j):
                                v.wait_ge(hi_ready, hidx)
                            v.tensor_tensor(pr[:, 8 * tg:8 * tg + 2 * nt, :].rearrange("p (t r) k -> p t r k", r=2), src,
                                            mt.rearrange("p (t r o) -> p t r o", r=2, o=1).broadcast_to([112, nt, 2, TAPS]),
                                            ALU.subtract).then_inc(centred, 1)
                        stage = {(1, 2): "norm", (1, 10): "rest", (1, 18): "lo"}.get((n % 4, m)) if n < 16 else \
                            {25: "norm", 26: "rest", 27: "lo"}.get(m)
                        if stage == "norm":
                            v.wait_ge(exp_done, hidx + 1)
                            v.tensor_reduce(rs[:, :], pr[:, :, :], AX.X, ALU.add).then_inc(sum_step, 1)
                            v.wait_ge(sum_step, 2 * hidx + 1)
                            v.reciprocal(rr[:, :], rs[:, :]).then_inc(sum_step, 1)
                            v.wait_ge(sum_step, 2 * hidx + 2)
                            v.tensor_tensor(pr[:, :, :], pr[:, :, :], rr[:, :].rearrange("p (r o) -> p r o", o=1).broadcast_to([112, 28, TAPS]),
                                            ALU.mult).then_inc(prob_ready, 1)
                        if stage == "rest":
                            v.wait_ge(hi_ready, hidx + 1)
                            v.tensor_tensor(res[:, :, 0:40].rearrange("p r (s k) -> p r s k", s=4),
                                            pr[:, :, 0:40].rearrange("p r (s k) -> p r s k", s=4), px[:, :, 0:4, j, 0, :], ALU.subtract)
                            v.tensor_tensor(res[:, :, 40:49], pr[:, :, 40:49], px[:, :, 4, j, 0, 0:9], ALU.subtract).then_inc(rest_ready, 1)
                        if stage == "lo":
                            v.wait_ge(mid_ready, hidx + 1)
                            v.wait_ge(rest_ready, hidx + 1)
                            v.tensor_tensor(px[:, :, 0:4, j, 2, :], res[:, :, 0:40].rearrange("p r (s k) -> p r s k", s=4),
                                            px[:, :, 0:4, j, 1, :], ALU.subtract)
                            v.tensor_tensor(px[:, :, 4, j, 2, 0:9], res[:, :, 40:49], px[:, :, 4, j, 1, 0:9], ALU.subtract).then_inc(lo_ready, 1)
            run(v, part)

        @block.gpsimd
        def _(p):
            def part(ua, uc):
                if ua is None:
                    return
                for c in range(NCH):
                    sl = accg[:, c * CH:(c + 1) * CH]
                    for i in range(1, len(G_TAPS)):
                        k = G_TAPS[i]
                        e = c * 28 + i - 1
                        p.wait_ge(weighted, NSTEP * ua + c * TAPS + k + 1)
                        p.wait_ge(gadded, NGA * ua + e)
                        p.tensor_tensor(sl, sl, prodg[:, e % GR, :], ALU.add).then_inc(gadded, 1)
                    p.wait_ge(gadded, NGA * ua + (c + 1) * (len(G_TAPS) - 1))
                    p.wait_ge(dadded, NDA * ua + (c + 1) * (len(D_TAPS) - 1))
                    p.tensor_tensor(sl, sl, accd[:, c * CH:(c + 1) * CH], ALU.add).then_inc(combined, 1)
            run(p, part)


def selector():
    import numpy as np
    s = np.zeros((4, 3, K1, K1, 4, HD), mybir.dt.np(BF16))
    for j in range(4):
        for k in range(K1):
            s[j, :, k, k, j, :] = 1
    return s.reshape(120, K1, 128)


def mixer(nc, x, att, proj_wT, proj_b, c1_wT, c1_b, c2_wT, c2_b, x1p, xp):
    with ExitStack() as ctx:
        sb = lambda name, shape, dt=F32: ctx.enter_context(nc.sbuf_tensor(name, shape, dt))
        pt = lambda name: ctx.enter_context(nc.psum_tensor(name, [G, 512], F32))
        sem = ctx.enter_context(stage_semaphores(nc))
        wp = sb("c_wp", [G, 2, C])
        w1 = sb("c_w1", [G, 2, F])
        w2 = sb("c_w2", [G, 8, C])
        bp = sb("c_bp", [G, 2])
        b1 = sb("c_b1", [G, 8])
        b2 = sb("c_b2", [G, 2])
        xin = [sb(f"c_xin{i}", [G, 2, CH]) for i in range(2)]
        ain = [sb(f"c_ain{i}", [G, 2, CH]) for i in range(2)]
        xa = [sb(f"c_xa{i}", [G, 2, CH]) for i in range(2)]
        hid = [sb(f"c_hid{i}", [G, 8, CH]) for i in range(2)]
        out = [sb(f"c_out{i}", [G, 2, 8, PW]) for i in range(2)]
        pool_sum = sb("c_pool", [G, 2, 7, 7])
        zero = sb("c_zero", [G, 8, 3 * PW])
        pp = [pt(f"c_pp{i}") for i in range(2)]
        p1 = [pt(f"c_p1{i}") for i in range(3)]
        p2 = [pt(f"c_p2{i}") for i in range(2)]
        par_loaded = sem("c_par_loaded")
        in_loaded = [sem(f"c_in_loaded{i}") for i in range(2)]
        cleared = sem("c_cleared")
        border_stored = sem("c_border_stored")
        projected = sem("c_projected")
        added = sem("c_added")
        hidden = sem("c_hidden")
        gelu_done = sem("c_gelu_done")
        mixed = sem("c_mixed")
        finished = sem("c_finished")
        pooled = sem("c_pooled")
        stored = [sem(f"c_stored{i}") for i in range(2)]
        pool_stored = sem("c_pool_stored")
        block = ctx.enter_context(nc.Block())
        xv = x.rearrange("b (g p) h w -> b p g (h w)", g=2)
        av = att.rearrange("(b g p) n -> b p g n", b=B, g=2)
        ov = x1p.rearrange("(b g p) h w -> b p g (h w)", b=B, g=2)

        @block.sync
        def _(sp):
            sp.dma_start(wp[:, :, :], proj_wT.rearrange("(g p) o -> p g o", p=G)).then_inc(par_loaded, 16)
            sp.dma_start(w1[:, :, :], c1_wT.rearrange("(g p) o -> p g o", p=G)).then_inc(par_loaded, 16)
            sp.dma_start(w2[:, :, :], c2_wT.rearrange("(g p) o -> p g o", p=G)).then_inc(par_loaded, 16)
            with nc.allow_non_contiguous_dma(reason="per-channel vectors"):
                sp.dma_start(bp[:, :], proj_b.rearrange("(g p) -> p g", p=G)).then_inc(par_loaded, 16)
                sp.dma_start(b1[:, :], c1_b.rearrange("(g p) -> p g", p=G)).then_inc(par_loaded, 16)
                sp.dma_start(b2[:, :], c2_b.rearrange("(g p) -> p g", p=G)).then_inc(par_loaded, 16)
            with sp.Fori(0, B) as b:
                for c in range(NCH):
                    o = c % 2
                    sp.wait_ge(added, 2 * NCH * b + 2 * max(c - 1, 0))
                    sl = slice(c * CH, (c + 1) * CH)
                    sp.dma_start(ain[o][:, :, :], av[b, :, :, sl]).then_inc(in_loaded[o], 16)
                    sp.dma_start(xin[o][:, :, :], xv[b, :, :, sl]).then_inc(in_loaded[o], 16)

        @block.gpsimd
        def _(p):
            p.memset(zero[:, :, :], 0.0).then_inc(cleared, 1)
            p.memset(out[0][:, :, :, :], 0.0).then_inc(cleared, 1)
            p.memset(out[1][:, :, :, :], 0.0).then_inc(cleared, 1)
            p.wait_ge(cleared, 1)
            for r in (0, PW - 3):
                dst = x1p.rearrange("(n p) h w -> p n (h w)", p=G)[:, :, r * PW:(r + 3) * PW]
                p.dma_start(dst, zero[:, :, :]).then_inc(border_stored, 16)
            with p.Fori(0, B) as b:
                for c in range(NCH):
                    o = c % 2
                    p.wait_ge(finished, 2 * NCH * b + 2 * c + 2)
                    p.dma_start(ov[b, :, :, (3 + 8 * c) * PW:(11 + 8 * c) * PW],
                                out[o][:, :, :, :].rearrange("p g h w -> p g (h w)")).then_inc(stored[o], 16)
                p.wait_ge(pooled, 2 * NCH * (b + 1))
                p.dma_start(xp.rearrange("(b g p) k -> b p g k", b=B, g=2)[b],
                            pool_sum[:, :, :, :].rearrange("p g a b -> p g (a b)")).then_inc(pool_stored, 16)
            p.wait_ge(border_stored, 32)
            p.wait_ge(stored[0], 16 * 4 * B)
            p.wait_ge(stored[1], 16 * 3 * B)
            p.wait_ge(pool_stored, 16 * B)

        @block.tensor
        def _(pe):
            pe.wait_ge(par_loaded, 96)
            with pe.Fori(0, B) as b:
                def project(c):
                    o = c % 2
                    pe.wait_ge(in_loaded[o], 32 * ((3 if o else 4) * b + c // 2 + 1))
                    for m in range(2):
                        pe.wait_ge(added, 2 * NCH * b + max(2 * (c - 1) + m + 1, 0))
                        for g in range(2):
                            mm = pe.matmul(pp[m][:, 0:CH], wp[:, g, m * G:(m + 1) * G], ain[o][:, g, :],
                                           start=(g == 0), stop=(g == 1))
                        mm.then_inc(projected, 1)
                project(0)
                for c in range(NCH):
                    o = c % 2
                    pe.wait_ge(added, 2 * NCH * b + 2 * c + 2)
                    for m in range(8):
                        pe.wait_ge(gelu_done, 8 * NCH * b + max(8 * c + m - 2, 0))
                        for g in range(2):
                            mm = pe.matmul(p1[(8 * c + m) % 3][:, 0:CH], w1[:, g, m * G:(m + 1) * G], xa[o][:, g, :],
                                           start=(g == 0), stop=(g == 1))
                        mm.then_inc(hidden, 1)
                    if c + 1 < NCH:
                        project(c + 1)
                    for m in range(2):
                        pe.wait_ge(finished, 2 * NCH * b + max(2 * (c - 1) + m + 1, 0))
                        for k in range(8):
                            if m == 0:
                                pe.wait_ge(gelu_done, 8 * NCH * b + 8 * c + k + 1)
                            mm = pe.matmul(p2[m][:, 0:CH], w2[:, k, m * G:(m + 1) * G], hid[o][:, k, :],
                                           start=(k == 0), stop=(k == 7))
                        mm.then_inc(mixed, 1)

        @block.scalar
        def _(a):
            with a.Fori(0, B) as b:
                for c in range(NCH):
                    o = c % 2
                    a.wait_ge(mixed, 2 * NCH * b + 2 * max(c - 1, 0))
                    for m in range(8):
                        a.wait_ge(hidden, 8 * NCH * b + 8 * c + m + 1)
                        a.activation(hid[o][:, m, :], p1[(8 * c + m) % 3][:, 0:CH], ACT.Gelu,
                                     bias=b1[:, m:m + 1]).then_inc(gelu_done, 1)

        @block.vector
        def _(v):
            v.wait_ge(par_loaded, 96)
            v.wait_ge(cleared, 3)
            with v.Fori(0, B) as b:
                def add(c):
                    o = c % 2
                    v.wait_ge(hidden, 8 * NCH * b + 8 * max(c - 1, 0))
                    for m in range(2):
                        v.wait_ge(projected, 2 * NCH * b + 2 * c + m + 1)
                        v.scalar_tensor_tensor(xa[o][:, m, :], pp[m][:, 0:CH], bp[:, m:m + 1], xin[o][:, m, :],
                                               ALU.add, ALU.add).then_inc(added, 1)
                add(0)
                for c in range(NCH):
                    o = c % 2
                    if c + 1 < NCH:
                        add(c + 1)
                    v.wait_ge(stored[o], 16 * ((3 if o else 4) * b + c // 2))
                    if c == 0:
                        v.wait_ge(pool_stored, 16 * b)
                    for m in range(2):
                        v.wait_ge(mixed, 2 * NCH * b + 2 * c + m + 1)
                        v.scalar_tensor_tensor(out[o][:, m, :, 3:3 + W], p2[m][:, 0:CH].rearrange("p (h w) -> p h w", w=W),
                                               b2[:, m:m + 1], xa[o][:, m, :].rearrange("p (h w) -> p h w", w=W),
                                               ALU.add, ALU.add).then_inc(finished, 1)
                    for m in range(2):
                        v.wait_ge(finished, 2 * NCH * b + 2 * c + m + 1)
                        v.tensor_reduce(pool_sum[:, m, c, :],
                                        out[o][:, m, :, 3:3 + W].rearrange("p h (a w) -> p a h w", w=8),
                                        AX.XY, ALU.add).then_inc(pooled, 1)


def channel_gate(nc, x1p, xp, wg1T, bn2, wg2T, bg2, beta, w1T, bn1, basis, chan, ident, gate):
    with ExitStack() as ctx:
        sb = lambda name, shape, dt=F32: ctx.enter_context(nc.sbuf_tensor(name, shape, dt))
        pt = lambda name: ctx.enter_context(nc.psum_tensor(name, [128, 512], F32))
        sem = ctx.enter_context(stage_semaphores(nc))
        xin = sb("g_xin", [G, 2, 56, PW])
        w1 = sb("g_w1", [G, 2, NF])
        w2 = sb("g_w2", [NF, NF])
        wo = sb("g_wo", [G, 2, C])
        p2 = sb("g_p2", [NF, 4])
        vb = sb("g_vb", [NF, 2])
        p1 = sb("g_p1", [G, 2, 5])
        bas = sb("g_bas", [NF, 49])
        ch = sb("g_ch", [G, 2])
        idf = sb("g_idf", [128, 128])
        xps = sb("g_xps", [G, B, 2, 49])
        s2 = sb("g_s2", [NF, 2])
        s1 = sb("g_s1", [G, 2, 2])
        act = [sb(f"g_act{i}", [NF, 8, PW]) for i in range(2)]
        gs = sb("g_gs", [NF, 7])
        gm = sb("g_gm", [NF, 4])
        diag = sb("g_diag", [NF, NF])
        ones = sb("g_ones", [NF, G])
        row = sb("g_row", [G, NF])
        tot = sb("g_tot", [G, 2])
        prm = sb("g_prm", [G, NF + 1])
        ge = sb("g_ge", [G, 2, NF + 1])
        lt = sb("g_lt", [G, 2, NF + 1])
        msk = sb("g_msk", [G, 2, NF])
        zer = sb("g_zer", [G, NF])
        suf = sb("g_suf", [G, 2, NF + 1])
        pick = sb("g_pick", [G, 2, NF])
        pickT = sb("g_pickT", [NF, 2, G])
        prod = sb("g_prod", [G, 2, B, 49])
        y0 = sb("g_y0", [G, 2, B])
        yo = sb("g_yo", [G, 2, B])
        pg = [pt(f"g_pg{i}") for i in range(2)]
        ps = pt("g_ps")
        pf = [pt(f"g_pf{i}") for i in range(2)]
        loaded = sem("g_loaded")
        x_loaded = sem("g_x_loaded")
        gate_step = sem("g_gate_step")
        norm_ready = sem("g_norm_ready")
        var_ready = sem("g_var_ready")
        product = sem("g_product")
        activated = sem("g_activated")
        mean_ready = sem("g_mean_ready")
        linear = sem("g_linear")
        mean_step = sem("g_mean_step")
        tanh_done = sem("g_tanh_done")
        diag_ready = sem("g_diag_ready")
        pick_ready = sem("g_pick_ready")
        pick_turned = sem("g_pick_turned")
        pick_copied = sem("g_pick_copied")
        filt_ready = sem("g_filt_ready")
        y0_ready = sem("g_y0_ready")
        y1_ready = sem("g_y1_ready")
        gate_ready = sem("g_gate_ready")
        stored = sem("g_stored")
        block = ctx.enter_context(nc.Block())

        @block.sync
        def _(sp):
            with nc.allow_non_contiguous_dma(reason="small vectors"):
                sp.dma_start(w1[:, :, :], wg1T.rearrange("(g p) o -> p g o", p=G)).then_inc(loaded, 16)
                sp.dma_start(w2[:, :], wg2T).then_inc(loaded, 16)
                sp.dma_start(wo[:, :, :], w1T.rearrange("(g p) o -> p g o", p=G)).then_inc(loaded, 16)
                for i in range(4):
                    sp.dma_start(p2[:, i:i + 1], bn2[i].rearrange("(k o) -> k o", o=1)).then_inc(loaded, 16)
                sp.dma_start(vb[:, 0:1], bg2.rearrange("(k o) -> k o", o=1)).then_inc(loaded, 16)
                sp.dma_start(vb[:, 1:2], beta.partition_broadcast(NF)).then_inc(loaded, 16)
                for i in range(5):
                    sp.dma_start(p1[:, :, i], bn1[i].rearrange("(g p) -> p g", p=G)).then_inc(loaded, 16)
                sp.dma_start(bas[:, :], basis).then_inc(loaded, 16)
                sp.dma_start(ch[:, :], chan).then_inc(loaded, 16)
                sp.dma_start(idf[:, :], ident).then_inc(loaded, 16)
                sp.dma_start(xps[:, :, :, :].rearrange("p b g k -> p (b g) k"), xp.rearrange("(n p) k -> p n k", p=G)).then_inc(loaded, 16)
            sp.dma_start(xin[:, :, :, :].rearrange("p g h w -> p g (h w)"),
                         x1p.rearrange("(b g p) h w -> b p g (h w)", b=B, g=2)[0, :, :, 3 * PW:59 * PW]).then_inc(x_loaded, 16)
            sp.wait_ge(gate_ready, 1)
            sp.dma_start(gate, yo[:, :, :].rearrange("p g b -> p (g b)")).then_inc(stored, 16)
            sp.wait_ge(stored, 16)

        @block.tensor
        def _(pe):
            pe.wait_ge(loaded, 16 * 18)
            pe.wait_ge(x_loaded, 16)
            for c in range(NCH):
                if c >= 2:
                    pe.wait_ge(activated, c - 1)
                for g in range(2):
                    mm = pe.matmul(pg[c % 2][0:NF, 0:8 * PW], w1[:, g, :],
                                   xin[:, g, 8 * c:8 * c + 8, :].rearrange("p h w -> p (h w)"), start=(g == 0), stop=(g == 1))
                mm.then_inc(product, 1)
            pe.wait_ge(mean_ready, 1)
            pe.matmul(ps[0:NF, 0:1], w2[:, :], gm[:, 0:1], start=True, stop=True).then_inc(linear, 1)
            pe.wait_ge(diag_ready, 1)
            pe.matmul(ps[0:G, 0:NF], ones[:, :], diag[:, :], start=True, stop=True).then_inc(linear, 1)
            pe.wait_ge(pick_ready, 1)
            for g in range(2):
                mm = pe.transpose(pg[g][0:NF, 0:G], pick[:, g, :], idf[0:G, 0:G])
            mm.then_inc(pick_turned, 1)
            pe.wait_ge(pick_copied, 1)
            for g in range(2):
                mm = pe.matmul(pf[g][0:G, 0:49], pickT[:, g, :], bas[:, :], start=True, stop=True)
            mm.then_inc(filt_ready, 1)
            pe.wait_ge(y0_ready, 1)
            for m in range(2):
                for g in range(2):
                    mm = pe.matmul(ps[0:G, B * m:B * m + B], wo[:, g, m * G:(m + 1) * G], y0[:, g, :],
                                   start=(g == 0), stop=(g == 1))
            mm.then_inc(y1_ready, 1)

        @block.scalar
        def _(a):
            a.wait_ge(loaded, 16 * 18)
            a.activation(s2[:, 0:1], p2[:, 3:4], ACT.Sqrt, bias=EPS)
            a.activation(s1[:, :, 0], p1[:, :, 3], ACT.Sqrt, bias=EPS).then_inc(var_ready, 1)
            a.wait_ge(norm_ready, 1)
            for c in range(NCH):
                a.wait_ge(product, c + 1)
                if c >= 2:
                    a.wait_ge(mean_step, c - 1)
                a.activation(act[c % 2][:, :, :], pg[c % 2][0:NF, 0:8 * PW].rearrange("p (h w) -> p h w", w=PW), ACT.Relu,
                             bias=s2[:, 1:2], scale=s2[:, 0:1]).then_inc(activated, 1)
            a.wait_ge(linear, 1)
            a.activation(gm[:, 1:2], ps[0:NF, 0:1], ACT.Tanh, bias=vb[:, 0:1]).then_inc(tanh_done, 1)

        @block.vector
        def _(v):
            count = 0

            def link(ins):
                nonlocal count
                count += 1
                ins.then_inc(gate_step, 1)
                v.wait_ge(gate_step, count)

            v.memset(ones[:, :], 1.0)
            v.memset(zer[:, :], 0.0)
            v.memset(prm[:, 0:1], 0.0)
            link(v.memset(suf[:, :, NF:], 1.0))
            v.wait_ge(var_ready, 1)
            link(v.reciprocal(s2[:, 0:1], s2[:, 0:1]))
            link(v.tensor_tensor(s2[:, 0:1], s2[:, 0:1], p2[:, 0:1], ALU.mult))
            link(v.tensor_tensor(s2[:, 1:2], s2[:, 0:1], p2[:, 2:3], ALU.mult))
            v.tensor_tensor(s2[:, 1:2], p2[:, 1:2], s2[:, 1:2], ALU.subtract).then_inc(norm_ready, 1)
            link(v.reciprocal(s1[:, :, 0], s1[:, :, 0]))
            link(v.tensor_tensor(s1[:, :, 0], s1[:, :, 0], p1[:, :, 0], ALU.mult))
            link(v.tensor_tensor(s1[:, :, 1], p1[:, :, 4], p1[:, :, 2], ALU.subtract))
            link(v.tensor_tensor(s1[:, :, 1], s1[:, :, 1], s1[:, :, 0], ALU.mult))
            link(v.tensor_tensor(s1[:, :, 1], s1[:, :, 1], p1[:, :, 1], ALU.add))
            for c in range(NCH):
                v.wait_ge(activated, c + 1)
                v.tensor_reduce(gs[:, c:c + 1], act[c % 2][:, :, 3:3 + W], AX.XY, ALU.add).then_inc(mean_step, 1)
            v.wait_ge(mean_step, NCH)
            link(v.tensor_reduce(gm[:, 0:1], gs[:, :], AX.X, ALU.add))
            v.tensor_scalar(gm[:, 0:1], gm[:, 0:1], 1.0 / N, None, ALU.mult).then_inc(mean_ready, 1)
            v.wait_ge(tanh_done, 1)
            link(v.tensor_scalar(gm[:, 2:3], gm[:, 1:2], 0.0, vb[:, 1:2], ALU.max, ALU.add))
            v.tensor_scalar(diag[:, :], idf[0:NF, 0:NF], gm[:, 2:3], None, ALU.mult).then_inc(diag_ready, 1)
            v.wait_ge(linear, 2)
            link(v.tensor_copy(row[:, :], ps[0:G, 0:NF]))
            link(v.tensor_reduce(tot[:, 0:1], row[:, :], AX.X, ALU.add))
            link(v.reciprocal(tot[:, 0:1], tot[:, 0:1]))
            link(v.tensor_scalar(row[:, :], row[:, :], tot[:, 0:1], None, ALU.mult))
            link(v.tensor_scalar(row[:, :], row[:, :], float(C), None, ALU.mult))
            link(v.tensor_scalar(row[:, :], row[:, :], ROUND, None, ALU.add))
            link(v.tensor_scalar(prm[:, 1:NF], row[:, 0:NF - 1], ROUND, None, ALU.subtract))
            link(v.tensor_reduce(tot[:, 1:2], prm[:, 1:NF], AX.X, ALU.add))
            link(v.tensor_scalar(prm[:, NF:], tot[:, 1:2], -1.0, float(C), ALU.mult, ALU.add))
            for g in range(2):
                v.tensor_scalar(ge[:, g, :], prm[:, :], ch[:, g:g + 1], None, ALU.is_le)
                link(v.tensor_scalar(lt[:, g, :], prm[:, :], ch[:, g:g + 1], None, ALU.is_gt))
            link(v.tensor_tensor(msk[:, :, :], ge[:, :, 0:NF], lt[:, :, 1:], ALU.mult))
            link(v.tensor_scalar(msk[:, :, :], msk[:, :, :], -1.0, 1.0, ALU.mult, ALU.add))
            for g in range(2):
                link(v.tensor_tensor_scan(suf[:, g, NF - 1::-1], msk[:, g, ::-1], zer[:, :], 1.0, ALU.mult, ALU.add))
            v.tensor_tensor(pick[:, :, :], suf[:, :, 1:], suf[:, :, 0:NF], ALU.subtract).then_inc(pick_ready, 1)
            v.wait_ge(pick_turned, 1)
            v.tensor_copy(pickT[:, 0, :], pg[0][0:NF, 0:G])
            v.tensor_copy(pickT[:, 1, :], pg[1][0:NF, 0:G]).then_inc(pick_copied, 1)
            v.wait_ge(filt_ready, 1)
            for g in range(2):
                link(v.tensor_tensor(prod[:, g, :, :], xps[:, :, g, :],
                                     pf[g][0:G, 0:49].rearrange("p (o k) -> p o k", o=1).broadcast_to([G, B, 49]), ALU.mult))
            link(v.tensor_reduce(y0[:, :, :], prod[:, :, :, :], AX.X, ALU.add))
            v.tensor_scalar(y0[:, :, :], y0[:, :, :], 1.0 / 64, None, ALU.mult).then_inc(y0_ready, 1)
            v.wait_ge(y1_ready, 1)
            for m in range(2):
                link(v.tensor_scalar(yo[:, m, :], ps[0:G, B * m:B * m + B], s1[:, m, 0:1], s1[:, m, 1:2], ALU.mult, ALU.add))
            v.tensor_scalar(yo[:, :, :], yo[:, :, :], 0.0, 1.0, ALU.max, ALU.add).then_inc(gate_ready, 1)


def dct_basis():
    import numpy as np
    t = np.arange(DCT, dtype=np.float32) + np.float32(0.5)

    def along(freq):
        f = np.array(freq, np.float32)[:, None]
        r = (np.cos(np.float32(np.pi) * f * t[None] / np.float32(DCT)) / np.sqrt(np.float32(DCT))).astype(np.float32)
        return np.where(f == 0, r, r * np.sqrt(np.float32(2.0))).astype(np.float32)
    return (along(LOW_X)[:, :, None] * along(LOW_Y)[:, None, :]).reshape(NF, 49).astype(np.float32)


def channels():
    import numpy as np
    return np.ascontiguousarray(np.arange(C, dtype=np.float32).reshape(2, G).T)


def window_strips(nc, x1p, gate, mask, n1g, n1b, qkv_wT, qkv_b, tempr, biasT, proj_wT, proj_b, ident, pout):
    with ExitStack() as ctx:
        sb = lambda name, shape, dt=F32: ctx.enter_context(nc.sbuf_tensor(name, shape, dt))
        pt = lambda name, p=128: ctx.enter_context(nc.psum_tensor(name, [p, 512], F32))
        sem = ctx.enter_context(stage_semaphores(nc))
        w0 = sb("d_w0", [97, 2, 3 * C])
        w = sb("d_w", [97, 2, 3 * C])
        ng = sb("d_ng", [96, 2])
        nb = sb("d_nb", [97, 2])
        tmp = sb("d_tmp", [97, C])
        bt = sb("d_bt", [128, HEADS, 64])
        wp = sb("d_wp", [G, 2, C])
        bp = sb("d_bp", [G, 2])
        idf = sb("d_idf", [128, 128])
        mean_w = sb("d_mean_w", [G, G])
        gt = [sb(f"d_gt{i}", [G, 2]) for i in range(2)]
        xs = [sb(f"d_xs{i}", [G, 2, SN]) for i in range(2)]
        ce = sb("d_ce", [G, 2, SN])
        sq = sb("d_sq", [G, 2, SN])
        rstd = sb("d_rstd", [G, SN])
        xn = [sb(f"d_xn{i}", [97, 2, WS, PW]) for i in range(2)]
        qs = [sb(f"d_qs{i}", [G, 2, 3, NR, 64]) for i in range(2)]
        xw = [sb(f"d_xw{i}", [97, 2, NR, 64]) for i in range(2)]
        ks = [sb(f"d_ks{i}", [G, 2, WS, PW]) for i in range(2)]
        vt = [sb(f"d_vt{i}", [128, 2, 3, 64]) for i in range(2)]
        sc = [sb(f"d_sc{i}", [128, HEADS, 64]) for i in range(2)]
        mx = [sb(f"d_mx{i}", [128, HEADS]) for i in range(2)]
        et = sb("d_et", [128, 3, 128])
        acc = [sb(f"d_acc{i}", [128, 3, WS, PW]) for i in range(2)]
        rec = sb("d_rec", [128, 3, ON])
        att = sb("d_att", [G, 2, ON])
        out = [sb(f"d_out{i}", [G, 2, ON]) for i in range(2)]
        pa_ = [pt(f"d_pa{i}") for i in range(2)]
        pS = [pt(f"d_ps{i}") for i in range(2)]
        pT, pV, pO, pP = pt("d_pt"), pt("d_pv"), pt("d_po"), pt("d_pp")
        par_loaded = sem("d_par_loaded")
        in_loaded = [sem(f"d_in_loaded{i}") for i in range(2)]
        consts = sem("d_consts")
        bias_sum = sem("d_bias_sum")
        folding = sem("d_folding")
        scaled = sem("d_scaled")
        mean_done = sem("d_mean_done")
        centred = sem("d_centred")
        squared = sem("d_squared")
        var_done = sem("d_var_done")
        std_ready = sem("d_std_ready")
        sums_moved = sem("d_sums_moved")
        tick = sem("d_tick")
        rstd_ready = sem("d_rstd_ready")
        normed = sem("d_normed")
        windowed = sem("d_windowed")
        qk_done = sem("d_qk_done")
        q_evac = sem("d_q_evac")
        k_evac = sem("d_k_evac")
        scores = sem("d_scores")
        v_done = sem("d_v_done")
        v_evac = sem("d_v_evac")
        biased = sem("d_biased")
        max_found = sem("d_max_found")
        shifted = sem("d_shifted")
        exp_done = sem("d_exp_done")
        turned = sem("d_turned")
        et_evac = sem("d_et_evac")
        summed = sem("d_summed")
        laid = sem("d_laid")
        acc_ready = sem("d_acc_ready")
        rec_ready = sem("d_rec_ready")
        divided = sem("d_divided")
        projected = sem("d_projected")
        p_evac = sem("d_p_evac")
        stored = [sem(f"d_stored{i}") for i in range(2)]
        block = ctx.enter_context(nc.Block())
        xv = x1p.rearrange("(b g p) h w -> b p g (h w)", b=B, g=2)
        ov = pout.rearrange("(b g p) h w -> b p g (h w)", b=B, g=2)
        gv = gate.rearrange("p (g b) -> b p g", g=2)
        mv = mask.rearrange("(o n) -> o n", o=1)

        def strips(eng, first, strip):
            with eng.Fori(0, B) as b:
                first(b)
                strip(b, 0, 0, 0, False, True)
                with eng.Fori(0, 4) as i:
                    strip(b, 2 * i + 1, i, 1, True, True)
                    strip(b, 2 * i + 2, i, 0, True, True)
                strip(b, NR - 1, 4, 1, True, False)

        def windows(t):
            a = t.copy()
            return bass.AP(tensor=a.tensor, offset=a.offset, ap=[list(a.ap[0]), [STEP, NR], [PW, WS], [1, WS]])

        def patch(t, k, g, wi):
            return t[k, g, :, STEP * wi:STEP * wi + WS]

        @block.sync
        def _(sp):
            with nc.allow_non_contiguous_dma(reason="small vectors, once"):
                sp.dma_start(w0[0:G, :, :], qkv_wT.rearrange("(g p) o -> p g o", p=G)).then_inc(par_loaded, 16)
                sp.dma_start(w0[G:97, 1, :], qkv_b.rearrange("(a o) -> a o", a=1)).then_inc(par_loaded, 16)
                sp.dma_start(ng[:, :], n1g.rearrange("(g p) -> p g", p=G)).then_inc(par_loaded, 16)
                sp.dma_start(nb[0:G, :], n1b.rearrange("(g p) -> p g", p=G)).then_inc(par_loaded, 16)
                sp.dma_start(tmp[:, :], tempr.partition_broadcast(97)).then_inc(par_loaded, 16)
                for k in range(2):
                    sp.dma_start(bt[64 * k:64 * k + 64, :, :], biasT).then_inc(par_loaded, 16)
                sp.dma_start(wp[:, :, :], proj_wT.rearrange("(g p) o -> p g o", p=G)).then_inc(par_loaded, 16)
                sp.dma_start(bp[:, :], proj_b.rearrange("(g p) -> p g", p=G)).then_inc(par_loaded, 16)
                sp.dma_start(idf[:, :], ident).then_inc(par_loaded, 16)

            def load(b, r, par, s):
                sp.dma_start(xs[par][:, :, :], xv[b, :, :, bass.ds(STEP * PW * r, SN)]).then_inc(in_loaded[par], 16)
                sp.dma_start(xn[par][G:97, 1, :, :].rearrange("p h w -> p (h w)"), mv[:, bass.ds(STEP * PW * r, SN)]).then_inc(in_loaded[par], 16)
                with nc.allow_non_contiguous_dma(reason="one gate per channel"):
                    sp.dma_start(gt[par][:, :], gv[b]).then_inc(in_loaded[par], 16)

            def first(b):
                sp.wait_ge(v_done, NP * NR * b)
                sp.sem_inc(tick, 1)
                sp.wait_ge(centred, NR * b)
                sp.sem_inc(tick, 1)
                load(b, 0, 0, NR * b)

            def strip(b, r, h, par, prev, nxt):
                s = NR * b + r
                if nxt:
                    sp.wait_ge(v_done, NP * s)
                    sp.sem_inc(tick, 1)
                    load(b, r + 1, 1 - par, s + 1)
            strips(sp, first, strip)

        @block.tensor
        def _(pe):
            pe.wait_ge(par_loaded, 160)
            pe.wait_ge(consts, 3)
            for o, n, bank in ((0, 512, pS[0]), (512, 64, pS[1])):
                pe.matmul(bank[0:1, 0:n], nb[0:G, 0:1], w0[0:G, 0, o:o + n], start=True, stop=False)
                mm = pe.matmul(bank[0:1, 0:n], nb[0:97, 1:2], w0[0:97, 1, o:o + n], start=False, stop=True)
            mm.then_inc(bias_sum, 1)
            pe.wait_ge(folding, 4)

            def moment(s, src, bank, ready, done):
                pe.wait_ge(ready, s + 1)
                for g in range(2):
                    mm = pe.matmul(bank[0:G, 0:SN], mean_w[:, :], src[:, g, :], start=(g == 0), stop=(g == 1))
                mm.then_inc(done, 1)

            def mean(s, par):
                pe.wait_ge(q_evac, 2 * s)
                moment(s, xs[par], pa_[0], scaled, mean_done)

            def var(s):
                pe.wait_ge(k_evac, 2 * s)
                moment(s, sq, pa_[1], squared, var_done)

            def qk(s, par, m):
                if m == 0:
                    pe.wait_ge(normed, s + 1)
                if m >= 2:
                    pe.wait_ge(q_evac if m == 2 else k_evac, 2 * s + 1)
                col = slice(G * m, G * m + G)
                for g in range(2):
                    kk = slice(0, G + g)
                    mm = pe.matmul(pa_[m % 2][0:G, 0:SN], w[kk, g, col], xn[par][kk, g, :, :].rearrange("p h w -> p (h w)"),
                                   start=(g == 0), stop=(g == 1))
                mm.then_inc(qk_done, 1)

            def score(s, i, par):
                t = NP * s + i
                tp = (par + i) % 2
                if i == 0:
                    pe.wait_ge(q_evac, 2 * s + 2)
                    pe.wait_ge(k_evac, 2 * s + 2)
                if not (isinstance(t, int)) or t >= 2:
                    pe.wait_ge(biased, (NP * s if i == 0 else t - 1) if i < 2 else t - 1)
                for h in range(HEADS):
                    kk = slice(0, G)
                    for k in range(2):
                        wi = 2 * i + k
                        mm = pe.matmul(pS[tp][64 * k:64 * k + 64, 64 * h:64 * h + 64], qs[par][kk, h // 3, h % 3, wi, :],
                                       patch(ks[par], kk, h // 3, wi), start=True, stop=True)
                mm.then_inc(scores, 1)

            def values(s, i, par):
                t = NP * s + i
                pe.wait_ge(v_evac, t)
                if i == 0:
                    pe.wait_ge(windowed, s + 1)
                for k in range(2):
                    for odd in range(2):
                        for g in range(2):
                            kk = slice(0, G + g)
                            rhs = w[kk, g, 2 * C:3 * C].rearrange("p (a o c) -> p a o c", o=2, c=32)[:, :, odd, :]
                            mm = pe.matmul(pV[64 * odd:64 * odd + 64, G * k:G * k + G], xw[par][kk, g, 2 * i + k, :], rhs,
                                           start=(g == 0), stop=(g == 1))
                mm.then_inc(v_done, 1)

            def turn(s, i, par):
                t = NP * s + i
                tp = (par + i) % 2
                pe.wait_ge(exp_done, t + 1)
                pe.wait_ge(et_evac, t)
                for a in range(3):
                    mm = pe.transpose(pT[:, 128 * a:128 * a + 128], sc[tp][:, 2 * a:2 * a + 2, :].rearrange("p a b -> p (a b)"), idf[:, :])
                mm.then_inc(turned, 1)

            def weigh(s, i, par):
                t = NP * s + i
                tp = (par + i) % 2
                pe.wait_ge(et_evac, t + 1)
                pe.wait_ge(v_evac, t + 1)
                pe.wait_ge(laid, 2 * t)
                pe.sem_inc(tick, 1)
                for k in range(2):
                    for a in range(3):
                        for odd in range(2):
                            kk = slice(64 * odd, 64 * odd + 64)
                            mm = pe.matmul(pO[kk, 128 * a + 64 * k:128 * a + 64 * k + 64], vt[tp][kk, k, a, :],
                                           et[kk, a, 64 * k:64 * k + 64], start=True, stop=True)
                mm.then_inc(summed, 1)

            def project(s):
                pe.wait_ge(divided, 3 * s + 3)
                for m in range(2):
                    pe.wait_ge(p_evac, 2 * s + m)
                    for g in range(2):
                        mm = pe.matmul(pP[0:G, 0:ON], wp[:, g, G * m:G * m + G], att[:, g, :], start=(g == 0), stop=(g == 1))
                    mm.then_inc(projected, 1)

            def first(b):
                s = NR * b
                mean(s, 0)
                var(s)
                for m in range(4):
                    qk(s, 0, m)

            def strip(b, r, h, par, prev, nxt):
                s = NR * b + r
                score(s, 0, par)
                values(s, 0, par)
                for i in range(NP):
                    if i + 1 < NP:
                        score(s, i + 1, par)
                    if nxt:
                        if i == 0:
                            mean(s + 1, 1 - par)
                        elif i == 1:
                            var(s + 1)
                        elif i == 2:
                            qk(s + 1, 1 - par, 0)
                            qk(s + 1, 1 - par, 1)
                        elif i == 3:
                            qk(s + 1, 1 - par, 2)
                            qk(s + 1, 1 - par, 3)
                    if prev and i == 3:
                        project(s - 1)
                    turn(s, i, par)
                    if i + 1 < NP:
                        values(s, i + 1, par)
                    weigh(s, i, par)
                if not nxt:
                    project(s)
            strips(pe, first, strip)

        @block.scalar
        def _(a):
            a.wait_ge(par_loaded, 160)

            def scale(b, before, par, s):
                a.wait_ge(in_loaded[par], 48 * (NP * b + before + 1))
                for g in range(2):
                    last = a.activation(xs[par][:, g, :], xs[par][:, g, :], ACT.Copy, scale=gt[par][:, g:g + 1])
                last.then_inc(scaled, 1)

            def square(s):
                a.wait_ge(centred, s + 1)
                a.activation(sq[:, :, :], ce[:, :, :], ACT.Square).then_inc(squared, 1)

            def root(s):
                a.wait_ge(var_done, s + 1)
                a.wait_ge(normed, s)
                a.activation(rstd[:, :], pa_[1][0:G, 0:SN], ACT.Sqrt, bias=EPS).then_inc(std_ready, 1)

            def move_sums(s, par):
                a.wait_ge(laid, 10 * s + 10)
                a.wait_ge(divided, 3 * s)
                for odd in range(2):
                    last = a.activation(rec[64 * odd:64 * odd + 32, :, :],
                                        acc[par][64 * odd + 32:64 * odd + 64, :, 0:STEP, :].rearrange("p a h w -> p a (h w)"), ACT.Copy)
                last.then_inc(sums_moved, 1)

            def evac(s, par, m):
                a.wait_ge(qk_done, 4 * s + m + 1)
                if m == 0:
                    for j in range(3):
                        kk = slice(32 * j, 32 * j + 32)
                        last = a.activation(qs[par][kk, 0, j, :, :].rearrange("p n (h w) -> p n h w", w=WS),
                                            windows(pa_[0][kk, 0:SN]), ACT.Copy)
                    last.then_inc(q_evac, 1)
                else:
                    a.activation(ks[par][:, 0, :, :].rearrange("p h w -> p (h w)"), pa_[0][0:G, 0:SN], ACT.Copy).then_inc(q_evac, 1)

            def values(s, i, par):
                t = NP * s + i
                a.wait_ge(v_done, t + 1)
                a.activation(vt[(par + i) % 2][:, :, :, 0:32], pV[:, 0:2 * G].rearrange("p (k a c) -> p k a c", k=2, c=32),
                             ACT.Copy).then_inc(v_evac, 1)

            def expo(s, i, par):
                t = NP * s + i
                a.wait_ge(shifted, t + 1)
                q = sc[(par + i) % 2]
                a.activation(q[:, :, :], q[:, :, :], ACT.Exp).then_inc(exp_done, 1)

            def turn(s, i):
                a.wait_ge(turned, NP * s + i + 1)
                a.activation(et[:, :, :], pT[:, 0:384].rearrange("p (a n) -> p a n", a=3), ACT.Copy).then_inc(et_evac, 1)

            def finish(s, par, before):
                a.wait_ge(stored[par], 16 * before)
                for m in range(2):
                    a.wait_ge(projected, 2 * s + m + 1)
                    a.activation(out[par][:, m, :], pP[0:G, 0:ON], ACT.Identity, bias=bp[:, m:m + 1]).then_inc(p_evac, 1)

            def first(b):
                s = NR * b
                scale(b, 0, 0, s)
                square(s)
                root(s)
                evac(s, 0, 0)
                evac(s, 0, 2)

            def strip(b, r, h, par, prev, nxt):
                s = NR * b + r
                if nxt:
                    scale(b, (h + 1 if par else h + 1 if prev else 0), 1 - par, s + 1)
                values(s, 0, par)
                expo(s, 0, par)
                for i in range(NP):
                    if prev and i == 0:
                        move_sums(s - 1, 1 - par)
                    if nxt:
                        if i == 0:
                            square(s + 1)
                        elif i == 1:
                            root(s + 1)
                        elif i == 2:
                            evac(s + 1, 1 - par, 0)
                        elif i == 3:
                            evac(s + 1, 1 - par, 2)
                    if prev and i == 3:
                        finish(s - 1, 1 - par, NP * b + h)
                    turn(s, i)
                    if i + 1 < NP:
                        values(s, i + 1, par)
                        expo(s, i + 1, par)
                if not nxt:
                    move_sums(s, par)
                    finish(s, par, NP * b + 4)
            strips(a, first, strip)

        @block.vector
        def _(v):
            v.memset(mean_w[:, :], 1.0 / C)
            v.memset(rec[:, :, :], 1.0)
            v.memset(nb[G:97, :], 1.0).then_inc(consts, 1)
            for k in range(2):
                v.memset(qs[k][:, :, :, :, :], 0.0)
                v.memset(vt[k][:, :, :, 32:64], 1.0).then_inc(consts, 1)
            v.wait_ge(par_loaded, 160)
            for g in range(2):
                last = v.tensor_scalar(w[0:G, g, :], w0[0:G, g, :], ng[:, g:g + 1], None, ALU.mult)
            last.then_inc(folding, 1)
            v.wait_ge(bias_sum, 1)
            v.tensor_copy(w[G:97, 1, 0:512], pS[0][0:1, 0:512])
            v.tensor_copy(w[G:97, 1, 512:576], pS[1][0:1, 0:64]).then_inc(folding, 1)
            v.wait_ge(folding, 2)
            for g in range(2):
                v.tensor_tensor(w[0:G + g, g, 0:C], w[0:G + g, g, 0:C], tmp[0:G + g, :], ALU.mult).then_inc(folding, 1)

            def centre(s, par):
                v.wait_ge(mean_done, s + 1)
                v.wait_ge(squared, s)
                v.tensor_tensor(ce[:, :, :], xs[par][:, :, :],
                                pa_[0][0:G, 0:SN].rearrange("p (o n) -> p o n", o=1).broadcast_to([G, 2, SN]), ALU.subtract).then_inc(centred, 1)

            def norm(s, par):
                v.wait_ge(std_ready, s + 1)
                v.reciprocal(rstd[:, :], rstd[:, :]).then_inc(rstd_ready, 1)
                v.wait_ge(rstd_ready, s + 1)
                v.tensor_tensor(xn[par][0:G, :, :, :].rearrange("p g h w -> p g (h w)"), ce[:, :, :],
                                rstd[:, :].rearrange("p (o n) -> p o n", o=1).broadcast_to([G, 2, SN]), ALU.mult).then_inc(normed, 1)

            def evac(s, par, m):
                v.wait_ge(qk_done, 4 * s + m + 1)
                if m == 1:
                    for j in range(3):
                        kk = slice(32 * j, 32 * j + 32)
                        last = v.tensor_copy(qs[par][kk, 1, j, :, :].rearrange("p n (h w) -> p n h w", w=WS), windows(pa_[1][kk, 0:SN]))
                    last.then_inc(k_evac, 1)
                else:
                    v.tensor_copy(ks[par][:, 1, :, :].rearrange("p h w -> p (h w)"), pa_[1][0:G, 0:SN]).then_inc(k_evac, 1)

            def soft(s, i, par):
                t = NP * s + i
                tp = (par + i) % 2
                v.wait_ge(scores, t + 1)
                v.tensor_tensor(sc[tp][:, :, :], pS[tp][:, 0:384].rearrange("p (h j) -> p h j", j=64), bt[:, :, :], ALU.add).then_inc(biased, 1)
                v.wait_ge(biased, t + 1)
                v.tensor_reduce(mx[tp][:, :], sc[tp][:, :, :], AX.X, ALU.max).then_inc(max_found, 1)
                v.wait_ge(max_found, t + 1)
                v.tensor_tensor(sc[tp][:, :, :], sc[tp][:, :, :],
                                mx[tp][:, :].rearrange("p (h o) -> p h o", o=1).broadcast_to([128, HEADS, 64]), ALU.subtract).then_inc(shifted, 1)

            def lay(s, i, par):
                t = NP * s + i
                if i == 0:
                    v.wait_ge(acc_ready, s + 1)
                v.wait_ge(summed, t + 1)
                for k in range(2):
                    dst = acc[par][:, :, :, STEP * (2 * i + k):STEP * (2 * i + k) + WS]
                    v.wait_ge(laid, 2 * t + k)
                    v.tensor_tensor(dst, dst, pO[:, 0:384].rearrange("p (a k h w) -> p a k h w", a=3, k=2, h=8)[:, :, k, :, :],
                                    ALU.add).then_inc(laid, 1)

            def divide(s, par, a):
                v.wait_ge(sums_moved, s + 1)
                v.wait_ge(laid, 10 * s + 10)
                v.wait_ge(projected, 2 * s)
                v.reciprocal(rec[0:96, a, :], rec[0:96, a, :]).then_inc(rec_ready, 1)
                v.wait_ge(rec_ready, 3 * s + a + 1)
                for odd in range(2):
                    h = 2 * a + odd
                    last = v.tensor_tensor(att[32 * (h % 3):32 * (h % 3) + 32, h // 3, :],
                                           acc[par][64 * odd:64 * odd + 32, a, 0:STEP, :].rearrange("p h w -> p (h w)"),
                                           rec[64 * odd:64 * odd + 32, a, :], ALU.mult)
                last.then_inc(divided, 1)

            def first(b):
                s = NR * b
                centre(s, 0)
                norm(s, 0)
                evac(s, 0, 1)
                evac(s, 0, 3)

            def strip(b, r, h, par, prev, nxt):
                s = NR * b + r
                soft(s, 0, par)
                for i in range(NP):
                    if i + 1 < NP:
                        soft(s, i + 1, par)
                    if prev and i < 3:
                        divide(s - 1, 1 - par, i)
                    if nxt:
                        if i == 0:
                            centre(s + 1, 1 - par)
                        elif i == 2:
                            evac(s + 1, 1 - par, 1)
                        elif i == 3:
                            evac(s + 1, 1 - par, 3)
                    lay(s, i, par)
                    if nxt and i == 1:
                        norm(s + 1, 1 - par)
                if not nxt:
                    for i in range(3):
                        divide(s, par, i)
            strips(v, first, strip)

        @block.gpsimd
        def _(p):
            def store(b, r, s, par):
                p.wait_ge(p_evac, 2 * s + 2)
                p.dma_start(ov[b, :, :, bass.ds(ON * r, ON)], out[par][:, :, :]).then_inc(stored[par], 16)

            def window(s, par):
                p.wait_ge(normed, s + 1)
                p.wait_ge(in_loaded[par], 48)
                p.sem_inc(tick, 1)
                for g in range(2):
                    last = p.tensor_copy(xw[par][0:G + g, g, :, :].rearrange("p n (h w) -> p n h w", w=WS),
                                         windows(xn[par][0:G + g, g, :, :].rearrange("p h w -> p (h w)")))
                last.then_inc(windowed, 1)

            def first(b):
                window(NR * b, 0)
                p.wait_ge(divided, 3 * NR * b)
                p.sem_inc(tick, 1)
                p.memset(acc[0][:, :, :, :], 0.0).then_inc(acc_ready, 1)

            def strip(b, r, h, par, prev, nxt):
                s = NR * b + r
                if nxt:
                    window(s + 1, 1 - par)
                    p.wait_ge(divided, 3 * s)
                    p.sem_inc(tick, 1)
                    p.memset(acc[1 - par][:, :, 2:, :], 0.0)
                    p.wait_ge(laid, 10 * s + 10)
                    p.sem_inc(tick, 1)
                    p.tensor_copy(acc[1 - par][:, :, 0:2, :], acc[par][:, :, STEP:WS, :]).then_inc(acc_ready, 1)
                if prev:
                    store(b, r - 1, s - 1, 1 - par)
                if not nxt:
                    store(b, r, s, par)
            strips(p, first, strip)
            p.wait_ge(stored[0], 16 * NP * B)
            p.wait_ge(stored[1], 16 * NP * B)


def inside():
    import numpy as np
    m = np.zeros((PW, PW), np.float32)
    m[3:59, 3:59] = 1
    return m.reshape(-1)


def relative(rpb):
    import numpy as np
    c = np.stack(np.meshgrid(np.arange(WS), np.arange(WS), indexing="ij"), 0).reshape(2, -1)
    d = c[:, :, None] - c[:, None, :] + WS - 1
    return np.ascontiguousarray(np.asarray(rpb)[d[0] * (2 * WS - 1) + d[1]].transpose(0, 2, 1))


def forward_block(nc, x1p, gate, pout, hft_w, hft_b, n2g, n2b, fc1_wT, fc1_b, sgn_g, sgn_b, sg_w, sg_b, fc2_wT, fc2_b, ident, x3):
    with ExitStack() as ctx:
        sb = lambda name, shape, dt=F32: ctx.enter_context(nc.sbuf_tensor(name, shape, dt))
        pt = lambda name, p=G: ctx.enter_context(nc.psum_tensor(name, [p, 512], F32))
        sem = ctx.enter_context(stage_semaphores(nc))
        w1 = sb("e_w1", [G, 2, HID])
        w2 = sb("e_w2", [G, 4, C])
        hw = sb("e_hw", [G, 2, 9])
        gw = sb("e_gw", [G, 4, 9])
        hb = sb("e_hb", [G, 2])
        ng = sb("e_ng", [G, 2])
        nb = sb("e_nb", [G, 2])
        b1o = sb("e_b1o", [G, 8])
        b1v = sb("e_b1", [G, 8])
        sgg = sb("e_sgg", [G, 4])
        sgb = sb("e_sgb", [G, 4])
        gb = sb("e_gb", [G, 4])
        b2v = sb("e_b2", [G, 2])
        idf = sb("e_idf", [128, 128])
        diag = sb("e_diag", [G, 2, 9, G])
        m192 = sb("e_m192", [G, G])
        m384 = sb("e_m384", [G, G])
        gt = [sb(f"e_gt{i}", [G, 2]) for i in range(4)]
        pin = [sb(f"e_pin{i}", [G, 2, 8, PW]) for i in range(4)]
        xin = [sb(f"e_xin{i}", [G, 2, 8, PW]) for i in range(4)]
        at = [sb(f"e_at{i}", [G, 2, 10, AW]) for i in range(4)]
        zt = [sb(f"e_zt{i}", [G, 4, 10, AW]) for i in range(4)]
        z1 = [sb(f"e_z1{i}", [G, 4, CH]) for i in range(4)]
        x1 = [sb(f"e_x1{i}", [G, 2, CH]) for i in range(NCH)]
        rows2, s2 = sb("e_rows2", [G, 2, 4, W]), sb("e_s2", [G, 2, 4, 28])
        rows4, s4 = sb("e_rows4", [G, 2, 2, 28]), sb("e_s4", [G, 2, 2, 14])
        rows8, s8 = sb("e_rows8", [G, 2, 14]), sb("e_s8", [G, 2, 7])
        sig = sb("e_sig", [G, 2, CH])
        ce = sb("e_ce", [G, 2, CH])
        sq = sb("e_sq", [G, 2, CH])
        rs = sb("e_rs", [G, CH])
        xn = sb("e_xn", [G, 2, CH])
        z2 = sb("e_z2", [G, 4, CH])
        sq2 = sb("e_sq2", [G, 4, CH])
        rs2 = sb("e_rs2", [G, CH])
        zc = sb("e_zc", [G, 4, CH])
        w1o = zc[:, :, :].rearrange("p a b -> p (a b)")[:, 0:2 * HID].rearrange("p (g o) -> p g o", g=2)
        out = [sb(f"e_out{i}", [G, 2, CH]) for i in range(2)]
        pC = [pt(f"e_pc{i}") for i in range(2)]
        pM, pV = pt("e_pm"), pt("e_pv")
        p1 = [pt(f"e_p1{i}") for i in range(2)]
        p2 = [pt(f"e_p2{i}") for i in range(2)]
        par_loaded = sem("e_par_loaded")
        in_loaded = [sem(f"e_in_loaded{i}") for i in range(4)]
        cleared = sem("e_cleared")
        folded = sem("e_folded")
        bias_sum = sem("e_bias_sum")
        tripled = sem("e_tripled")
        pool_step = sem("e_pool_step")
        high_ready = sem("e_high_ready")
        conv_done = sem("e_conv_done")
        sig_done = sem("e_sig_done")
        sig_mul = sem("e_sig_mul")
        x1_ready = sem("e_x1_ready")
        mean1 = sem("e_mean1")
        centred1 = sem("e_centred1")
        squared1 = sem("e_squared1")
        var1 = sem("e_var1")
        std1 = sem("e_std1")
        rstd1 = sem("e_rstd1")
        normed1 = sem("e_normed1")
        hidden = sem("e_hidden")
        gelu_done = sem("e_gelu_done")
        mean2 = sem("e_mean2")
        centred2 = sem("e_centred2")
        squared2 = sem("e_squared2")
        var2 = sem("e_var2")
        std2 = sem("e_std2")
        rstd2 = sem("e_rstd2")
        normed2 = sem("e_normed2")
        affine2 = sem("e_affine2")
        halo_ready = sem("e_halo_ready")
        dw_step = sem("e_dw_step")
        gated = sem("e_gated")
        mixed = sem("e_mixed")
        finished = sem("e_finished")
        stored = [sem(f"e_stored{i}") for i in range(2)]
        tick = sem("e_tick")
        block = ctx.enter_context(nc.Block())
        xv = x1p.rearrange("(b g p) h w -> b p g (h w)", b=B, g=2)
        pv = pout.rearrange("(b g p) h w -> b p g (h w)", b=B, g=2)
        ov = x3.rearrange("(b g p) n -> b p g n", b=B, g=2)
        gv = gate.rearrange("p (g b) -> b p g", g=2)

        def steps(eng, step):
            for k in range(NCH):
                step(0, k)
            with eng.Fori(1, B) as b:
                for k in range(NCH):
                    step(b, k)
            for k in range(LAG):
                step(B, k)

        def chunk(b, k, lag):
            if k >= lag:
                return None if isinstance(b, int) and b == B else (b, k - lag)
            return None if isinstance(b, int) and b == 0 else (b - 1, k - lag + NCH)

        def loads(b, c):
            return 48 * (USES[PLACE[c]] * b + PLACE[:c].count(PLACE[c]) + 1)

        def before(b, c, n, per=1, extra=0):
            if isinstance(b, int) and NCH * b + c - n + 1 < 0:
                return 0
            return per * (NCH * b + c - n + 1) + extra

        def img(ap):
            return ap.rearrange("p (h w) -> p h w", w=W)

        def spread(ap, n):
            return ap.rearrange("p (o m) -> p o m", o=1).broadcast_to([G, n, CH])

        @block.sync
        def _(sp):
            with nc.allow_non_contiguous_dma(reason="small vectors, once"):
                sp.dma_start(w1o[:, :, :], fc1_wT.rearrange("(g p) o -> p g o", p=G)).then_inc(par_loaded, 16)
                sp.dma_start(w2[:, :, :], fc2_wT.rearrange("(g p) o -> p g o", p=G)).then_inc(par_loaded, 16)
                sp.dma_start(hw[:, :, :], hft_w.rearrange("(g p) k -> p g k", p=G)).then_inc(par_loaded, 16)
                sp.dma_start(gw[:, :, :], sg_w.rearrange("(g p) k -> p g k", p=G)).then_inc(par_loaded, 16)
                for dst, src in ((hb, hft_b), (ng, n2g), (nb, n2b), (b1o, fc1_b), (sgg, sgn_g), (sgb, sgn_b), (gb, sg_b), (b2v, fc2_b)):
                    sp.dma_start(dst[:, :], src.rearrange("(g p) -> p g", p=G)).then_inc(par_loaded, 16)
                sp.dma_start(idf[:, :], ident).then_inc(par_loaded, 16)

            def store(b, c):
                sp.wait_ge(finished, 2 * NCH * b + 2 * c + 2)
                sp.sem_inc(tick, 1)
                sp.dma_start(ov[b, :, :, c * CH:(c + 1) * CH], out[c % 2][:, :, :]).then_inc(stored[c % 2], 16)

            def step(b, k):
                now, old = chunk(b, k, 0), chunk(b, k, LAG)
                if now:
                    b, c = now
                    o = PLACE[c]
                    sp.wait_ge(x1_ready, before(b, c, 3, 2))
                    sp.sem_inc(tick, 1)
                    sp.dma_start(pin[o][:, :, :, :].rearrange("p g h w -> p g (h w)"), pv[b, :, :, (3 + 8 * c) * PW:(11 + 8 * c) * PW])\
                        .then_inc(in_loaded[o], 16)
                    sp.dma_start(xin[o][:, :, :, :].rearrange("p g h w -> p g (h w)"), xv[b, :, :, (3 + 8 * c) * PW:(11 + 8 * c) * PW])\
                        .then_inc(in_loaded[o], 16)
                    with nc.allow_non_contiguous_dma(reason="one gate per channel"):
                        sp.dma_start(gt[o][:, :], gv[b]).then_inc(in_loaded[o], 16)
                if old:
                    store(*old)
            steps(sp, step)
            sp.wait_ge(stored[0], 16 * 4 * B)
            sp.wait_ge(stored[1], 16 * 3 * B)

        @block.gpsimd
        def _(p):
            for i in range(4):
                p.memset(at[i][:, :, :, :], 0.0)
                p.memset(zt[i][:, :, :, :], 0.0).then_inc(cleared, 1)

            def high(b, c):
                q = NCH * b + c
                o = PLACE[c]
                n = 21 * c - (c > 0)

                def link(ins):
                    nonlocal n
                    n += 1
                    ins.then_inc(pool_step, 1)
                    p.wait_ge(pool_step, 21 * NCH * b + n)
                    p.sem_inc(tick, 1)
                p.wait_ge(tripled, q + 1)
                src = pin[o][:, :, :, 3:3 + W]
                link(p.tensor_tensor(rows2[:, :, :, :], src[:, :, 0::2, :], src[:, :, 1::2, :], ALU.add))
                link(p.tensor_tensor(s2[:, :, :, :], rows2[:, :, :, 0::2], rows2[:, :, :, 1::2], ALU.add))
                link(p.tensor_tensor(rows4[:, :, :, :], s2[:, :, 0::2, :], s2[:, :, 1::2, :], ALU.add))
                link(p.tensor_tensor(s4[:, :, :, :], rows4[:, :, :, 0::2], rows4[:, :, :, 1::2], ALU.add))
                link(p.tensor_tensor(rows8[:, :, :], s4[:, :, 0, :], s4[:, :, 1, :], ALU.add))
                link(p.tensor_tensor(s8[:, :, :], rows8[:, :, 0::2], rows8[:, :, 1::2], ALU.add))
                link(p.tensor_scalar(s8[:, :, :], s8[:, :, :], 1.0 / 64, None, ALU.mult))
                link(p.tensor_scalar(s4[:, :, :, :], s4[:, :, :, :], 1.0 / 16, None, ALU.mult))
                link(p.tensor_scalar(s2[:, :, :, :], s2[:, :, :, :], 1.0 / 4, None, ALU.mult))
                for g in range(2):
                    t = s4[:, g, :, :].rearrange("p r (a w) -> p r a w", w=2)
                    link(p.tensor_tensor(t, t, s8[:, g, :].rearrange("p (o a i) -> p o a i", o=1, i=1).broadcast_to([G, 2, 7, 2]), ALU.add))
                for g in range(2):
                    for w in range(2):
                        t = s2[:, g, :, w::2].rearrange("p (a r) w -> p a r w", r=2)
                        link(p.tensor_tensor(t, t, s4[:, g, :, :].rearrange("p a (o w) -> p a o w", o=1).broadcast_to([G, 2, 2, 14]), ALU.add))
                for g in range(2):
                    for r in range(2):
                        t = at[o][:, g, 1 + r:9:2, 1:1 + W].rearrange("p h (a w) -> p h a w", w=2)
                        link(p.tensor_tensor(t, t, s2[:, g, :, :].rearrange("p h (w o) -> p h w o", o=1).broadcast_to([G, 4, 28, 2]), ALU.subtract))
                if c == 0:
                    link(p.memset(at[o][:, :, 0, :], 0.0))
                else:
                    link(p.tensor_copy(at[o][:, :, 0, :], at[PLACE[c - 1]][:, :, 8, :]))
                    link(p.tensor_copy(at[PLACE[c - 1]][:, :, 9, :], at[o][:, :, 1, :]))
                if c == NCH - 1:
                    link(p.memset(at[o][:, :, 9, :], 0.0))
                p.sem_inc(high_ready, 1)

            def halo(b, c):
                q = NCH * b + c
                o = PLACE[c]
                p.wait_ge(affine2, q + 1)
                p.sem_inc(tick, 1)
                if c == 0:
                    p.memset(zt[o][:, :, 0, :], 0.0)
                else:
                    p.tensor_copy(zt[o][:, :, 0, :], zt[PLACE[c - 1]][:, :, 8, :])
                    p.tensor_copy(zt[PLACE[c - 1]][:, :, 9, :], zt[o][:, :, 1, :])
                if c == NCH - 1:
                    p.memset(zt[o][:, :, 9, :], 0.0)
                p.drain().then_inc(halo_ready, 1)

            def step(b, k):
                if chunk(b, k, 0):
                    high(b, k)
                if chunk(b, k, 3):
                    halo(*chunk(b, k, 3))
            steps(p, step)

        @block.tensor
        def _(pe):
            pe.wait_ge(par_loaded, 16 * 13)
            pe.wait_ge(cleared, 4 + 2)
            for m in range(8):
                for g in range(2):
                    mm = pe.matmul(pM[:, m:m + 1], w1o[:, g, G * m:G * m + G], nb[:, g:g + 1], start=(g == 0), stop=(g == 1))
            mm.then_inc(bias_sum, 1)
            pe.wait_ge(folded, 3)

            def moment(bank, weights, src, n, done):
                for g in range(n):
                    mm = pe.matmul(bank[:, 0:CH], weights[:, :], src[:, g, :], start=(g == 0), stop=(g == n - 1))
                mm.then_inc(done, 1)

            def conv(b, c, g):
                q = NCH * b + c
                if g == 0:
                    pe.wait_ge(high_ready, q + 2 if c + 1 < NCH else q + 1)
                pe.wait_ge(sig_done, 2 * q + g - (1 if g else 0))
                for k in range(9):
                    dy, dx = divmod(k, 3)
                    mm = pe.matmul(pC[g][:, 0:CH], diag[:, g, k, :], at[PLACE[c]][:, g, dy:dy + 8, dx:dx + W], start=(k == 0), stop=(k == 8))
                mm.then_inc(conv_done, 1)

            def expand(qm, m0):
                if m0 == 0:
                    pe.wait_ge(normed1, qm + 1)
                for m in range(m0, m0 + 4):
                    pe.wait_ge(gelu_done, 8 * qm + (m - 1 if m >= 2 else 0))
                    for g in range(2):
                        mm = pe.matmul(p1[m % 2][:, 0:CH], w1[:, g, G * m:G * m + G], xn[:, g, :], start=(g == 0), stop=(g == 1))
                    mm.then_inc(hidden, 1)

            def step(b, k):
                on1, on2, onm, on3 = (chunk(b, k, lag) for lag in (1, 2, 3, LAG))
                b1, c1 = on1 or (0, 0)
                b2, c2 = on2 or (0, 0)
                bm, cm = onm or (0, 0)
                b3, c3 = on3 or (0, 0)
                q1, q2, qm, q3 = NCH * b1 + c1, NCH * b2 + c2, NCH * bm + cm, NCH * b3 + c3
                if onm:
                    expand(qm, 0)
                if on2:
                    pe.wait_ge(x1_ready, 2 * q2 + 2)
                    pe.wait_ge(centred2, q2 - 1 if onm else 0)
                    moment(pM, m192, x1[c2], 2, mean1)
                if onm:
                    expand(qm, 4)
                if on1:
                    conv(b1, c1, 0)
                if on2:
                    pe.wait_ge(squared1, q2 + 1)
                    pe.wait_ge(std2, q2 - 1 if onm else 0)
                    moment(pV, m192, sq, 2, var1)
                if onm:
                    pe.wait_ge(gelu_done, 8 * qm + 8)
                    pe.wait_ge(centred1, q2 + 1 if on2 else qm + 1)
                    moment(pM, m384, z2, 4, mean2)
                if on1:
                    conv(b1, c1, 1)
                if onm:
                    pe.wait_ge(squared2, qm + 1)
                    pe.wait_ge(std1, q2 + 1 if on2 else qm + 1)
                    moment(pV, m384, sq2, 4, var2)
                if on3:
                    pe.wait_ge(gated, q3 + 1)
                    pe.wait_ge(finished, 2 * q3)
                    for m in range(2):
                        for g in range(4):
                            mm = pe.matmul(p2[m][:, 0:CH], w2[:, g, G * m:G * m + G], zc[:, g, :], start=(g == 0), stop=(g == 3))
                        mm.then_inc(mixed, 1)
            steps(pe, step)

        @block.scalar
        def _(a):
            a.wait_ge(par_loaded, 16 * 13)
            a.wait_ge(folded, 3)
            a.wait_ge(cleared, 4 + 2)
            def step(b, k):
                on1, on2, onm, on3 = (chunk(b, k, lag) for lag in (1, 2, 3, LAG))
                b1, c1 = on1 or (0, 0)
                b2, c2 = on2 or (0, 0)
                bm, cm = onm or (0, 0)
                b3, c3 = on3 or (0, 0)
                q1, q2, qm, q3 = NCH * b1 + c1, NCH * b2 + c2, NCH * bm + cm, NCH * b3 + c3
                if chunk(b, k, 0):
                    o = PLACE[k]
                    a.wait_ge(in_loaded[o], loads(b, k))
                    a.wait_ge(conv_done, before(b, k, 3, 2))
                    a.activation(at[o][:, :, 1:9, 1:1 + W], pin[o][:, :, :, 3:3 + W], ACT.Copy, scale=3.0).then_inc(tripled, 1)
                if onm:
                    for m in range(8):
                        a.wait_ge(hidden, 8 * qm + m + 1)
                        if m == 0:
                            a.wait_ge(gated, before(bm, cm, 3))
                            a.wait_ge(normed2, qm)
                        dst = z1[PLACE[cm]][:, m, :] if m < 4 else z2[:, m - 4, :]
                        a.activation(dst, p1[m % 2][:, 0:CH], ACT.Gelu, bias=b1v[:, m:m + 1]).then_inc(gelu_done, 1)
                if on2:
                    a.wait_ge(centred1, q2 + 1)
                    a.activation(sq[:, :, :], ce[:, :, :], ACT.Square).then_inc(squared1, 1)
                    a.wait_ge(var1, q2 + 1)
                    a.wait_ge(normed1, q2)
                    a.activation(rs[:, :], pV[:, 0:CH], ACT.Sqrt, bias=EPS).then_inc(std1, 1)
                if onm:
                    a.wait_ge(centred2, qm + 1)
                    a.activation(sq2[:, :, :], z2[:, :, :], ACT.Square).then_inc(squared2, 1)
                    a.wait_ge(var2, qm + 1)
                    a.activation(rs2[:, :], pV[:, 0:CH], ACT.Sqrt, bias=EPS).then_inc(std2, 1)
                if on1:
                    a.wait_ge(x1_ready, 2 * q1)
                    for g in range(2):
                        a.wait_ge(conv_done, 2 * q1 + g + 1)
                        a.activation(sig[:, g, :], pC[g][:, 0:CH], ACT.Sigmoid, bias=hb[:, g:g + 1]).then_inc(sig_done, 1)
                if onm:
                    a.wait_ge(normed2, qm + 1)
                    a.wait_ge(gated, before(bm, cm, 3))
                    for g in range(4):
                        last = a.activation(zt[PLACE[cm]][:, g, 1:9, 1:1 + W], img(z2[:, g, :]), ACT.Identity,
                                            bias=sgb[:, g:g + 1], scale=sgg[:, g:g + 1])
                    last.then_inc(affine2, 1)
            steps(a, step)

        @block.vector
        def _(v):
            v.memset(m192[:, :], 1.0 / C).then_inc(cleared, 1)
            v.memset(m384[:, :], 1.0 / (2 * C)).then_inc(cleared, 1)
            v.wait_ge(par_loaded, 16 * 13)
            for g in range(2):
                for k in range(9):
                    v.tensor_scalar(diag[:, g, k, :], idf[0:G, 0:G], hw[:, g, k:k + 1], None, ALU.mult)
                v.tensor_scalar(w1[:, g, :], w1o[:, g, :], ng[:, g:g + 1], None, ALU.mult).then_inc(folded, 1)
            v.wait_ge(bias_sum, 1)
            v.tensor_tensor(b1v[:, :], pM[:, 0:8], b1o[:, :], ALU.add).then_inc(folded, 1)

            def depthwise(b, c, g0):
                q = NCH * b + c
                base = 36 * q + 9 * g0
                for k in range(9):
                    dy, dx = divmod(k, 3)
                    for i in range(2):
                        g = g0 + i
                        src = zt[PLACE[c]][:, g, dy:dy + 8, dx:dx + W]
                        dst = img(zc[:, g, :])
                        if k == 0:
                            v.tensor_scalar(dst, src, gw[:, g, 0:1], gb[:, g:g + 1], ALU.mult, ALU.add).then_inc(dw_step, 1)
                        else:
                            v.wait_ge(dw_step, base + 2 * (k - 1) + i + 1)
                            v.scalar_tensor_tensor(dst, src, gw[:, g, k:k + 1], dst, ALU.mult, ALU.add).then_inc(dw_step, 1)

            def norm(ready, done, rdone, q, rs_, src, dst, n):
                v.wait_ge(ready, q + 1)
                v.reciprocal(rs_[:, :], rs_[:, :]).then_inc(rdone, 1)
                v.wait_ge(rdone, q + 1)
                v.tensor_tensor(dst[:, :, :], src[:, :, :], spread(rs_[:, :], n), ALU.mult).then_inc(done, 1)

            def step(b, k):
                on1, on2, onm, on3 = (chunk(b, k, lag) for lag in (1, 2, 3, LAG))
                b1, c1 = on1 or (0, 0)
                b2, c2 = on2 or (0, 0)
                bm, cm = onm or (0, 0)
                b3, c3 = on3 or (0, 0)
                q1, q2, qm, q3 = NCH * b1 + c1, NCH * b2 + c2, NCH * bm + cm, NCH * b3 + c3
                if on3:
                    v.wait_ge(halo_ready, q3 + 2 if c3 + 1 < NCH else q3 + 1)
                    v.wait_ge(mixed, 2 * q3)
                    depthwise(b3, c3, 0)
                if on2:
                    v.wait_ge(mean1, q2 + 1)
                    v.wait_ge(squared1, q2)
                    v.tensor_tensor(ce[:, :, :], x1[c2][:, :, :], spread(pM[:, 0:CH], 2), ALU.subtract).then_inc(centred1, 1)
                if on3:
                    depthwise(b3, c3, 2)
                    v.wait_ge(dw_step, 36 * q3 + 36)
                    v.tensor_tensor(zc[:, :, :], zc[:, :, :], z1[PLACE[c3]][:, :, :], ALU.mult).then_inc(gated, 1)
                if onm:
                    v.wait_ge(mean2, qm + 1)
                    v.wait_ge(squared2, qm)
                    v.tensor_tensor(z2[:, :, :], z2[:, :, :], spread(pM[:, 0:CH], 4), ALU.subtract).then_inc(centred2, 1)
                if on2:
                    v.wait_ge(hidden, 8 * q2)
                    norm(std1, normed1, rstd1, q2, rs, ce, xn, 2)
                if onm:
                    norm(std2, normed2, rstd2, qm, rs2, z2, z2, 4)
                if on1:
                    o = PLACE[c1]
                    v.wait_ge(in_loaded[o], loads(b1, c1))
                    for g in range(2):
                        v.wait_ge(sig_done, 2 * q1 + g + 1)
                        v.tensor_tensor(img(sig[:, g, :]), img(sig[:, g, :]), pin[o][:, g, :, 3:3 + W], ALU.mult).then_inc(sig_mul, 1)
                    for g in range(2):
                        v.wait_ge(sig_mul, 2 * q1 + g + 1)
                        v.scalar_tensor_tensor(img(x1[c1][:, g, :]), xin[o][:, g, :, 3:3 + W], gt[o][:, g:g + 1], img(sig[:, g, :]),
                                               ALU.mult, ALU.add).then_inc(x1_ready, 1)
                if on3:
                    o = c3 % 2
                    v.wait_ge(stored[o], 16 * ((3 if o else 4) * b3 + c3 // 2))
                    for m in range(2):
                        v.wait_ge(mixed, 2 * q3 + m + 1)
                        v.scalar_tensor_tensor(out[o][:, m, :], p2[m][:, 0:CH], b2v[:, m:m + 1], x1[c3][:, m, :],
                                               ALU.add, ALU.add).then_inc(finished, 1)
            steps(v, step)


def scan_inputs(nc, x3, ln_w, ln_b, in_wT, conv_w, conv_b, dts_wT, bc_wT, xc, zs, dts, bcs):
    with ExitStack() as ctx:
        sb = lambda name, shape, dt=F32: ctx.enter_context(nc.sbuf_tensor(name, shape, dt))
        pt = lambda name: ctx.enter_context(nc.psum_tensor(name, [G, 512], F32))
        sem = ctx.enter_context(stage_semaphores(nc))
        wo = sb("f_wo", [G, 2, 2 * C])
        w = sb("f_w", [G, 2, 2 * C])
        wd = sb("f_wd", [G, 2, KD * RANK])
        wb = sb("f_wb", [G, 2, NBC])
        wb3 = sb("f_wb3", [G, 2, 3, NBC])
        cw = sb("f_cw", [G, 2, 9])
        cb = sb("f_cb", [G, 2])
        lg = sb("f_lg", [G, 2])
        lb = sb("f_lb", [G, 2])
        bi = sb("f_bi", [G, 4])
        m192 = sb("f_m192", [G, G])
        xin = [sb(f"f_xin{i}", [G, 2, CH]) for i in range(2)]
        ce = [sb(f"f_ce{i}", [G, 2, CH]) for i in range(2)]
        sq = sb("f_sq", [G, 2, CH])
        rs = sb("f_rs", [G, CH])
        xn = sb("f_xn", [G, 2, CH])
        ct = [sb(f"f_ct{i}", [G, 2, 10, AW]) for i in range(R3)]
        cv = sb("f_cv", [G, 2, CH])
        xo = [sb(f"f_xo{i}", [G, 2, CH]) for i in range(2)]
        zo = [sb(f"f_zo{i}", [G, 2, CH]) for i in range(2)]
        do = [sb(f"f_do{i}", [KD * RANK, CH]) for i in range(2)]
        hi = sb("f_hi", [G, CH], BF16)
        r1 = sb("f_r1", [G, CH])
        mid = sb("f_mid", [G, CH], BF16)
        bo = [sb(f"f_bo{i}", [G, CH], BF16) for i in range(2)]
        pM, pV, pD, pB = pt("f_pm"), pt("f_pv"), pt("f_pd"), pt("f_pb")
        pI = [pt(f"f_pi{i}") for i in range(4)]
        par_loaded = sem("f_par_loaded")
        consts = sem("f_consts")
        bias_sum = sem("f_bias_sum")
        folded = sem("f_folded")
        in_loaded = [sem(f"f_in_loaded{i}") for i in range(2)]
        mean_done = sem("f_mean")
        centred = sem("f_centred")
        squared = sem("f_squared")
        var_done = sem("f_var")
        std_done = sem("f_std")
        rstd_done = sem("f_rstd")
        normed = sem("f_normed")
        projected = sem("f_projected")
        xc_evac = sem("f_xc_evac")
        z_evac = sem("f_z_evac")
        halo_ready = sem("f_halo_ready")
        conv_step = sem("f_conv_step")
        silu_done = sem("f_silu_done")
        dts_done = sem("f_dts_done")
        bc_done = sem("f_bc_done")
        dts_evac = sem("f_dts_evac")
        hi_done = sem("f_hi_done")
        rest_done = sem("f_rest_done")
        mid_done = sem("f_mid_done")
        lo_done = sem("f_lo_done")
        z_stored = [sem(f"f_z_stored{i}") for i in range(2)]
        x_stored = [sem(f"f_x_stored{i}") for i in range(2)]
        tick = sem("f_tick")
        block = ctx.enter_context(nc.Block())
        v3 = lambda t: t.rearrange("(b g p) n -> b p g n", b=B, g=2)
        STEPS = NCH + 2

        def img(ap):
            return ap.rearrange("p (h w) -> p h w", w=W)

        def use(c, b):
            return (3 if c % 2 else 4) * b + c // 2

        @block.sync
        def _(sp):
            with nc.allow_non_contiguous_dma(reason="small vectors, once"):
                sp.dma_start(wo[:, :, :], in_wT.rearrange("(g p) o -> p g o", p=G)).then_inc(par_loaded, 16)
                sp.dma_start(wd[:, :, :], dts_wT.rearrange("(g p) o -> p g o", p=G)).then_inc(par_loaded, 16)
                sp.dma_start(wb[:, :, :], bc_wT.rearrange("(g p) o -> p g o", p=G)).then_inc(par_loaded, 16)
                sp.dma_start(cw[:, :, :], conv_w.rearrange("(g p) k -> p g k", p=G)).then_inc(par_loaded, 16)
                for dst, src in ((cb, conv_b), (lg, ln_w), (lb, ln_b)):
                    sp.dma_start(dst[:, :], src.rearrange("(g p) -> p g", p=G)).then_inc(par_loaded, 16)

            def load(b, c):
                sp.wait_ge(centred, NCH * b + max(c - 1, 0))
                sp.sem_inc(tick, 1)
                sp.dma_start(xin[c % 2][:, :, :], v3(x3)[b, :, :, c * CH:(c + 1) * CH]).then_inc(in_loaded[c % 2], 16)

            with sp.Fori(0, B) as b:
                for k in range(STEPS + 1):
                    if k < NCH:
                        load(b, k)
                    c1, c2 = k - 1, k - 3
                    if 0 <= c1 < NCH:
                        o = c1 % 2
                        sp.wait_ge(z_evac, NCH * b + c1 + 1)
                        sp.sem_inc(tick, 1)
                        sp.dma_start(v3(zs)[b, :, :, c1 * CH:(c1 + 1) * CH], zo[o][:, :, :]).then_inc(z_stored[o], 16)
                    if 0 <= c2 < NCH:
                        o = c2 % 2
                        sl = slice(c2 * CH, (c2 + 1) * CH)
                        sp.wait_ge(lo_done, NCH * b + c2 + 1)
                        sp.sem_inc(tick, 1)
                        sp.wait_ge(dts_evac, NCH * b + c2 + 1)
                        sp.sem_inc(tick, 1)
                        sp.dma_start(v3(xc)[b, :, :, sl], xo[o][:, :, :]).then_inc(x_stored[o], 16)
                        sp.dma_start(dts[b, :, sl], do[o][:, :]).then_inc(x_stored[o], 16)
                        sp.dma_start(bcs[b, :, sl], bo[o][:, :]).then_inc(x_stored[o], 16)
            for o in range(2):
                sp.wait_ge(z_stored[o], 16 * (4 - o) * B)
                sp.wait_ge(x_stored[o], 48 * (4 - o) * B)

        @block.gpsimd
        def _(p):
            for i in range(R3):
                p.memset(ct[i][:, :, :, :], 0.0).then_inc(consts, 1)
            with p.Fori(0, B) as b:
                for c in range(NCH):
                    o = c % R3
                    p.wait_ge(xc_evac, NCH * b + c + 1)
                    p.sem_inc(tick, 1)
                    if c == 0:
                        p.memset(ct[o][:, :, 0, :], 0.0)
                    else:
                        p.tensor_copy(ct[o][:, :, 0, :], ct[(c - 1) % R3][:, :, 8, :])
                        p.tensor_copy(ct[(c - 1) % R3][:, :, 9, :], ct[o][:, :, 1, :])
                    if c == NCH - 1:
                        p.memset(ct[o][:, :, 9, :], 0.0)
                    p.drain().then_inc(halo_ready, 1)

        @block.tensor
        def _(pe):
            pe.wait_ge(par_loaded, 16 * 7)
            pe.wait_ge(consts, R3 + 1)
            for m in range(4):
                for g in range(2):
                    mm = pe.matmul(pD[:, m:m + 1], wo[:, g, G * m:G * m + G], lb[:, g:g + 1], start=(g == 0), stop=(g == 1))
            mm.then_inc(bias_sum, 1)
            pe.wait_ge(folded, 3)

            def moment(bank, src, done):
                for g in range(2):
                    mm = pe.matmul(bank[:, 0:CH], m192[:, :], src[:, g, :], start=(g == 0), stop=(g == 1))
                mm.then_inc(done, 1)

            with pe.Fori(0, B) as b:
                for k in range(STEPS):
                    c2 = k - 2
                    q, q2 = NCH * b + k, NCH * b + c2
                    if k < NCH:
                        pe.wait_ge(in_loaded[k % 2], 16 * (use(k, b) + 1))
                        pe.wait_ge(centred, q)
                        moment(pM, xin[k % 2], mean_done)
                        pe.wait_ge(squared, q + 1)
                        pe.wait_ge(std_done, q)
                        moment(pV, sq, var_done)
                    if 0 <= c2:
                        o = c2 % 2
                        pe.wait_ge(silu_done, q2 + 1)
                        pe.wait_ge(dts_evac, q2)
                        for g in range(2):
                            mm = pe.matmul(pD[0:KD * RANK, 0:CH], wd[:, g, :], xo[o][:, g, :], start=(g == 0), stop=(g == 1))
                        mm.then_inc(dts_done, 1)
                        pe.wait_ge(rest_done, q2)
                        for g in range(2):
                            mm = pe.matmul(pB[:, 0:CH], wb3[:, g, :, :].rearrange("p a b -> p (a b)"), xo[o][:, g, :], start=(g == 0), stop=(g == 1))
                        mm.then_inc(bc_done, 1)
                    if k < NCH:
                        pe.wait_ge(normed, q + 1)
                        pe.wait_ge(xc_evac, q)
                        pe.wait_ge(z_evac, q)
                        for m in range(4):
                            for g in range(2):
                                mm = pe.matmul(pI[m][:, 0:CH], w[:, g, G * m:G * m + G], xn[:, g, :], start=(g == 0), stop=(g == 1))
                            mm.then_inc(projected, 1)

        @block.scalar
        def _(a):
            a.wait_ge(par_loaded, 16 * 7)
            a.wait_ge(folded, 3)
            a.wait_ge(consts, R3 + 1)
            with a.Fori(0, B) as b:
                for k in range(STEPS):
                    c2 = k - 2
                    q, q2 = NCH * b + k, NCH * b + c2
                    if k < NCH:
                        o = k % 2
                        a.wait_ge(centred, q + 1)
                        a.activation(sq[:, :, :], ce[o][:, :, :], ACT.Square).then_inc(squared, 1)
                        a.wait_ge(var_done, q + 1)
                        a.wait_ge(normed, q)
                        a.activation(rs[:, :], pV[:, 0:CH], ACT.Sqrt, bias=EPS).then_inc(std_done, 1)
                    if 0 <= c2:
                        o = c2 % 2
                        a.wait_ge(conv_step, 18 * q2 + 18)
                        a.wait_ge(x_stored[o], 48 * use(c2, b))
                        a.activation(xo[o][:, :, :], cv[:, :, :], ACT.Silu).then_inc(silu_done, 1)
                        a.wait_ge(bc_done, q2 + 1)
                        a.wait_ge(lo_done, q2)
                        a.activation(hi[:, :], pB[:, 0:CH], ACT.Copy).then_inc(hi_done, 1)
                        a.wait_ge(dts_done, q2 + 1)
                        a.activation(do[o][:, :], pD[0:KD * RANK, 0:CH], ACT.Copy).then_inc(dts_evac, 1)
                    if k < NCH:
                        o = k % 2
                        a.wait_ge(z_stored[o], 16 * use(k, b))
                        a.wait_ge(conv_step, 18 * (NCH * b + max(k - 2, 0)))
                        for g in range(2):
                            a.wait_ge(projected, 4 * q + g + 1)
                            last = a.activation(ct[k % R3][:, g, 1:9, 1:1 + W], img(pI[g][:, 0:CH]), ACT.Identity, bias=bi[:, g:g + 1])
                        last.then_inc(xc_evac, 1)
                        for g in range(2):
                            a.wait_ge(projected, 4 * q + g + 3)
                            last = a.activation(zo[o][:, g, :], pI[2 + g][:, 0:CH], ACT.Silu, bias=bi[:, 2 + g:3 + g])
                        last.then_inc(z_evac, 1)
                    if 0 <= c2:
                        a.wait_ge(rest_done, q2 + 1)
                        a.activation(mid[:, :], r1[:, :], ACT.Copy).then_inc(mid_done, 1)

        @block.vector
        def _(v):
            v.memset(m192[:, :], 1.0 / C).then_inc(consts, 1)
            v.wait_ge(par_loaded, 16 * 7)
            for g in range(2):
                for i in range(3):
                    v.tensor_copy(wb3[:, g, i, :], wb[:, g, :])
                v.tensor_scalar(w[:, g, :], wo[:, g, :], lg[:, g:g + 1], None, ALU.mult).then_inc(folded, 1)
            v.wait_ge(bias_sum, 1)
            v.tensor_copy(bi[:, :], pD[:, 0:4]).then_inc(folded, 1)
            with v.Fori(0, B) as b:
                for k in range(STEPS):
                    c2 = k - 2
                    q, q2 = NCH * b + k, NCH * b + c2
                    if k < NCH:
                        v.wait_ge(mean_done, q + 1)
                        v.tensor_tensor(ce[k % 2][:, :, :], xin[k % 2][:, :, :],
                                        pM[:, 0:CH].rearrange("p (o m) -> p o m", o=1).broadcast_to([G, 2, CH]), ALU.subtract).then_inc(centred, 1)
                    if 0 <= c2:
                        v.wait_ge(halo_ready, q2 + 2 if c2 + 1 < NCH else q2 + 1)
                        v.wait_ge(silu_done, q2)
                        for t in range(9):
                            dy, dx = divmod(t, 3)
                            for g in range(2):
                                src = ct[c2 % R3][:, g, dy:dy + 8, dx:dx + W]
                                dst = img(cv[:, g, :])
                                if t == 0:
                                    v.tensor_scalar(dst, src, cw[:, g, 0:1], cb[:, g:g + 1], ALU.mult, ALU.add).then_inc(conv_step, 1)
                                else:
                                    v.wait_ge(conv_step, 18 * q2 + 2 * (t - 1) + g + 1)
                                    v.scalar_tensor_tensor(dst, src, cw[:, g, t:t + 1], dst, ALU.mult, ALU.add).then_inc(conv_step, 1)
                    if k < NCH:
                        v.wait_ge(std_done, q + 1)
                        v.reciprocal(rs[:, :], rs[:, :]).then_inc(rstd_done, 1)
                        v.wait_ge(rstd_done, q + 1)
                        v.wait_ge(projected, 4 * q)
                        v.tensor_tensor(xn[:, :, :], ce[k % 2][:, :, :],
                                        rs[:, :].rearrange("p (o m) -> p o m", o=1).broadcast_to([G, 2, CH]), ALU.mult).then_inc(normed, 1)
                    if 0 <= c2:
                        v.wait_ge(hi_done, q2 + 1)
                        v.wait_ge(mid_done, q2)
                        v.tensor_tensor(r1[:, :], pB[:, 0:CH], hi[:, :], ALU.subtract).then_inc(rest_done, 1)
                        o = c2 % 2
                        v.wait_ge(x_stored[o], 48 * use(c2, b))
                        v.tensor_copy(bo[o][0:32, :], hi[0:32, :])
                        v.wait_ge(mid_done, q2 + 1)
                        v.tensor_copy(bo[o][32:64, :], mid[32:64, :])
                        v.tensor_tensor(bo[o][64:96, :], r1[64:96, :], mid[64:96, :], ALU.subtract).then_inc(lo_done, 1)


def scan_outputs(nc, x3, ys, zs, on_w, on_b, out_wT, out):
    with ExitStack() as ctx:
        sb = lambda name, shape, dt=F32: ctx.enter_context(nc.sbuf_tensor(name, shape, dt))
        pt = lambda name: ctx.enter_context(nc.psum_tensor(name, [G, 512], F32))
        sem = ctx.enter_context(stage_semaphores(nc))
        w = sb("h_w", [G, 2, C])
        og = sb("h_og", [G, 2])
        ob = sb("h_ob", [G, 2])
        m192 = sb("h_m192", [G, G])
        yin = [sb(f"h_yin{i}", [G, 2, CH]) for i in range(2)]
        zin = [sb(f"h_zin{i}", [G, 2, CH]) for i in range(R3)]
        xin = [sb(f"h_xin{i}", [G, 2, CH]) for i in range(R3)]
        ce = [sb(f"h_ce{i}", [G, 2, CH]) for i in range(2)]
        sq = sb("h_sq", [G, 2, CH])
        rs = [sb(f"h_rs{i}", [G, CH]) for i in range(2)]
        yn = [sb(f"h_yn{i}", [G, 2, CH]) for i in range(2)]
        ot = [sb(f"h_ot{i}", [G, 2, CH]) for i in range(2)]
        pM = [pt(f"h_pm{i}") for i in range(2)]
        pV = [pt(f"h_pv{i}") for i in range(2)]
        pO = [pt(f"h_po{i}") for i in range(2)]
        par_loaded = sem("h_par_loaded")
        consts = sem("h_consts")
        y_loaded = [sem(f"h_y_loaded{i}") for i in range(2)]
        zx_loaded = [sem(f"h_zx_loaded{i}") for i in range(R3)]
        mean_done = sem("h_mean")
        centred = sem("h_centred")
        squared = sem("h_squared")
        var_done = sem("h_var")
        std_done = sem("h_std")
        rstd_done = sem("h_rstd")
        normed = sem("h_normed")
        affine = sem("h_affine")
        gated = sem("h_gated")
        projected = sem("h_projected")
        finished = sem("h_finished")
        stored = [sem(f"h_stored{i}") for i in range(2)]
        tick = sem("h_tick")
        block = ctx.enter_context(nc.Block())
        v3 = lambda t: t.rearrange("(b g p) n -> b p g n", b=B, g=2)
        xo = out.rearrange("b (g p) h w -> b p g (h w)", g=2)
        uses = [len([c for c in range(NCH) if c % R3 == i]) for i in range(R3)]

        def use(c, b):
            return (3 if c % 2 else 4) * b + c // 2

        @block.sync
        def _(sp):
            with nc.allow_non_contiguous_dma(reason="small vectors, once"):
                sp.dma_start(w[:, :, :], out_wT.rearrange("(g p) o -> p g o", p=G)).then_inc(par_loaded, 16)
                sp.dma_start(og[:, :], on_w.rearrange("(g p) -> p g", p=G)).then_inc(par_loaded, 16)
                sp.dma_start(ob[:, :], on_b.rearrange("(g p) -> p g", p=G)).then_inc(par_loaded, 16)
            with sp.Fori(0, B) as b:
                for c in range(NCH):
                    sl = slice(c * CH, (c + 1) * CH)
                    sp.wait_ge(centred, NCH * b + max(c - 1, 0))
                    sp.sem_inc(tick, 1)
                    sp.dma_start(yin[c % 2][:, :, :], v3(ys)[b, :, :, sl]).then_inc(y_loaded[c % 2], 16)
                    sp.wait_ge(finished, 2 * (NCH * b + max(c - 2, 0)))
                    sp.sem_inc(tick, 1)
                    sp.dma_start(zin[c % R3][:, :, :], v3(zs)[b, :, :, sl]).then_inc(zx_loaded[c % R3], 16)
                    sp.dma_start(xin[c % R3][:, :, :], v3(x3)[b, :, :, sl]).then_inc(zx_loaded[c % R3], 16)

        @block.gpsimd
        def _(p):
            with p.Fori(0, B) as b:
                for c in range(NCH):
                    p.wait_ge(finished, 2 * (NCH * b + c + 1))
                    p.sem_inc(tick, 1)
                    p.dma_start(xo[b, :, :, c * CH:(c + 1) * CH], ot[c % 2][:, :, :]).then_inc(stored[c % 2], 16)
            for o in range(2):
                p.wait_ge(stored[o], 16 * (4 - o) * B)

        @block.tensor
        def _(pe):
            pe.wait_ge(par_loaded, 48)
            pe.wait_ge(consts, 1)
            with pe.Fori(0, B) as b:
                for k in range(NCH + 1):
                    q = NCH * b + k
                    if k < NCH:
                        pe.wait_ge(y_loaded[k % 2], 16 * (use(k, b) + 1))
                        pe.wait_ge(centred, NCH * b + max(k - 1, 0))
                        for g in range(2):
                            mm = pe.matmul(pM[k % 2][:, 0:CH], m192[:, :], yin[k % 2][:, g, :], start=(g == 0), stop=(g == 1))
                        mm.then_inc(mean_done, 1)
                        pe.wait_ge(squared, q + 1)
                        pe.wait_ge(std_done, NCH * b + max(k - 1, 0))
                        for g in range(2):
                            mm = pe.matmul(pV[k % 2][:, 0:CH], m192[:, :], sq[:, g, :], start=(g == 0), stop=(g == 1))
                        mm.then_inc(var_done, 1)
                    if k >= 1:
                        for m in range(2):
                            if m == 0:
                                pe.wait_ge(gated, q)
                            pe.wait_ge(finished, 2 * (q - 1) if m == 0 else 2 * (q - 1))
                            for g in range(2):
                                mm = pe.matmul(pO[m][:, 0:CH], w[:, g, G * m:G * m + G], yn[(k - 1) % 2][:, g, :], start=(g == 0), stop=(g == 1))
                            mm.then_inc(projected, 1)

        @block.scalar
        def _(a):
            a.wait_ge(par_loaded, 48)
            with a.Fori(0, B) as b:
                for k in range(NCH + 1):
                    q = NCH * b + k
                    if k < NCH:
                        a.wait_ge(centred, q + 1)
                        a.wait_ge(var_done, q)
                        a.activation(sq[:, :, :], ce[k % 2][:, :, :], ACT.Square).then_inc(squared, 1)
                        a.wait_ge(var_done, q + 1)
                        a.wait_ge(normed, NCH * b + max(k - 1, 0))
                        a.activation(rs[k % 2][:, :], pV[k % 2][:, 0:CH], ACT.Sqrt, bias=EPS).then_inc(std_done, 1)
                        a.wait_ge(normed, q + 1)
                        for g in range(2):
                            last = a.activation(yn[k % 2][:, g, :], yn[k % 2][:, g, :], ACT.Identity, bias=ob[:, g:g + 1], scale=og[:, g:g + 1])
                        last.then_inc(affine, 1)

        @block.vector
        def _(v):
            v.memset(m192[:, :], 1.0 / C).then_inc(consts, 1)
            with v.Fori(0, B) as b:
                for k in range(NCH + 1):
                    q = NCH * b + k
                    bc = lambda t: t.rearrange("p (o m) -> p o m", o=1).broadcast_to([G, 2, CH])
                    if k < NCH:
                        o = k % 2
                        v.wait_ge(mean_done, q + 1)
                        v.tensor_tensor(ce[o][:, :, :], yin[o][:, :, :], bc(pM[o][:, 0:CH]), ALU.subtract).then_inc(centred, 1)
                        v.wait_ge(std_done, q + 1)
                        v.reciprocal(rs[o][:, :], rs[o][:, :]).then_inc(rstd_done, 1)
                        v.wait_ge(rstd_done, q + 1)
                        v.wait_ge(projected, 2 * (NCH * b + max(k - 1, 0)))
                        v.tensor_tensor(yn[o][:, :, :], ce[o][:, :, :], bc(rs[o][:, :]), ALU.mult).then_inc(normed, 1)
                    if k >= 1:
                        o = (k - 1) % 2
                        v.wait_ge(stored[o], 16 * use(k - 1, b))
                        for m in range(2):
                            v.wait_ge(projected, 2 * (q - 1) + m + 1)
                            v.tensor_tensor(ot[o][:, m, :], pO[m][:, 0:CH], xin[(k - 1) % R3][:, m, :], ALU.add).then_inc(finished, 1)
                    if k < NCH:
                        o = k % R3
                        v.wait_ge(zx_loaded[o], 32 * (uses[o] * b + k // R3 + 1))
                        v.wait_ge(affine, q + 1)
                        v.tensor_tensor(yn[k % 2][:, :, :], yn[k % 2][:, :, :], zin[o][:, :, :], ALU.mult).then_inc(gated, 1)


def scans(nc, xc, dts, bcs, dt_wT, dt_b, a_log, ds, sel, ys):
    with ExitStack() as ctx:
        sb = lambda name, shape, dt=F32: ctx.enter_context(nc.sbuf_tensor(name, shape, dt))
        pt = lambda name: ctx.enter_context(nc.psum_tensor(name, [128, 512], F32))
        sem = ctx.enter_context(stage_semaphores(nc))
        wd = sb("s_wd", [RANK, KD, C])
        db = sb("s_db", [128, 3, KD])
        al = sb("s_al", [128, 3, KD * NST])
        dsk = sb("s_dsk", [128, 3, KD])
        dsum = sb("s_dsum", [128, 3])
        selt = sb("s_sel", [G, NBC], BF16)
        bct = [sb(f"s_bct{i}", [G, N], BF16) for i in range(2)]
        dtt = [sb(f"s_dtt{i}", [RANK, 2, CH]) for i in range(2)]
        xt = [sb(f"s_xt{i}", [128, N]) for i in range(3)]
        yt = [sb(f"s_yt{i}", [128, N]) for i in range(2)]
        dt = [sb(f"s_dt{i}", [128, N]) for i in range(2)]
        dtu = [sb(f"s_dtu{i}", [128, N]) for i in range(2)]
        tmp = sb("s_tmp", [128, N])
        da = [sb(f"s_da{i}", [128, N]) for i in range(2)]
        dbu = sb("s_dbu", [128, N])
        hs = sb("s_hs", [128, N])
        prod = sb("s_prod", [128, RP, CH])
        pB = [pt(f"s_pb{i}") for i in range(3)]
        pC = [pt(f"s_pc{i}") for i in range(3)]
        pD = [pt(f"s_pd{i}") for i in range(2)]
        par_loaded = sem("s_par_loaded")
        a_exp = sem("s_a_exp")
        a_ready = sem("s_a_ready")
        bc_loaded = sem("s_bc_loaded")
        x_loaded = [sem(f"s_x_loaded{i}") for i in range(3)]
        dts_loaded = [sem(f"s_dts_loaded{i}") for i in range(2)]
        step_done = sem("s_step_done")
        step_evac = sem("s_step_evac")
        exp_taken = sem("s_exp_taken")
        log_taken = sem("s_log_taken")
        dt_ready = sem("s_dt_ready")
        dtu_ready = sem("s_dtu_ready")
        b_spread = sem("s_b_spread")
        c_spread = sem("s_c_spread")
        b_used = sem("s_b_used")
        c_used = sem("s_c_used")
        decay_ready = sem("s_decay_ready")
        scanned = sem("s_scanned")
        y_begun = sem("s_y_begun")
        y_added = sem("s_y_added")
        stored = [sem(f"s_stored{i}") for i in range(2)]
        tick = sem("s_tick")
        block = ctx.enter_context(nc.Block())
        NP2 = B // 2
        NB = NIT * NCH
        xv = xc.rearrange("(q u p) n -> q u p n", u=3, p=128)
        yv = ys.rearrange("(q u p) n -> q u p n", u=3, p=128)
        dv = dts.rearrange("(q i) (k r) n -> q k r i n", i=2, k=KD)
        bv = bcs.rearrange("(q i) r n -> q i r n", i=2)

        def chunk(t, c, k):
            if k % 2:
                return t.rearrange("p (w h) -> p h w", h=H)[:, 8 * c:8 * c + 8, :]
            return t[:, c * CH:(c + 1) * CH].rearrange("p (h w) -> p h w", w=W)

        def img(t):
            return t.rearrange("p (h w) -> p h w", w=W)

        def along(t, k):
            return t[:, ::-1] if k >= 2 else t[:, :]

        @block.sync
        def _(sp):
            with nc.allow_non_contiguous_dma(reason="small vectors, once"):
                sp.dma_start(wd[:, :, :], dt_wT.rearrange("k r d -> r k d")).then_inc(par_loaded, 16)
                sp.dma_start(db[:, :, :], dt_b.rearrange("(u p) k -> p u k", p=128)).then_inc(par_loaded, 16)
                sp.dma_start(al[:, :, :], a_log.rearrange("(u p) k -> p u k", p=128)).then_inc(par_loaded, 16)
                sp.dma_start(dsk[:, :, :], ds.rearrange("(u p) k -> p u k", p=128)).then_inc(par_loaded, 16)
                sp.dma_start(selt[:, :], sel).then_inc(par_loaded, 16)
            with sp.Fori(0, NP2) as q:
                sp.wait_ge(b_spread, NB * q)
                sp.sem_inc(tick, 1)
                sp.wait_ge(c_spread, NB * q)
                sp.sem_inc(tick, 1)
                for i in range(2):
                    sp.dma_start(bct[i][:, :], bv[q, i]).then_inc(bc_loaded, 16)
                for u in range(3):
                    sp.wait_ge(dtu_ready, NSEC * q)
                    sp.sem_inc(tick, 1)
                    sp.wait_ge(y_begun, 3 * q)
                    sp.sem_inc(tick, 1)
                    sp.dma_start(xt[u][:, :], xv[q, u]).then_inc(x_loaded[u], 16)
                for s in range(NSEC):
                    for c in range(NCH):
                        n = NCH * s + c
                        sp.wait_ge(step_done, NSEC * NCH * q + max(n - 1, 0))
                        sp.sem_inc(tick, 1)
                        sp.dma_start(dtt[n % 2][:, :, :], dv[q, s % KD, :, :, c * CH:(c + 1) * CH]).then_inc(dts_loaded[n % 2], 16)

        @block.tensor
        def _(pe):
            pe.wait_ge(par_loaded, 80)

            def steps(q, s):
                u, k = divmod(s, KD)
                for c in range(NCH):
                    n = NCH * s + c
                    pe.wait_ge(dts_loaded[n % 2], 16 * (NSEC * NCH // 2 * q + n // 2 + 1))
                    pe.wait_ge(step_evac, NSEC * NCH * q + max(n - 1, 0))
                    pe.sem_inc(tick, 1)
                    for i, d0, p0, m in PIECES[u]:
                        mm = pe.matmul(pD[n % 2][p0:p0 + m, 0:CH], wd[:, k, d0:d0 + m], dtt[n % 2][:, i, :], start=True, stop=True)
                    mm.then_inc(step_done, 1)

            def rows(q, e, banks, used, done, bc):
                s, n = divmod(e, NST)
                u, k = divmod(s, KD)
                row = (2 * k + bc) * NST + n
                for c in range(NCH):
                    j = NCH * e + c
                    pe.wait_ge(used, NB * q + max(j - 2, 0))
                    pe.sem_inc(tick, 1)
                    for i, d0, p0, m in PIECES[u]:
                        mm = pe.matmul(banks[j % 3][p0:p0 + m, 0:CH], selt[:, row:row + 1].broadcast_to([G, m]),
                                       bct[i][:, c * CH:(c + 1) * CH], start=True, stop=True)
                    mm.then_inc(done, 1)

            with pe.Fori(0, NP2) as q:
                steps(q, 0)
                pe.wait_ge(bc_loaded, 32 * (q + 1))
                for s in range(NSEC):
                    for n in range(NST):
                        e = NST * s + n
                        rows(q, e, pB, b_used, b_spread, 0)
                        rows(q, e, pC, c_used, c_spread, 1)
                        if n == 0 and s + 1 < NSEC:
                            steps(q, s + 1)

        @block.scalar
        def _(a):
            a.wait_ge(par_loaded, 80)
            a.activation(al[:, :, :], al[:, :, :], ACT.Exp).then_inc(a_exp, 1)
            a.wait_ge(a_ready, 2)

            def begin(q, u):
                a.wait_ge(x_loaded[u], 16 * (q + 1))
                a.wait_ge(stored[u % 2], 16 * ((1 if u % 2 else 2) * q + u // 2))
                a.activation(yt[u % 2][:, :], xt[u][:, :], ACT.Copy, scale=dsum[:, u:u + 1]).then_inc(y_begun, 1)

            def softplus(q, s):
                u, k = divmod(s, KD)
                o = s % 2
                a.wait_ge(dtu_ready, NSEC * q + max(s, 0))
                for c in range(NCH):
                    n = NCH * s + c
                    sl = slice(c * CH, (c + 1) * CH)
                    a.wait_ge(step_done, NSEC * NCH * q + n + 1)
                    a.activation(dt[o][:, sl], pD[n % 2][:, 0:CH], ACT.Relu, bias=db[:, u, k:k + 1])
                    a.activation(tmp[:, sl], pD[n % 2][:, 0:CH], ACT.Abs, bias=db[:, u, k:k + 1]).then_inc(step_evac, 1)
                a.wait_ge(step_evac, NSEC * NCH * q + NCH * (s + 1))
                a.activation(tmp[:, :], tmp[:, :], ACT.Exp, scale=-1.0).then_inc(exp_taken, 1)
                a.wait_ge(exp_taken, NSEC * q + s + 1)
                a.activation(tmp[:, :], tmp[:, :], ACT.Ln, bias=1.0).then_inc(log_taken, 1)

            def decay(q, e):
                s, n = divmod(e, NST)
                u, k = divmod(s, KD)
                if n == 0:
                    a.wait_ge(dt_ready, NSEC * q + s + 1)
                a.wait_ge(scanned, NIT * q + max(e - 1, 0))
                src = dt[s % 2][:, :]
                dst = da[e % 2][:, :]
                if k % 2:
                    src = src.rearrange("p (h w) -> p w h", w=W)
                    dst = dst.rearrange("p (w h) -> p w h", h=H)
                a.activation(dst, src, ACT.Exp, scale=al[:, u, NST * k + n:NST * k + n + 1]).then_inc(decay_ready, 1)

            with a.Fori(0, NP2) as q:
                softplus(q, 0)
                for s in range(NSEC):
                    if s % KD == 0:
                        begin(q, s // KD)
                    decay(q, NST * s)
                    decay(q, NST * s + 1)
                    if s + 1 < NSEC:
                        softplus(q, s + 1)
                    decay(q, NST * s + 2)
                    decay(q, NST * s + 3)

        @block.vector
        def _(v):
            v.wait_ge(par_loaded, 80)
            v.tensor_reduce(dsum[:, :], dsk[:, :, :], AX.X, ALU.add).then_inc(a_ready, 1)
            v.wait_ge(a_exp, 1)
            v.tensor_scalar(al[:, :, :], al[:, :, :], -1.0, None, ALU.mult).then_inc(a_ready, 1)
            with v.Fori(0, NP2) as q:
                for e in range(NIT):
                    s, n = divmod(e, NST)
                    k = s % KD
                    if n == 0:
                        v.wait_ge(dtu_ready, NSEC * q + s + 1)
                    for c in range(NCH):
                        j = NCH * e + c
                        v.wait_ge(b_spread, NB * q + j + 1)
                        v.tensor_tensor(chunk(dbu[:, :], c, k), img(dtu[s % 2][:, c * CH:(c + 1) * CH]), img(pB[j % 3][:, 0:CH]),
                                        ALU.mult).then_inc(b_used, 1)
                    v.wait_ge(decay_ready, NIT * q + e + 1)
                    v.wait_ge(b_used, NB * q + NCH * (e + 1))
                    v.tensor_tensor_scan(along(hs, k), along(da[e % 2], k), along(dbu, k), 0.0, ALU.mult, ALU.add).then_inc(scanned, 1)
                    v.wait_ge(scanned, NIT * q + e + 1)
                    for c in range(NCH):
                        j = NCH * e + c
                        v.wait_ge(c_spread, NB * q + j + 1)
                        v.wait_ge(y_added, NB * q + max(j - RP + 1, 0))
                        v.tensor_tensor(img(prod[:, j % RP, :]), chunk(hs[:, :], c, k), img(pC[j % 3][:, 0:CH]), ALU.mult).then_inc(c_used, 1)

        @block.gpsimd
        def _(p):
            def step_size(q, s):
                p.wait_ge(log_taken, NSEC * q + s + 1)
                p.tensor_tensor(dt[s % 2][:, :], dt[s % 2][:, :], tmp[:, :], ALU.add).then_inc(dt_ready, 1)

            def step_input(q, s):
                p.wait_ge(dt_ready, NSEC * q + s + 1)
                p.wait_ge(x_loaded[s // KD], 16 * (q + 1))
                p.wait_ge(b_used, NB * q + NCH * NST * max(s - 1, 0))
                p.tensor_tensor(dtu[s % 2][:, :], dt[s % 2][:, :], xt[s // KD][:, :], ALU.mult).then_inc(dtu_ready, 1)

            with p.Fori(0, NP2) as q:
                step_size(q, 0)
                step_input(q, 0)
                for e in range(NIT):
                    s, n = divmod(e, NST)
                    u, k = divmod(s, KD)
                    if k == 0 and n == 0:
                        p.wait_ge(y_begun, 3 * q + u + 1)
                    for c in range(NCH):
                        j = NCH * e + c
                        p.wait_ge(c_used, NB * q + j + 1)
                        p.wait_ge(y_added, NB * q + max(j - NCH + 1, 0))
                        y = yt[u % 2][:, c * CH:(c + 1) * CH]
                        p.tensor_tensor(y, y, prod[:, j % RP, :], ALU.add).then_inc(y_added, 1)
                    if n == 1 and s + 1 < NSEC:
                        step_size(q, s + 1)
                    if n == 2 and s + 1 < NSEC:
                        step_input(q, s + 1)
                    if k == KD - 1 and n == NST - 1:
                        p.wait_ge(y_added, NB * q + NCH * (e + 1))
                        p.sem_inc(tick, 1)
                        p.dma_start(yv[q, u], yt[u % 2][:, :]).then_inc(stored[u % 2], 16)
            p.wait_ge(stored[0], 16 * 2 * NP2)
            p.wait_ge(stored[1], 16 * NP2)


def bc_selector():
    import numpy as np
    return np.tile(np.eye(NBC, dtype=mybir.dt.np(BF16)), (3, 1))


def network(nc, a, s, out):
    batchnorm_qkv(nc, a["x"], a["bn_gamma"], a["bn_beta"], a["qkv1_wT"], a["qkv1_b"], s["qkvp"])
    window_attention(nc, s["qkvp"], a["dm_wT"], a["dm_b"], a["rel_bias"], a["tap_sel"], a["ident"], s["att"])
    mixer(nc, a["x"], s["att"], a["proj1_wT"], a["proj1_b"], a["c1_wT"], a["c1_b"], a["c2_wT"], a["c2_b"], s["x1p"], s["xp"])
    channel_gate(nc, s["x1p"], s["xp"], a["wg1T"], a["bn2"], a["wg2T"], a["bg2"], a["beta"], a["w1T"], a["bn1"],
                 a["basis"], a["chan"], a["ident"], s["gate"])
    window_strips(nc, s["x1p"], s["gate"], a["inside"], a["n1g"], a["n1b"], a["qkv2_wT"], a["qkv2_b"], a["tempr"],
                  a["biasT"], a["proj2_wT"], a["proj2_b"], a["ident"], s["pout"])
    forward_block(nc, s["x1p"], s["gate"], s["pout"], a["hft_w"], a["hft_b"], a["n2g"], a["n2b"], a["fc1_wT"], a["fc1_b"],
                  a["sgn_g"], a["sgn_b"], a["sg_w"], a["sg_b"], a["fc2_wT"], a["fc2_b"], a["ident"], s["x3"])
    scan_inputs(nc, s["x3"], a["ln_w"], a["ln_b"], a["in_wT"], a["conv_w"], a["conv_b"], a["dts_wT"], a["bc_wT"],
                s["xc"], s["zs"], s["dts"], s["bcs"])
    scans(nc, s["xc"], s["dts"], s["bcs"], a["dt_wT"], a["dt_b"], a["a_log"], a["ds"], a["bc_sel"], s["ys"])
    scan_outputs(nc, s["x3"], s["ys"], s["zs"], a["on_w"], a["on_b"], a["out_wT"], out)


def kernel(**inputs):
    import numpy as np
    import concourse.bacc as bacc
    from concourse.bass_utils import run_bass_kernel_spmd

    v = {name: np.asarray(value) for name, value in inputs.items()}
    l0 = {name[8:]: a for name, a in v.items() if name.startswith("L0_conv_")}
    l1 = {name[8:]: a for name, a in v.items() if name.startswith("L1_conv_")}
    l2 = {name[8:]: a for name, a in v.items() if name.startswith("L2_conv_")}
    l3 = {name[8:]: a for name, a in v.items() if name.startswith("L3_conv_")}
    two = lambda a: np.tile(a, (2, 1))
    laid = dict(
        x=v["x"],
        bn_gamma=l0["bn_gamma"], bn_beta=l0["bn_beta"], qkv1_wT=l0["qkv_w"].T, qkv1_b=l0["qkv_b"],
        dm_wT=l0["dm_w"].transpose(1, 2, 3, 0), dm_b=l0["dm_b"], rel_bias=l0["rel_bias"], tap_sel=selector(),
        proj1_wT=l0["proj_w"].T, proj1_b=l0["proj_b"], c1_wT=l0["c1_w"].T, c1_b=l0["c1_b"],
        c2_wT=l0["c2_w"].T, c2_b=l0["c2_b"],
        wg1T=l1["wg1"].T, bn2=np.stack([l1["bn2_g"], l1["bn2_b"], l1["bn2_m"], l1["bn2_v"]]), wg2T=l1["wg2"].T,
        bg2=l1["bg2"], beta=l1["beta"], w1T=l1["w1d"][:, :, 1].T,
        bn1=np.stack([l1["bn1_g"], l1["bn1_b"], l1["bn1_m"], l1["bn1_v"], l1["b1d"]]),
        basis=dct_basis(), chan=channels(), ident=np.eye(128, dtype=np.float32), inside=inside(),
        n1g=l2["n1g"], n1b=l2["n1b"], qkv2_wT=l2["qkv_w"].T, qkv2_b=l2["qkv_b"],
        tempr=np.repeat(l2["temp"].reshape(HEADS), HD), biasT=relative(l2["rpb"]),
        proj2_wT=l2["proj_w"].T, proj2_b=l2["proj_b"],
        hft_w=l2["hft_w"].reshape(C, 9), hft_b=l2["hft_b"], n2g=l2["n2g"], n2b=l2["n2b"],
        fc1_wT=l2["fc1_w"].T, fc1_b=l2["fc1_b"], sgn_g=l2["sgn_g"], sgn_b=l2["sgn_b"],
        sg_w=l2["sg_w"].reshape(HID // 2, 9), sg_b=l2["sg_b"], fc2_wT=l2["fc2_w"].T, fc2_b=l2["fc2_b"],
        ln_w=l3["ln_w"], ln_b=l3["ln_b"], in_wT=l3["in_proj_w"].T, conv_w=l3["conv_w"].reshape(C, 9), conv_b=l3["conv_b"],
        dts_wT=l3["x_proj_w"][:, :RANK].reshape(KD * RANK, C).T, bc_wT=l3["x_proj_w"][:, RANK:].reshape(NBC, C).T,
        dt_wT=l3["dt_proj_w"].transpose(0, 2, 1), dt_b=two(l3["dt_proj_b"].T),
        a_log=two(l3["A_log"].transpose(1, 0, 2).reshape(C, KD * NST)), ds=two(l3["Ds"].T), bc_sel=bc_selector(),
        on_w=l3["out_norm_w"], on_b=l3["out_norm_b"], out_wT=l3["out_proj_w"].T,
    )
    between = dict(
        qkvp=((3, B * C, PW, PW), F32), att=((B * C, N), F32), x1p=((B * C, PW, PW), F32), xp=((B * C, DCT * DCT), F32),
        gate=((G, 2 * B), F32), pout=((B * C, NR * STEP, PW), F32), x3=((B * C, N), F32),
        xc=((B * C, N), F32), zs=((B * C, N), F32), dts=((B, KD * RANK, N), F32), bcs=((B, 3 * NBC, N), BF16),
        ys=((B * C, N), F32),
    )
    nc = bacc.Bacc("TRN2", target_bir_lowering=False, num_devices=1)
    arrays, args = {}, {}
    for name, a in laid.items():
        arrays[f"in_{name}"] = np.ascontiguousarray(a)
        args[name] = nc.dram_tensor(f"in_{name}", a.shape, mybir.dt.from_np(a.dtype), kind="ExternalInput").ap()
    scratch = {name: nc.dram_tensor(f"mid_{name}", shape, dt, kind="Internal").ap() for name, (shape, dt) in between.items()}
    out = nc.dram_tensor("out_y", (B, C, H, W), F32, kind="ExternalOutput").ap()
    network(nc, args, scratch, out)
    r = run_bass_kernel_spmd(nc, [arrays], core_ids=[0])
    return r.results[0]["out_y"]
```

```python
from contextlib import ExitStack, contextmanager
import concourse.bass as bass
from concourse import mybir
F32 = mybir.dt.float32
BF16 = mybir.dt.bfloat16
ALU = mybir.AluOpType
ACT = mybir.ActivationFunctionType
AX = mybir.AxisListType
B, C, H, W = 4, 192, 56, 56
N = H * W
G = 96
NCH = 7
CH = 8 * W
PW = 62
PN = PW * PW
HD = 32
EPS = 1e-5

PLACE = [0, 1, 2, 0, 1, 2, 3]
USES = [PLACE.count(i) for i in range(4)]


def pipeline(eng, step, lag):
    for k in range(NCH):
        step(0, k)
    with eng.Fori(1, B) as b:
        for k in range(NCH):
            step(b, k)
    for k in range(lag):
        step(B, k)


def chunk(b, k, lag):
    if k >= lag:
        return None if isinstance(b, int) and b == B else (b, k - lag)
    return None if isinstance(b, int) and b == 0 else (b - 1, k - lag + NCH)


def turns(b, c):
    return USES[PLACE[c]] * b + PLACE[:c].count(PLACE[c])


def before(b, c, n, per=1):
    if isinstance(b, int) and NCH * b + c - n + 1 < 0:
        return 0
    return per * (NCH * b + c - n + 1)

NU = 6
TAPS = 49
K1 = 10
NS = 5
NT = 14
MB = 28
G_TAPS = [k for k in range(TAPS) if k % 5 in (0, 2, 4)]
D_TAPS = [k for k in range(TAPS) if k % 5 in (1, 3)]
NSTEP = NCH * TAPS
SLOTS = 17 * MB
AGG_SLOT = [12 + a * (SLOTS - 14) // NSTEP for a in range(NSTEP)]
NGA = (len(G_TAPS) - 1) * NCH
NDA = (len(D_TAPS) - 1) * NCH
GR, DR = 6, 2
F = 4 * C
DCT = 7
LOW_X = [0, 0, 1, 1, 0, 2, 2, 1, 2, 0, 3, 4, 0, 1, 3, 0, 1, 2, 3, 4, 5, 0, 1, 2, 3, 4, 5, 6, 1, 2, 3, 4]
LOW_Y = [0, 1, 0, 1, 2, 0, 1, 2, 2, 3, 0, 0, 4, 3, 1, 5, 4, 3, 2, 1, 0, 6, 5, 4, 3, 2, 1, 0, 6, 5, 4, 3]
NF = 32
ROUND = 1.5 * 2.0 ** 23
HEADS = 6
WS = 8
STEP = 6
NR = 10
SN = WS * PW
ON = STEP * PW
NP = NR // 2
HID = 4 * C
AW = W + 2
LAG = 6
AW = W + 2
SLAG = 5
KD, NST, RANK = 4, 4, 12
NBC = 2 * KD * NST
NSEC = 3 * KD
NIT = NSEC * NST
AMONG = {(0, 0): (0,), (0, 1): (1, 2, 3), (1, 0): (4,), (1, 1): (5, 6)}
SR = 4
RP = 10
PIECES = [[(0, 0, 0, 128)], [(0, 128, 0, 64), (1, 0, 64, 64)], [(1, 64, 0, 128)]]


def pipeline(eng, step, lag):
    for k in range(NCH):
        step(0, k)
    with eng.Fori(1, B) as b:
        for k in range(NCH):
            step(b, k)
    for k in range(lag):
        step(B, k)


def chunk(b, k, lag):
    if k >= lag:
        return None if isinstance(b, int) and b == B else (b, k - lag)
    return None if isinstance(b, int) and b == 0 else (b - 1, k - lag + NCH)


def turns(b, c):
    return USES[PLACE[c]] * b + PLACE[:c].count(PLACE[c])


def before(b, c, n, per=1):
    if isinstance(b, int) and NCH * b + c - n + 1 < 0:
        return 0
    return per * (NCH * b + c - n + 1)


@contextmanager
def stage_semaphores(nc):
    held = []

    def sem(name):
        held.append(nc.alloc_semaphore(name))
        return held[-1]
    yield sem
    nc.clear_and_free_semaphores(held)
    nc.all_engine_barrier()


def batchnorm_qkv(nc, x, gamma, beta, qkv_wT, qkv_b, qkvp):
    with ExitStack() as ctx:
        sb = lambda name, shape, dt=F32: ctx.enter_context(nc.sbuf_tensor(name, shape, dt))
        sem = ctx.enter_context(stage_semaphores(nc))
        xs = sb("a_x", [G, 2, B, N])
        wt = sb("a_wt", [G, 2, 3 * C])
        wf = sb("a_wf", [G, 2, 3 * C])
        par = sb("a_par", [G, 2, 2])
        qb = sb("a_qb", [G, 6])
        stats = sb("a_stats", [G, 2, B * NCH, 6])
        mv = sb("a_mv", [G, 2, 2])
        std = sb("a_std", [G, 2])
        sc = sb("a_sc", [G, 2])
        sh = sb("a_sh", [G, 2])
        bias = sb("a_bias", [G, 6])
        zero = sb("a_zero", [G, B * 2, 3 * PW])
        out = [sb(f"a_out{i}", [G, 6, 8, PW]) for i in range(2)]
        ps = [ctx.enter_context(nc.psum_tensor(f"a_ps{i}", [G, 512], F32)) for i in range(4)]
        psb = ctx.enter_context(nc.psum_tensor("a_psb", [G, 512], F32))
        x_loaded = [sem(f"a_x_loaded{b}") for b in range(B)]
        par_loaded = sem("a_par_loaded")
        zero_set = sem("a_zero_set")
        border_stored = sem("a_border_stored")
        stats_done = sem("a_stats_done")
        norm_step = sem("a_norm_step")
        std_done = sem("a_std_done")
        bias_summed = sem("a_bias_summed")
        folded = sem("a_folded")
        product = sem("a_product")
        evacuated_even = sem("a_evacuated_even")
        evacuated_odd = sem("a_evacuated_odd")
        stored = [sem(f"a_stored{i}") for i in range(2)]
        block = ctx.enter_context(nc.Block())
        xv = x.rearrange("b (g p) h w -> b p g (h w)", g=2)
        qv = qkvp.rearrange("t (b g p) h w -> t b p g (h w)", b=B, g=2)

        @block.sync
        def _(sp):
            for b in range(B):
                sp.dma_start(xs[:, :, b, :], xv[b]).then_inc(x_loaded[b], 16)
            sp.dma_start(wt[:, :, :], qkv_wT.rearrange("(g p) o -> p g o", g=2)).then_inc(par_loaded, 16)
            with nc.allow_non_contiguous_dma(reason="per-channel vectors"):
                sp.dma_start(par[:, :, 0], gamma.rearrange("(g p) -> p g", g=2)).then_inc(par_loaded, 16)
                sp.dma_start(par[:, :, 1], beta.rearrange("(g p) -> p g", g=2)).then_inc(par_loaded, 16)
                sp.dma_start(qb[:, :], qkv_b.rearrange("(m p) -> p m", p=G)).then_inc(par_loaded, 16)
            sp.wait_ge(zero_set, 1)
            for t in range(3):
                for r in (0, PW - 3):
                    dst = qkvp[t].rearrange("(n p) h w -> p n (h w)", p=G)[:, :, r * PW:(r + 3) * PW]
                    sp.dma_start(dst, zero[:, :, :]).then_inc(border_stored, 16)
            with sp.Fori(0, B) as b:
                for c in range(NCH):
                    o = c % 2
                    sp.wait_ge(evacuated_even, 3 * NCH * b + 3 * (c + 1))
                    sp.wait_ge(evacuated_odd, 3 * NCH * b + 3 * (c + 1))
                    for t in range(3):
                        sp.dma_start(qv[t, b, :, :, (3 + 8 * c) * PW:(11 + 8 * c) * PW],
                                     out[o][:, 2 * t:2 * t + 2, :, :].rearrange("p g h w -> p g (h w)")
                                     ).then_inc(stored[o], 16)
            sp.wait_ge(stored[0], 16 * 3 * 4 * B)
            sp.wait_ge(stored[1], 16 * 3 * 3 * B)
            sp.wait_ge(border_stored, 16 * 6)

        @block.gpsimd
        def _(pool):
            pool.memset(zero[:, :, :], 0.0).then_inc(zero_set, 1)
            pool.memset(out[0][:, :, :, :], 0.0).then_inc(zero_set, 1)
            pool.memset(out[1][:, :, :, :], 0.0).then_inc(zero_set, 1)

        @block.vector
        def _(v):
            for b in range(B):
                v.wait_ge(x_loaded[b], 16)
                for g in range(2):
                    for c in range(NCH):
                        last = v.bn_stats(stats[:, g, b * NCH + c, :], xs[:, g, b, c * CH:(c + 1) * CH])
            last.then_inc(stats_done, 1)
            v.wait_ge(stats_done, 1)
            for g in range(2):
                v.bn_aggr(mv[:, g, :], stats[:, g, :, :]).then_inc(norm_step, 1)
            v.wait_ge(par_loaded, 64)
            v.wait_ge(std_done, 1)
            v.reciprocal(sc[:, :], std[:, :]).then_inc(norm_step, 1)
            v.wait_ge(norm_step, 3)
            v.tensor_tensor(sc[:, :], sc[:, :], par[:, :, 0], ALU.mult).then_inc(norm_step, 1)
            v.wait_ge(norm_step, 4)
            v.tensor_tensor(sh[:, :], mv[:, :, 0], sc[:, :], ALU.mult).then_inc(norm_step, 1)
            v.wait_ge(norm_step, 5)
            v.tensor_tensor(sh[:, :], par[:, :, 1], sh[:, :], ALU.subtract).then_inc(norm_step, 1)
            for g in range(2):
                v.tensor_scalar(wf[:, g, 0:C], wt[:, g, 0:C], sc[:, g:g + 1], HD ** -0.5, ALU.mult, ALU.mult)
                v.tensor_scalar(wf[:, g, C:], wt[:, g, C:], sc[:, g:g + 1], None, ALU.mult).then_inc(folded, 1)
            v.wait_ge(bias_summed, 1)
            v.tensor_tensor(bias[:, :], psb[:, 0:6], qb[:, :], ALU.add).then_inc(norm_step, 1)
            v.wait_ge(norm_step, 7)
            v.tensor_scalar(bias[:, 0:2], bias[:, 0:2], HD ** -0.5, None, ALU.mult).then_inc(folded, 1)
            v.wait_ge(folded, 3)
            v.wait_ge(zero_set, 3)
            with v.Fori(0, B) as b:
                for c in range(NCH):
                    o = c % 2
                    v.wait_ge(stored[o], 16 * 3 * ((3 if o else 4) * b + c // 2))
                    for m in (1, 3, 5):
                        v.wait_ge(product, 6 * NCH * b + 6 * c + m + 1)
                        v.tensor_scalar(out[o][:, m, :, 3:3 + W],
                                        ps[(6 * c + m) % 4][:, 0:CH].rearrange("p (h w) -> p h w", w=W),
                                        bias[:, m:m + 1], None, ALU.add).then_inc(evacuated_odd, 1)

        @block.scalar
        def _(a):
            a.wait_ge(norm_step, 2)
            a.activation(std[:, :], mv[:, :, 1], ACT.Sqrt, bias=EPS).then_inc(std_done, 1)
            a.wait_ge(folded, 3)
            a.wait_ge(zero_set, 3)
            with a.Fori(0, B) as b:
                for c in range(NCH):
                    o = c % 2
                    a.wait_ge(stored[o], 16 * 3 * ((3 if o else 4) * b + c // 2))
                    for m in (0, 2, 4):
                        a.wait_ge(product, 6 * NCH * b + 6 * c + m + 1)
                        a.activation(out[o][:, m, :, 3:3 + W],
                                     ps[(6 * c + m) % 4][:, 0:CH].rearrange("p (h w) -> p h w", w=W),
                                     ACT.Identity, bias=bias[:, m:m + 1]).then_inc(evacuated_even, 1)

        @block.tensor
        def _(pe):
            pe.wait_ge(norm_step, 6)
            for m in range(6):
                for g in range(2):
                    last = pe.matmul(psb[:, m:m + 1], wt[:, g, m * G:(m + 1) * G], sh[:, g:g + 1],
                                     start=(g == 0), stop=(g == 1))
            last.then_inc(bias_summed, 1)
            pe.wait_ge(folded, 2)
            with pe.Fori(0, B) as b:
                for c in range(NCH):
                    for m in range(6):
                        n = 6 * c + m
                        k = 3 * NCH * b + (n - 4) // 2 + 1
                        if n >= 4:
                            pe.wait_ge(evacuated_odd if m % 2 else evacuated_even, k)
                        else:
                            pe.wait_ge(evacuated_odd if m % 2 else evacuated_even, 3 * NCH * b)
                        for g in range(2):
                            last = pe.matmul(ps[n % 4][:, 0:CH], wf[:, g, m * G:(m + 1) * G],
                                             xs[:, g, b, c * CH:(c + 1) * CH], start=(g == 0), stop=(g == 1))
                        last.then_inc(product, 1)


def window_attention(nc, qkvp, dm_wT, dm_b, rel_bias, sel, ident, att):
    with ExitStack() as ctx:
        sb = lambda name, shape, dt=F32: ctx.enter_context(nc.sbuf_tensor(name, shape, dt))
        pt = lambda name, dt=F32, n=512: ctx.enter_context(nc.psum_tensor(name, [128, n], dt))
        sem = ctx.enter_context(stage_semaphores(nc))
        wdm = sb("b_wdm", [128, 4, 7, 128])
        rel = sb("b_rel", [128, 6])
        dmb = sb("b_dmb", [128, 1])
        mapb = sb("b_mapb", [128, 4, 6])
        curb = sb("b_curb", [128, 4])
        selt = sb("b_sel", [120, K1, 128], BF16)
        idf = sb("b_idf", [128, 128])
        idb = sb("b_idb", [128, 128], BF16)
        qk = [sb(f"b_qk{i}", [128, 61, PW]) for i in range(2)]
        vv = sb("b_v", [128, PW, PW])
        lg = [sb(f"b_lg{i}", [128, 28, W]) for i in range(2)]
        mx = sb("b_mx", [112, 28])
        rs = sb("b_rs", [112, 28])
        rr = sb("b_rr", [112, 28])
        pr = sb("b_pr", [112, 28, TAPS])
        res = sb("b_res", [112, 28, TAPS])
        px = sb("b_px", [112, 28, NS, 4, 3, K1], BF16)
        at = sb("b_at", [120, NS, N], BF16)
        prodg = sb("b_prodg", [128, GR, CH])
        prodd = sb("b_prodd", [128, DR, CH])
        accg = sb("b_accg", [128, N])
        accd = sb("b_accd", [128, N])
        pc = [pt(f"b_pc{i}") for i in range(2)]
        pbc = [pt(f"b_pbc{i}") for i in range(2)]
        ptr = [pt(f"b_ptr{i}") for i in range(2)]
        pbt = [pt(f"b_pbt{i}", BF16, 1024) for i in range(2)]
        const_loaded = sem("b_const_loaded")
        cleared = sem("b_cleared")
        bias_ready = sem("b_bias_ready")
        bias_set = sem("b_bias_set")
        idb_ready = sem("b_idb_ready")
        qk_loaded = [sem(f"b_qk_loaded{i}") for i in range(2)]
        v_loaded = sem("b_v_loaded")
        conv_done = sem("b_conv_done")
        conv_evac = sem("b_conv_evac")
        turned = sem("b_turned")
        max_found = sem("b_max_found")
        centred = sem("b_centred")
        exp_done = sem("b_exp_done")
        sum_step = sem("b_sum_step")
        prob_ready = sem("b_prob_ready")
        hi_ready = sem("b_hi_ready")
        rest_ready = sem("b_rest_ready")
        mid_ready = sem("b_mid_ready")
        lo_ready = sem("b_lo_ready")
        back_turned = sem("b_back_turned")
        back_evac = sem("b_back_evac")
        spread = sem("b_spread")
        weighted = sem("b_weighted")
        dadded = sem("b_dadded")
        gadded = sem("b_gadded")
        combined = sem("b_combined")
        stored = sem("b_stored")
        block = ctx.enter_context(nc.Block())
        qv = qkvp.rearrange("t (n r) h w -> t n r (h w)", r=HD)
        vvd = qkvp[2].rearrange("(u r) h w -> u r (h w)", r=128)
        av = att.rearrange("(u r) n -> u r n", r=128)

        def run(eng, part):
            part(None, 0)
            with eng.Fori(0, NU - 1) as u:
                part(u, u + 1)
            part(NU - 1, None)

        @block.sync
        def _(sp):
            sp.wait_ge(cleared, 2)
            with nc.allow_non_contiguous_dma(reason="weights, once"):
                for s, r, p0, d0, n in ((0, 0, 0, 0, 4), (1, 1, 0, 0, 4), (1, 0, 0, 1, 3), (0, 1, 1, 1, 3)):
                    for i in range(n):
                        sp.dma_start(wdm[64 * s:64 * s + 64, p0 + i, :, 64 * r:64 * r + TAPS],
                                     dm_wT[:, d0 + 2 * i, :, :]).then_inc(const_loaded, 16)
                for r in range(2):
                    sp.dma_start(rel[64 * r:64 * r + TAPS, :], rel_bias).then_inc(const_loaded, 16)
                    sp.dma_start(dmb[64 * r:64 * r + TAPS, :], dm_b.rearrange("(k o) -> k o", o=1)).then_inc(const_loaded, 16)
            sp.dma_start(selt[:, :, :], sel).then_inc(const_loaded, 16)
            sp.dma_start(idf[:, :], ident).then_inc(const_loaded, 16)

            def part(ua, uc):
                if ua is not None:
                    sp.wait_ge(weighted, NSTEP * ua)
                    sp.dma_start(vv[:, :, :].rearrange("p h w -> p (h w)"), vvd[ua]).then_inc(v_loaded, 16)
                for j in range(4):
                    if uc is not None:
                        o = j % 2
                        hidx = 4 * uc + j
                        if ua is not None or j >= 2:
                            sp.wait_ge(conv_done, 16 * uc + 4 * (j - 1))
                        for t in range(2):
                            for s in range(2):
                                sp.dma_start(qk[o][64 * s + 32 * t:64 * s + 32 * t + 32, :, :].rearrange("p h w -> p (h w)"),
                                             qv[t, hidx, :, s * PW:(s + 61) * PW]).then_inc(qk_loaded[o], 16)
                    if ua is not None:
                        for c in ((), (0,), (1, 2), (3, 4, 5, 6))[j]:
                            sp.wait_ge(combined, NCH * ua + c + 1)
                            sp.dma_start(av[ua, :, c * CH:(c + 1) * CH], accg[:, c * CH:(c + 1) * CH]).then_inc(stored, 16)
            run(sp, part)
            sp.wait_ge(stored, 16 * NCH * NU)

        @block.tensor
        def _(pe):
            pe.wait_ge(const_loaded, 16 * 20)
            pe.wait_ge(idb_ready, 1)

            def part(ua, uc):
                step = 0
                for slot in range(SLOTS):
                    n, m = divmod(slot, MB)
                    if uc is not None and n < 16:
                        j, cc = divmod(n, 4)
                        if m == 0:
                            if cc == 0:
                                pe.wait_ge(qk_loaded[j % 2], 64 * (2 * uc + j // 2 + 1))
                            if ua is not None or n >= 2:
                                pe.wait_ge(conv_evac, 16 * uc + n - 1)
                        p, dx = divmod(m, 7)
                        y0 = 14 * cc + 2 * p
                        mm = pe.matmul(pc[n % 2][0:113, 0:392], wdm[:, p, dx, 0:113],
                                       qk[j % 2][:, y0:y0 + 13:2, dx:dx + W], start=(m == 0), stop=(m == MB - 1))
                        if m == MB - 1:
                            mm.then_inc(conv_done, 1)
                    if uc is not None and n >= 4 and n % 4 == 0 and m in (8, 10, 16, 22):
                        j = n // 4 - 1
                        tg = (8, 10, 16, 22).index(m)
                        if tg == 0:
                            pe.wait_ge(conv_evac, 16 * uc + 4 * (j + 1))
                        if ua is not None or 4 * j + tg >= 2:
                            pe.wait_ge(centred, 16 * uc + 4 * j + tg - 1)
                        for t in range(4 * tg, min(4 * tg + 4, NT)):
                            o = (t - 4 * tg) * 128
                            mm = pe.transpose(ptr[tg % 2][0:112, o:o + 113],
                                              lg[j % 2][0:113, 2 * t:2 * t + 2, :].rearrange("p a b -> p (a b)"), idf[0:113, 0:113])
                        mm.then_inc(turned, 1)
                    if ua is not None and n < 4 and m in (1, 5, 9, 13, 17, 21):
                        c, gg = divmod(6 * n + (m - 1) // 4, 3)
                        if c < NCH:
                            q = 3 * c + gg
                            if q == 0:
                                pe.wait_ge(lo_ready, 4 * ua + 4)
                                pe.wait_ge(mid_ready, 4 * ua + 4)
                            pe.wait_ge(back_evac, 21 * ua + (q - 1 if q >= 2 else 0))
                            for s in range(2 * gg, min(2 * gg + 2, NS)):
                                for t2 in range(2):
                                    for r in range(2):
                                        o = (s - 2 * gg) * CH + (4 * t2 + r) * W
                                        mm = pe.transpose(
                                            pbt[q % 2][0:120, o:o + 3 * W].rearrange("p (a b) -> p a b", b=W)[:, 0:3:2, :],
                                            px[:, 2 * (2 * c + t2) + r, s, :, :, :].rearrange("p a b c -> p (a b c)"),
                                            idb[0:112, 0:112])
                            mm.then_inc(back_turned, 1)
                    while ua is not None and step < NSTEP and AGG_SLOT[step] == slot:
                        c, k = divmod(step, TAPS)
                        if k == 0:
                            pe.wait_ge(back_evac, 21 * ua + 3 * c + 3)
                        pe.wait_ge(weighted, NSTEP * ua + (step - 1 if step >= 2 else 0))
                        pe.matmul(pbc[step % 2][:, 0:CH], selt[:, k % K1, :], at[:, k // K1, c * CH:(c + 1) * CH],
                                  start=True, stop=True).then_inc(spread, 1)
                        step += 1
            run(pe, part)

        @block.scalar
        def _(a):
            a.wait_ge(bias_ready, 1)

            def part(ua, uc):
                if uc is not None:
                    a.activation(curb[:, :], mapb[:, :, :].rearrange("p a b -> p (a b)")[:, bass.ds(4 * uc, 4)],
                                 ACT.Copy).then_inc(bias_set, 1)
                    a.wait_ge(bias_set, uc + 1)
                for slot in range(SLOTS):
                    n, m = divmod(slot, MB)
                    if ua is not None and n < 4 and m in (3, 7, 11, 15, 19, 23):
                        c, gg = divmod(6 * n + (m - 3) // 4, 3)
                        if c < NCH:
                            q = 3 * c + gg
                            ns = min(2, NS - 2 * gg)
                            if q == 0:
                                a.wait_ge(spread, NSTEP * ua)
                            a.wait_ge(back_turned, 21 * ua + q + 1)
                            a.activation(at[:, 2 * gg:2 * gg + ns, c * CH:(c + 1) * CH],
                                         pbt[q % 2][0:120, 0:ns * CH].rearrange("p (s n) -> p s n", s=ns),
                                         ACT.Copy).then_inc(back_evac, 1)
                    if uc is not None and n < 16 and m == MB - 1:
                        j, cc = divmod(n, 4)
                        a.wait_ge(conv_done, 16 * uc + n + 1)
                        if cc == 0 and (ua is not None or j >= 2):
                            a.wait_ge(turned, 16 * uc + 4 * (j - 1))
                        a.activation(lg[j % 2][0:113, 7 * cc:7 * cc + 7, :],
                                     pc[n % 2][0:113, 0:392].rearrange("p (a b) -> p a b", b=W), ACT.Identity,
                                     bias=curb[0:113, j:j + 1]).then_inc(conv_evac, 1)
                    if uc is not None and n >= 4:
                        j = n // 4 - 1
                        hidx = 4 * uc + j
                        stage = {(0, 27): "exp", (1, 6): "hi", (1, 14): "mid"}.get((n % 4, m)) if n < 16 else \
                            {24: "exp", 26: "hi", 27: "mid"}.get(m)
                        if stage == "exp":
                            a.wait_ge(centred, 4 * hidx + 4)
                            a.activation(pr[:, :, :], pr[:, :, :], ACT.Exp).then_inc(exp_done, 1)
                        if stage in ("hi", "mid"):
                            part_i = 0 if stage == "hi" else 1
                            src = pr if stage == "hi" else res
                            a.wait_ge(prob_ready if stage == "hi" else rest_ready, hidx + 1)
                            if stage == "hi" and ua is not None:
                                a.wait_ge(back_turned, 21 * uc)
                            a.activation(px[:, :, 0:4, j, part_i, :], src[:, :, 0:40].rearrange("p r (s k) -> p r s k", s=4), ACT.Copy)
                            a.activation(px[:, :, 4, j, part_i, 0:9], src[:, :, 40:49], ACT.Copy)\
                                .then_inc(hi_ready if stage == "hi" else mid_ready, 1)
            run(a, part)

        @block.vector
        def _(v):
            v.memset(wdm[:, :, :, :], 0.0).then_inc(cleared, 1)
            v.memset(rel[:, :], 0.0)
            v.memset(dmb[:, :], 0.0).then_inc(cleared, 1)
            v.memset(px[:, :, :, :, :, :], 0.0).then_inc(cleared, 1)
            v.wait_ge(const_loaded, 16 * 20)
            v.wait_ge(cleared, 3)
            for i in range(4):
                last = v.tensor_scalar(mapb[:, i, :], rel[:, :], dmb[:, 0:1], None, ALU.add)
            last.then_inc(bias_ready, 1)
            v.tensor_copy(idb[:, :], idf[:, :]).then_inc(idb_ready, 1)

            def part(ua, uc):
                step = 0
                pend = None

                def flush():
                    nonlocal pend
                    if pend is not None:
                        stp, i, c = pend
                        v.wait_ge(weighted, NSTEP * ua + stp + 1)
                        v.wait_ge(dadded, NDA * ua + c * (len(D_TAPS) - 1) + i - 1)
                        sl = accd[:, c * CH:(c + 1) * CH]
                        v.tensor_tensor(sl, sl, prodd[:, i % DR, :], ALU.add).then_inc(dadded, 1)
                        pend = None
                for slot in range(SLOTS):
                    n, m = divmod(slot, MB)
                    while ua is not None and step < NSTEP and AGG_SLOT[step] == slot:
                        c, k = divmod(step, TAPS)
                        if step == 0:
                            v.wait_ge(v_loaded, 16 * (ua + 1))
                        v.wait_ge(spread, NSTEP * ua + step + 1)
                        if k in G_TAPS:
                            i = G_TAPS.index(k)
                            if i == 0:
                                out = accg[:, c * CH:(c + 1) * CH]
                                if c == 0:
                                    v.wait_ge(stored, 16 * NCH * ua)
                            else:
                                out = prodg[:, (c * 28 + i - 1) % GR, :]
                                e = c * 28 + i - 1 - GR
                                v.wait_ge(gadded, NGA * ua + (e + 1 if e >= 0 else 0))
                        else:
                            i = D_TAPS.index(k)
                            if i == 0 and c == 0:
                                v.wait_ge(combined, NCH * ua)
                            out = accd[:, c * CH:(c + 1) * CH] if i == 0 else prodd[:, i % DR, :]
                        dy, dx = divmod(k, 7)
                        v.tensor_tensor(out.rearrange("p (h w) -> p h w", w=W),
                                        pbc[step % 2][:, 0:CH].rearrange("p (h w) -> p h w", w=W),
                                        vv[:, 8 * c + dy:8 * c + dy + 8, dx:dx + W], ALU.mult).then_inc(weighted, 1)
                        flush()
                        if k in D_TAPS and D_TAPS.index(k):
                            pend = (step, D_TAPS.index(k), c)
                        if k == TAPS - 1:
                            flush()
                        step += 1
                    if uc is not None and n >= 4:
                        j = n // 4 - 1
                        hidx = 4 * uc + j
                        if n % 4 == 0 and m in (14, 16, 20, 24 if n < 16 else 23):
                            tg = {14: 0, 16: 1, 20: 2}.get(m, 3)
                            nt = min(4, NT - 4 * tg)
                            v.wait_ge(turned, 4 * hidx + tg + 1)
                            src = ptr[tg % 2][0:112, :].rearrange("p (t r k) -> p t r k", t=4, r=2)[:, 0:nt, :, 0:TAPS]
                            mt = mx[:, 8 * tg:8 * tg + 2 * nt]
                            v.tensor_reduce(mt.rearrange("p (t r) -> p t r", r=2), src, AX.X, ALU.max).then_inc(max_found, 1)
                            v.wait_ge(max_found, 4 * hidx + tg + 1)
                            if tg == 0 and (ua is not None or j):
                                v.wait_ge(hi_ready, hidx)
                            v.tensor_tensor(pr[:, 8 * tg:8 * tg + 2 * nt, :].rearrange("p (t r) k -> p t r k", r=2), src,
                                            mt.rearrange("p (t r o) -> p t r o", r=2, o=1).broadcast_to([112, nt, 2, TAPS]),
                                            ALU.subtract).then_inc(centred, 1)
                        stage = {(1, 2): "norm", (1, 10): "rest", (1, 18): "lo"}.get((n % 4, m)) if n < 16 else \
                            {25: "norm", 26: "rest", 27: "lo"}.get(m)
                        if stage == "norm":
                            v.wait_ge(exp_done, hidx + 1)
                            v.tensor_reduce(rs[:, :], pr[:, :, :], AX.X, ALU.add).then_inc(sum_step, 1)
                            v.wait_ge(sum_step, 2 * hidx + 1)
                            v.reciprocal(rr[:, :], rs[:, :]).then_inc(sum_step, 1)
                            v.wait_ge(sum_step, 2 * hidx + 2)
                            v.tensor_tensor(pr[:, :, :], pr[:, :, :], rr[:, :].rearrange("p (r o) -> p r o", o=1).broadcast_to([112, 28, TAPS]),
                                            ALU.mult).then_inc(prob_ready, 1)
                        if stage == "rest":
                            v.wait_ge(hi_ready, hidx + 1)
                            v.tensor_tensor(res[:, :, 0:40].rearrange("p r (s k) -> p r s k", s=4),
                                            pr[:, :, 0:40].rearrange("p r (s k) -> p r s k", s=4), px[:, :, 0:4, j, 0, :], ALU.subtract)
                            v.tensor_tensor(res[:, :, 40:49], pr[:, :, 40:49], px[:, :, 4, j, 0, 0:9], ALU.subtract).then_inc(rest_ready, 1)
                        if stage == "lo":
                            v.wait_ge(mid_ready, hidx + 1)
                            v.wait_ge(rest_ready, hidx + 1)
                            v.tensor_tensor(px[:, :, 0:4, j, 2, :], res[:, :, 0:40].rearrange("p r (s k) -> p r s k", s=4),
                                            px[:, :, 0:4, j, 1, :], ALU.subtract)
                            v.tensor_tensor(px[:, :, 4, j, 2, 0:9], res[:, :, 40:49], px[:, :, 4, j, 1, 0:9], ALU.subtract).then_inc(lo_ready, 1)
            run(v, part)

        @block.gpsimd
        def _(p):
            def part(ua, uc):
                if ua is None:
                    return
                for c in range(NCH):
                    sl = accg[:, c * CH:(c + 1) * CH]
                    for i in range(1, len(G_TAPS)):
                        k = G_TAPS[i]
                        e = c * 28 + i - 1
                        p.wait_ge(weighted, NSTEP * ua + c * TAPS + k + 1)
                        p.wait_ge(gadded, NGA * ua + e)
                        p.tensor_tensor(sl, sl, prodg[:, e % GR, :], ALU.add).then_inc(gadded, 1)
                    p.wait_ge(gadded, NGA * ua + (c + 1) * (len(G_TAPS) - 1))
                    p.wait_ge(dadded, NDA * ua + (c + 1) * (len(D_TAPS) - 1))
                    p.tensor_tensor(sl, sl, accd[:, c * CH:(c + 1) * CH], ALU.add).then_inc(combined, 1)
            run(p, part)


def selector():
    import numpy as np
    s = np.zeros((4, 3, K1, K1, 4, HD), mybir.dt.np(BF16))
    for j in range(4):
        for k in range(K1):
            s[j, :, k, k, j, :] = 1
    return s.reshape(120, K1, 128)


def mixer(nc, x, att, proj_wT, proj_b, c1_wT, c1_b, c2_wT, c2_b, x1p, xp):
    with ExitStack() as ctx:
        sb = lambda name, shape, dt=F32: ctx.enter_context(nc.sbuf_tensor(name, shape, dt))
        pt = lambda name: ctx.enter_context(nc.psum_tensor(name, [G, 512], F32))
        sem = ctx.enter_context(stage_semaphores(nc))
        wp = sb("c_wp", [G, 2, C])
        w1 = sb("c_w1", [G, 2, F])
        w2 = sb("c_w2", [G, 8, C])
        bp = sb("c_bp", [G, 2])
        b1 = sb("c_b1", [G, 8])
        b2 = sb("c_b2", [G, 2])
        xin = [sb(f"c_xin{i}", [G, 2, CH]) for i in range(2)]
        ain = [sb(f"c_ain{i}", [G, 2, CH]) for i in range(2)]
        xa = [sb(f"c_xa{i}", [G, 2, CH]) for i in range(2)]
        hid = [sb(f"c_hid{i}", [G, 8, CH]) for i in range(2)]
        out = [sb(f"c_out{i}", [G, 2, 8, PW]) for i in range(2)]
        pool_sum = sb("c_pool", [G, 2, 7, 7])
        zero = sb("c_zero", [G, 8, 3 * PW])
        pp = [pt(f"c_pp{i}") for i in range(2)]
        p1 = [pt(f"c_p1{i}") for i in range(3)]
        p2 = [pt(f"c_p2{i}") for i in range(2)]
        par_loaded = sem("c_par_loaded")
        in_loaded = [sem(f"c_in_loaded{i}") for i in range(2)]
        cleared = sem("c_cleared")
        border_stored = sem("c_border_stored")
        projected = sem("c_projected")
        added = sem("c_added")
        hidden = sem("c_hidden")
        gelu_done = sem("c_gelu_done")
        mixed = sem("c_mixed")
        finished = sem("c_finished")
        pooled = sem("c_pooled")
        stored = [sem(f"c_stored{i}") for i in range(2)]
        pool_stored = sem("c_pool_stored")
        block = ctx.enter_context(nc.Block())
        xv = x.rearrange("b (g p) h w -> b p g (h w)", g=2)
        av = att.rearrange("(b g p) n -> b p g n", b=B, g=2)
        ov = x1p.rearrange("(b g p) h w -> b p g (h w)", b=B, g=2)

        @block.sync
        def _(sp):
            sp.dma_start(wp[:, :, :], proj_wT.rearrange("(g p) o -> p g o", p=G)).then_inc(par_loaded, 16)
            sp.dma_start(w1[:, :, :], c1_wT.rearrange("(g p) o -> p g o", p=G)).then_inc(par_loaded, 16)
            sp.dma_start(w2[:, :, :], c2_wT.rearrange("(g p) o -> p g o", p=G)).then_inc(par_loaded, 16)
            with nc.allow_non_contiguous_dma(reason="per-channel vectors"):
                sp.dma_start(bp[:, :], proj_b.rearrange("(g p) -> p g", p=G)).then_inc(par_loaded, 16)
                sp.dma_start(b1[:, :], c1_b.rearrange("(g p) -> p g", p=G)).then_inc(par_loaded, 16)
                sp.dma_start(b2[:, :], c2_b.rearrange("(g p) -> p g", p=G)).then_inc(par_loaded, 16)
            with sp.Fori(0, B) as b:
                for c in range(NCH):
                    o = c % 2
                    sp.wait_ge(added, 2 * NCH * b + 2 * max(c - 1, 0))
                    sl = slice(c * CH, (c + 1) * CH)
                    sp.dma_start(ain[o][:, :, :], av[b, :, :, sl]).then_inc(in_loaded[o], 16)
                    sp.dma_start(xin[o][:, :, :], xv[b, :, :, sl]).then_inc(in_loaded[o], 16)

        @block.gpsimd
        def _(p):
            p.memset(zero[:, :, :], 0.0).then_inc(cleared, 1)
            p.memset(out[0][:, :, :, :], 0.0).then_inc(cleared, 1)
            p.memset(out[1][:, :, :, :], 0.0).then_inc(cleared, 1)
            p.wait_ge(cleared, 1)
            for r in (0, PW - 3):
                dst = x1p.rearrange("(n p) h w -> p n (h w)", p=G)[:, :, r * PW:(r + 3) * PW]
                p.dma_start(dst, zero[:, :, :]).then_inc(border_stored, 16)
            with p.Fori(0, B) as b:
                for c in range(NCH):
                    o = c % 2
                    p.wait_ge(finished, 2 * NCH * b + 2 * c + 2)
                    p.dma_start(ov[b, :, :, (3 + 8 * c) * PW:(11 + 8 * c) * PW],
                                out[o][:, :, :, :].rearrange("p g h w -> p g (h w)")).then_inc(stored[o], 16)
                p.wait_ge(pooled, 2 * NCH * (b + 1))
                p.dma_start(xp.rearrange("(b g p) k -> b p g k", b=B, g=2)[b],
                            pool_sum[:, :, :, :].rearrange("p g a b -> p g (a b)")).then_inc(pool_stored, 16)
            p.wait_ge(border_stored, 32)
            p.wait_ge(stored[0], 16 * 4 * B)
            p.wait_ge(stored[1], 16 * 3 * B)
            p.wait_ge(pool_stored, 16 * B)

        @block.tensor
        def _(pe):
            pe.wait_ge(par_loaded, 96)
            with pe.Fori(0, B) as b:
                def project(c):
                    o = c % 2
                    pe.wait_ge(in_loaded[o], 32 * ((3 if o else 4) * b + c // 2 + 1))
                    for m in range(2):
                        pe.wait_ge(added, 2 * NCH * b + max(2 * (c - 1) + m + 1, 0))
                        for g in range(2):
                            mm = pe.matmul(pp[m][:, 0:CH], wp[:, g, m * G:(m + 1) * G], ain[o][:, g, :],
                                           start=(g == 0), stop=(g == 1))
                        mm.then_inc(projected, 1)
                project(0)
                for c in range(NCH):
                    o = c % 2
                    pe.wait_ge(added, 2 * NCH * b + 2 * c + 2)
                    for m in range(8):
                        pe.wait_ge(gelu_done, 8 * NCH * b + max(8 * c + m - 2, 0))
                        for g in range(2):
                            mm = pe.matmul(p1[(8 * c + m) % 3][:, 0:CH], w1[:, g, m * G:(m + 1) * G], xa[o][:, g, :],
                                           start=(g == 0), stop=(g == 1))
                        mm.then_inc(hidden, 1)
                    if c + 1 < NCH:
                        project(c + 1)
                    for m in range(2):
                        pe.wait_ge(finished, 2 * NCH * b + max(2 * (c - 1) + m + 1, 0))
                        for k in range(8):
                            if m == 0:
                                pe.wait_ge(gelu_done, 8 * NCH * b + 8 * c + k + 1)
                            mm = pe.matmul(p2[m][:, 0:CH], w2[:, k, m * G:(m + 1) * G], hid[o][:, k, :],
                                           start=(k == 0), stop=(k == 7))
                        mm.then_inc(mixed, 1)

        @block.scalar
        def _(a):
            with a.Fori(0, B) as b:
                for c in range(NCH):
                    o = c % 2
                    a.wait_ge(mixed, 2 * NCH * b + 2 * max(c - 1, 0))
                    for m in range(8):
                        a.wait_ge(hidden, 8 * NCH * b + 8 * c + m + 1)
                        a.activation(hid[o][:, m, :], p1[(8 * c + m) % 3][:, 0:CH], ACT.Gelu,
                                     bias=b1[:, m:m + 1]).then_inc(gelu_done, 1)

        @block.vector
        def _(v):
            v.wait_ge(par_loaded, 96)
            v.wait_ge(cleared, 3)
            with v.Fori(0, B) as b:
                def add(c):
                    o = c % 2
                    v.wait_ge(hidden, 8 * NCH * b + 8 * max(c - 1, 0))
                    for m in range(2):
                        v.wait_ge(projected, 2 * NCH * b + 2 * c + m + 1)
                        v.scalar_tensor_tensor(xa[o][:, m, :], pp[m][:, 0:CH], bp[:, m:m + 1], xin[o][:, m, :],
                                               ALU.add, ALU.add).then_inc(added, 1)
                add(0)
                for c in range(NCH):
                    o = c % 2
                    if c + 1 < NCH:
                        add(c + 1)
                    v.wait_ge(stored[o], 16 * ((3 if o else 4) * b + c // 2))
                    if c == 0:
                        v.wait_ge(pool_stored, 16 * b)
                    for m in range(2):
                        v.wait_ge(mixed, 2 * NCH * b + 2 * c + m + 1)
                        v.scalar_tensor_tensor(out[o][:, m, :, 3:3 + W], p2[m][:, 0:CH].rearrange("p (h w) -> p h w", w=W),
                                               b2[:, m:m + 1], xa[o][:, m, :].rearrange("p (h w) -> p h w", w=W),
                                               ALU.add, ALU.add).then_inc(finished, 1)
                    for m in range(2):
                        v.wait_ge(finished, 2 * NCH * b + 2 * c + m + 1)
                        v.tensor_reduce(pool_sum[:, m, c, :],
                                        out[o][:, m, :, 3:3 + W].rearrange("p h (a w) -> p a h w", w=8),
                                        AX.XY, ALU.add).then_inc(pooled, 1)


def channel_gate(nc, x1p, xp, wg1T, bn2, wg2T, bg2, beta, w1T, bn1, basis, chan, ident, gate):
    with ExitStack() as ctx:
        sb = lambda name, shape, dt=F32: ctx.enter_context(nc.sbuf_tensor(name, shape, dt))
        pt = lambda name: ctx.enter_context(nc.psum_tensor(name, [128, 512], F32))
        sem = ctx.enter_context(stage_semaphores(nc))
        xin = sb("g_xin", [G, 2, 56, PW])
        w1 = sb("g_w1", [G, 2, NF])
        w2 = sb("g_w2", [NF, NF])
        wo = sb("g_wo", [G, 2, C])
        p2 = sb("g_p2", [NF, 4])
        vb = sb("g_vb", [NF, 2])
        p1 = sb("g_p1", [G, 2, 5])
        bas = sb("g_bas", [NF, 49])
        ch = sb("g_ch", [G, 2])
        idf = sb("g_idf", [128, 128])
        xps = sb("g_xps", [G, B, 2, 49])
        s2 = sb("g_s2", [NF, 2])
        s1 = sb("g_s1", [G, 2, 2])
        act = [sb(f"g_act{i}", [NF, 8, PW]) for i in range(2)]
        gs = sb("g_gs", [NF, 7])
        gm = sb("g_gm", [NF, 4])
        diag = sb("g_diag", [NF, NF])
        ones = sb("g_ones", [NF, G])
        row = sb("g_row", [G, NF])
        tot = sb("g_tot", [G, 2])
        prm = sb("g_prm", [G, NF + 1])
        ge = sb("g_ge", [G, 2, NF + 1])
        lt = sb("g_lt", [G, 2, NF + 1])
        msk = sb("g_msk", [G, 2, NF])
        zer = sb("g_zer", [G, NF])
        suf = sb("g_suf", [G, 2, NF + 1])
        pick = sb("g_pick", [G, 2, NF])
        pickT = sb("g_pickT", [NF, 2, G])
        prod = sb("g_prod", [G, 2, B, 49])
        y0 = sb("g_y0", [G, 2, B])
        yo = sb("g_yo", [G, 2, B])
        pg = [pt(f"g_pg{i}") for i in range(2)]
        ps = pt("g_ps")
        pf = [pt(f"g_pf{i}") for i in range(2)]
        loaded = sem("g_loaded")
        x_loaded = sem("g_x_loaded")
        gate_step = sem("g_gate_step")
        norm_ready = sem("g_norm_ready")
        var_ready = sem("g_var_ready")
        product = sem("g_product")
        activated = sem("g_activated")
        mean_ready = sem("g_mean_ready")
        linear = sem("g_linear")
        mean_step = sem("g_mean_step")
        tanh_done = sem("g_tanh_done")
        diag_ready = sem("g_diag_ready")
        pick_ready = sem("g_pick_ready")
        pick_turned = sem("g_pick_turned")
        pick_copied = sem("g_pick_copied")
        filt_ready = sem("g_filt_ready")
        y0_ready = sem("g_y0_ready")
        y1_ready = sem("g_y1_ready")
        gate_ready = sem("g_gate_ready")
        stored = sem("g_stored")
        block = ctx.enter_context(nc.Block())

        @block.sync
        def _(sp):
            with nc.allow_non_contiguous_dma(reason="small vectors"):
                sp.dma_start(w1[:, :, :], wg1T.rearrange("(g p) o -> p g o", p=G)).then_inc(loaded, 16)
                sp.dma_start(w2[:, :], wg2T).then_inc(loaded, 16)
                sp.dma_start(wo[:, :, :], w1T.rearrange("(g p) o -> p g o", p=G)).then_inc(loaded, 16)
                for i in range(4):
                    sp.dma_start(p2[:, i:i + 1], bn2[i].rearrange("(k o) -> k o", o=1)).then_inc(loaded, 16)
                sp.dma_start(vb[:, 0:1], bg2.rearrange("(k o) -> k o", o=1)).then_inc(loaded, 16)
                sp.dma_start(vb[:, 1:2], beta.partition_broadcast(NF)).then_inc(loaded, 16)
                for i in range(5):
                    sp.dma_start(p1[:, :, i], bn1[i].rearrange("(g p) -> p g", p=G)).then_inc(loaded, 16)
                sp.dma_start(bas[:, :], basis).then_inc(loaded, 16)
                sp.dma_start(ch[:, :], chan).then_inc(loaded, 16)
                sp.dma_start(idf[:, :], ident).then_inc(loaded, 16)
                sp.dma_start(xps[:, :, :, :].rearrange("p b g k -> p (b g) k"), xp.rearrange("(n p) k -> p n k", p=G)).then_inc(loaded, 16)
            sp.dma_start(xin[:, :, :, :].rearrange("p g h w -> p g (h w)"),
                         x1p.rearrange("(b g p) h w -> b p g (h w)", b=B, g=2)[0, :, :, 3 * PW:59 * PW]).then_inc(x_loaded, 16)
            sp.wait_ge(gate_ready, 1)
            sp.dma_start(gate, yo[:, :, :].rearrange("p g b -> p (g b)")).then_inc(stored, 16)
            sp.wait_ge(stored, 16)

        @block.tensor
        def _(pe):
            pe.wait_ge(loaded, 16 * 18)
            pe.wait_ge(x_loaded, 16)
            for c in range(NCH):
                if c >= 2:
                    pe.wait_ge(activated, c - 1)
                for g in range(2):
                    mm = pe.matmul(pg[c % 2][0:NF, 0:8 * PW], w1[:, g, :],
                                   xin[:, g, 8 * c:8 * c + 8, :].rearrange("p h w -> p (h w)"), start=(g == 0), stop=(g == 1))
                mm.then_inc(product, 1)
            pe.wait_ge(mean_ready, 1)
            pe.matmul(ps[0:NF, 0:1], w2[:, :], gm[:, 0:1], start=True, stop=True).then_inc(linear, 1)
            pe.wait_ge(diag_ready, 1)
            pe.matmul(ps[0:G, 0:NF], ones[:, :], diag[:, :], start=True, stop=True).then_inc(linear, 1)
            pe.wait_ge(pick_ready, 1)
            for g in range(2):
                mm = pe.transpose(pg[g][0:NF, 0:G], pick[:, g, :], idf[0:G, 0:G])
            mm.then_inc(pick_turned, 1)
            pe.wait_ge(pick_copied, 1)
            for g in range(2):
                mm = pe.matmul(pf[g][0:G, 0:49], pickT[:, g, :], bas[:, :], start=True, stop=True)
            mm.then_inc(filt_ready, 1)
            pe.wait_ge(y0_ready, 1)
            for m in range(2):
                for g in range(2):
                    mm = pe.matmul(ps[0:G, B * m:B * m + B], wo[:, g, m * G:(m + 1) * G], y0[:, g, :],
                                   start=(g == 0), stop=(g == 1))
            mm.then_inc(y1_ready, 1)

        @block.scalar
        def _(a):
            a.wait_ge(loaded, 16 * 18)
            a.activation(s2[:, 0:1], p2[:, 3:4], ACT.Sqrt, bias=EPS)
            a.activation(s1[:, :, 0], p1[:, :, 3], ACT.Sqrt, bias=EPS).then_inc(var_ready, 1)
            a.wait_ge(norm_ready, 1)
            for c in range(NCH):
                a.wait_ge(product, c + 1)
                if c >= 2:
                    a.wait_ge(mean_step, c - 1)
                a.activation(act[c % 2][:, :, :], pg[c % 2][0:NF, 0:8 * PW].rearrange("p (h w) -> p h w", w=PW), ACT.Relu,
                             bias=s2[:, 1:2], scale=s2[:, 0:1]).then_inc(activated, 1)
            a.wait_ge(linear, 1)
            a.activation(gm[:, 1:2], ps[0:NF, 0:1], ACT.Tanh, bias=vb[:, 0:1]).then_inc(tanh_done, 1)

        @block.vector
        def _(v):
            count = 0

            def link(ins):
                nonlocal count
                count += 1
                ins.then_inc(gate_step, 1)
                v.wait_ge(gate_step, count)

            v.memset(ones[:, :], 1.0)
            v.memset(zer[:, :], 0.0)
            v.memset(prm[:, 0:1], 0.0)
            link(v.memset(suf[:, :, NF:], 1.0))
            v.wait_ge(var_ready, 1)
            link(v.reciprocal(s2[:, 0:1], s2[:, 0:1]))
            link(v.tensor_tensor(s2[:, 0:1], s2[:, 0:1], p2[:, 0:1], ALU.mult))
            link(v.tensor_tensor(s2[:, 1:2], s2[:, 0:1], p2[:, 2:3], ALU.mult))
            v.tensor_tensor(s2[:, 1:2], p2[:, 1:2], s2[:, 1:2], ALU.subtract).then_inc(norm_ready, 1)
            link(v.reciprocal(s1[:, :, 0], s1[:, :, 0]))
            link(v.tensor_tensor(s1[:, :, 0], s1[:, :, 0], p1[:, :, 0], ALU.mult))
            link(v.tensor_tensor(s1[:, :, 1], p1[:, :, 4], p1[:, :, 2], ALU.subtract))
            link(v.tensor_tensor(s1[:, :, 1], s1[:, :, 1], s1[:, :, 0], ALU.mult))
            link(v.tensor_tensor(s1[:, :, 1], s1[:, :, 1], p1[:, :, 1], ALU.add))
            for c in range(NCH):
                v.wait_ge(activated, c + 1)
                v.tensor_reduce(gs[:, c:c + 1], act[c % 2][:, :, 3:3 + W], AX.XY, ALU.add).then_inc(mean_step, 1)
            v.wait_ge(mean_step, NCH)
            link(v.tensor_reduce(gm[:, 0:1], gs[:, :], AX.X, ALU.add))
            v.tensor_scalar(gm[:, 0:1], gm[:, 0:1], 1.0 / N, None, ALU.mult).then_inc(mean_ready, 1)
            v.wait_ge(tanh_done, 1)
            link(v.tensor_scalar(gm[:, 2:3], gm[:, 1:2], 0.0, vb[:, 1:2], ALU.max, ALU.add))
            v.tensor_scalar(diag[:, :], idf[0:NF, 0:NF], gm[:, 2:3], None, ALU.mult).then_inc(diag_ready, 1)
            v.wait_ge(linear, 2)
            link(v.tensor_copy(row[:, :], ps[0:G, 0:NF]))
            link(v.tensor_reduce(tot[:, 0:1], row[:, :], AX.X, ALU.add))
            link(v.reciprocal(tot[:, 0:1], tot[:, 0:1]))
            link(v.tensor_scalar(row[:, :], row[:, :], tot[:, 0:1], None, ALU.mult))
            link(v.tensor_scalar(row[:, :], row[:, :], float(C), None, ALU.mult))
            link(v.tensor_scalar(row[:, :], row[:, :], ROUND, None, ALU.add))
            link(v.tensor_scalar(prm[:, 1:NF], row[:, 0:NF - 1], ROUND, None, ALU.subtract))
            link(v.tensor_reduce(tot[:, 1:2], prm[:, 1:NF], AX.X, ALU.add))
            link(v.tensor_scalar(prm[:, NF:], tot[:, 1:2], -1.0, float(C), ALU.mult, ALU.add))
            for g in range(2):
                v.tensor_scalar(ge[:, g, :], prm[:, :], ch[:, g:g + 1], None, ALU.is_le)
                link(v.tensor_scalar(lt[:, g, :], prm[:, :], ch[:, g:g + 1], None, ALU.is_gt))
            link(v.tensor_tensor(msk[:, :, :], ge[:, :, 0:NF], lt[:, :, 1:], ALU.mult))
            link(v.tensor_scalar(msk[:, :, :], msk[:, :, :], -1.0, 1.0, ALU.mult, ALU.add))
            for g in range(2):
                link(v.tensor_tensor_scan(suf[:, g, NF - 1::-1], msk[:, g, ::-1], zer[:, :], 1.0, ALU.mult, ALU.add))
            v.tensor_tensor(pick[:, :, :], suf[:, :, 1:], suf[:, :, 0:NF], ALU.subtract).then_inc(pick_ready, 1)
            v.wait_ge(pick_turned, 1)
            v.tensor_copy(pickT[:, 0, :], pg[0][0:NF, 0:G])
            v.tensor_copy(pickT[:, 1, :], pg[1][0:NF, 0:G]).then_inc(pick_copied, 1)
            v.wait_ge(filt_ready, 1)
            for g in range(2):
                link(v.tensor_tensor(prod[:, g, :, :], xps[:, :, g, :],
                                     pf[g][0:G, 0:49].rearrange("p (o k) -> p o k", o=1).broadcast_to([G, B, 49]), ALU.mult))
            link(v.tensor_reduce(y0[:, :, :], prod[:, :, :, :], AX.X, ALU.add))
            v.tensor_scalar(y0[:, :, :], y0[:, :, :], 1.0 / 64, None, ALU.mult).then_inc(y0_ready, 1)
            v.wait_ge(y1_ready, 1)
            for m in range(2):
                link(v.tensor_scalar(yo[:, m, :], ps[0:G, B * m:B * m + B], s1[:, m, 0:1], s1[:, m, 1:2], ALU.mult, ALU.add))
            v.tensor_scalar(yo[:, :, :], yo[:, :, :], 0.0, 1.0, ALU.max, ALU.add).then_inc(gate_ready, 1)


def dct_basis():
    import numpy as np
    t = np.arange(DCT, dtype=np.float32) + np.float32(0.5)

    def along(freq):
        f = np.array(freq, np.float32)[:, None]
        r = (np.cos(np.float32(np.pi) * f * t[None] / np.float32(DCT)) / np.sqrt(np.float32(DCT))).astype(np.float32)
        return np.where(f == 0, r, r * np.sqrt(np.float32(2.0))).astype(np.float32)
    return (along(LOW_X)[:, :, None] * along(LOW_Y)[:, None, :]).reshape(NF, 49).astype(np.float32)


def channels():
    import numpy as np
    return np.ascontiguousarray(np.arange(C, dtype=np.float32).reshape(2, G).T)


def window_strips(nc, x1p, gate, mask, n1g, n1b, qkv_wT, qkv_b, tempr, biasT, proj_wT, proj_b, ident, pout):
    with ExitStack() as ctx:
        sb = lambda name, shape, dt=F32: ctx.enter_context(nc.sbuf_tensor(name, shape, dt))
        pt = lambda name, p=128: ctx.enter_context(nc.psum_tensor(name, [p, 512], F32))
        sem = ctx.enter_context(stage_semaphores(nc))
        w0 = sb("d_w0", [97, 2, 3 * C])
        w = sb("d_w", [97, 2, 3 * C])
        ng = sb("d_ng", [96, 2])
        nb = sb("d_nb", [97, 2])
        tmp = sb("d_tmp", [97, C])
        bt = sb("d_bt", [128, HEADS, 64])
        wp = sb("d_wp", [G, 2, C])
        bp = sb("d_bp", [G, 2])
        idf = sb("d_idf", [128, 128])
        mean_w = sb("d_mean_w", [G, G])
        gt = [sb(f"d_gt{i}", [G, 2]) for i in range(2)]
        xs = [sb(f"d_xs{i}", [G, 2, SN]) for i in range(2)]
        ce = sb("d_ce", [G, 2, SN])
        sq = sb("d_sq", [G, 2, SN])
        rstd = sb("d_rstd", [G, SN])
        xn = [sb(f"d_xn{i}", [97, 2, WS, PW]) for i in range(2)]
        qs = [sb(f"d_qs{i}", [G, 2, 3, NR, 64]) for i in range(2)]
        xw = [sb(f"d_xw{i}", [97, 2, NR, 64]) for i in range(2)]
        ks = [sb(f"d_ks{i}", [G, 2, WS, PW]) for i in range(2)]
        vt = [sb(f"d_vt{i}", [128, 2, 3, 128]) for i in range(2)]
        sc = [sb(f"d_sc{i}", [128, HEADS, 64]) for i in range(2)]
        mx = [sb(f"d_mx{i}", [128, HEADS]) for i in range(2)]
        et = sb("d_et", [128, 3, 128])
        acc = [sb(f"d_acc{i}", [128, 3, WS, PW]) for i in range(2)]
        rec = sb("d_rec", [128, 3, ON])
        att = sb("d_att", [G, 2, ON])
        out = [sb(f"d_out{i}", [G, 2, ON]) for i in range(2)]
        pa_ = [pt(f"d_pa{i}") for i in range(2)]
        pS = [pt(f"d_ps{i}") for i in range(2)]
        pT, pV, pO, pP = pt("d_pt"), pt("d_pv"), pt("d_po"), pt("d_pp")
        par_loaded = sem("d_par_loaded")
        in_loaded = [sem(f"d_in_loaded{i}") for i in range(2)]
        consts = sem("d_consts")
        bias_sum = sem("d_bias_sum")
        folding = sem("d_folding")
        scaled = sem("d_scaled")
        mean_done = sem("d_mean_done")
        centred = sem("d_centred")
        squared = sem("d_squared")
        var_done = sem("d_var_done")
        std_ready = sem("d_std_ready")
        sums_moved = sem("d_sums_moved")
        tick = sem("d_tick")
        rstd_ready = sem("d_rstd_ready")
        normed = sem("d_normed")
        windowed = sem("d_windowed")
        qk_done = sem("d_qk_done")
        q_evac = sem("d_q_evac")
        k_evac = sem("d_k_evac")
        scores = sem("d_scores")
        v_done = sem("d_v_done")
        v_evac = sem("d_v_evac")
        biased = sem("d_biased")
        max_found = sem("d_max_found")
        shifted = sem("d_shifted")
        exp_done = sem("d_exp_done")
        turned = sem("d_turned")
        et_evac = sem("d_et_evac")
        summed = sem("d_summed")
        laid = sem("d_laid")
        acc_ready = sem("d_acc_ready")
        rec_ready = sem("d_rec_ready")
        divided = sem("d_divided")
        projected = sem("d_projected")
        p_evac = sem("d_p_evac")
        stored = [sem(f"d_stored{i}") for i in range(2)]
        block = ctx.enter_context(nc.Block())
        xv = x1p.rearrange("(b g p) h w -> b p g (h w)", b=B, g=2)
        ov = pout.rearrange("(b g p) h w -> b p g (h w)", b=B, g=2)
        gv = gate.rearrange("p (g b) -> b p g", g=2)
        mv = mask.rearrange("(o n) -> o n", o=1)

        def strips(eng, first, strip):
            with eng.Fori(0, B) as b:
                first(b)
                strip(b, 0, 0, 0, False, True)
                with eng.Fori(0, 4) as i:
                    strip(b, 2 * i + 1, i, 1, True, True)
                    strip(b, 2 * i + 2, i, 0, True, True)
                strip(b, NR - 1, 4, 1, True, False)

        def following(s, i, par, nxt):
            if i + 1 < NP:
                return s, i + 1, par
            return (s + 1, 0, 1 - par) if nxt else None

        def windows(t):
            a = t.copy()
            return bass.AP(tensor=a.tensor, offset=a.offset, ap=[list(a.ap[0]), [STEP, NR], [PW, WS], [1, WS]])

        def patch(t, k, g, wi):
            return t[k, g, :, STEP * wi:STEP * wi + WS]

        @block.sync
        def _(sp):
            with nc.allow_non_contiguous_dma(reason="small vectors, once"):
                sp.dma_start(w0[0:G, :, :], qkv_wT.rearrange("(g p) o -> p g o", p=G)).then_inc(par_loaded, 16)
                sp.dma_start(w0[G:97, 1, :], qkv_b.rearrange("(a o) -> a o", a=1)).then_inc(par_loaded, 16)
                sp.dma_start(ng[:, :], n1g.rearrange("(g p) -> p g", p=G)).then_inc(par_loaded, 16)
                sp.dma_start(nb[0:G, :], n1b.rearrange("(g p) -> p g", p=G)).then_inc(par_loaded, 16)
                sp.dma_start(tmp[:, :], tempr.partition_broadcast(97)).then_inc(par_loaded, 16)
                for k in range(2):
                    sp.dma_start(bt[64 * k:64 * k + 64, :, :], biasT).then_inc(par_loaded, 16)
                sp.dma_start(wp[:, :, :], proj_wT.rearrange("(g p) o -> p g o", p=G)).then_inc(par_loaded, 16)
                sp.dma_start(bp[:, :], proj_b.rearrange("(g p) -> p g", p=G)).then_inc(par_loaded, 16)
                sp.dma_start(idf[:, :], ident).then_inc(par_loaded, 16)

            def load(b, r, par, s):
                sp.dma_start(xs[par][:, :, :], xv[b, :, :, bass.ds(STEP * PW * r, SN)]).then_inc(in_loaded[par], 16)
                sp.dma_start(xn[par][G:97, 1, :, :].rearrange("p h w -> p (h w)"), mv[:, bass.ds(STEP * PW * r, SN)]).then_inc(in_loaded[par], 16)
                with nc.allow_non_contiguous_dma(reason="one gate per channel"):
                    sp.dma_start(gt[par][:, :], gv[b]).then_inc(in_loaded[par], 16)

            def move_sums(s, par):
                sp.wait_ge(laid, 10 * s + 10)
                sp.sem_inc(tick, 1)
                sp.wait_ge(divided, 3 * s)
                sp.sem_inc(tick, 1)
                for odd in range(2):
                    sp.dma_start(rec[64 * odd:64 * odd + 32, :, :],
                                 acc[par][64 * odd + 32:64 * odd + 64, :, 0:STEP, :].rearrange("p a h w -> p a (h w)")
                                 ).then_inc(sums_moved, 16)

            def first(b):
                sp.wait_ge(v_done, NP * NR * b)
                sp.sem_inc(tick, 1)
                sp.wait_ge(centred, NR * b)
                sp.sem_inc(tick, 1)
                load(b, 0, 0, NR * b)

            def strip(b, r, h, par, prev, nxt):
                s = NR * b + r
                if nxt:
                    sp.wait_ge(v_done, NP * s)
                    sp.sem_inc(tick, 1)
                    load(b, r + 1, 1 - par, s + 1)
                if prev:
                    move_sums(s - 1, 1 - par)
                if not nxt:
                    move_sums(s, par)
            strips(sp, first, strip)

        @block.tensor
        def _(pe):
            pe.wait_ge(par_loaded, 160)
            pe.wait_ge(consts, 3)
            for o, n, bank in ((0, 512, pS[0]), (512, 64, pS[1])):
                pe.matmul(bank[0:1, 0:n], nb[0:G, 0:1], w0[0:G, 0, o:o + n], start=True, stop=False)
                mm = pe.matmul(bank[0:1, 0:n], nb[0:97, 1:2], w0[0:97, 1, o:o + n], start=False, stop=True)
            mm.then_inc(bias_sum, 1)
            pe.wait_ge(folding, 4)

            def moment(s, src, bank, ready, done):
                pe.wait_ge(ready, s + 1)
                for g in range(2):
                    mm = pe.matmul(bank[0:G, 0:SN], mean_w[:, :], src[:, g, :], start=(g == 0), stop=(g == 1))
                mm.then_inc(done, 1)

            def mean(s, par):
                pe.wait_ge(q_evac, 2 * s)
                moment(s, xs[par], pa_[0], scaled, mean_done)

            def var(s):
                pe.wait_ge(k_evac, 2 * s)
                moment(s, sq, pa_[1], squared, var_done)

            def qk(s, par, m):
                if m == 0:
                    pe.wait_ge(normed, s + 1)
                if m >= 2:
                    pe.wait_ge(q_evac if m == 2 else k_evac, 2 * s + 1)
                col = slice(G * m, G * m + G)
                for g in range(2):
                    kk = slice(0, G + g)
                    mm = pe.matmul(pa_[m % 2][0:G, 0:SN], w[kk, g, col], xn[par][kk, g, :, :].rearrange("p h w -> p (h w)"),
                                   start=(g == 0), stop=(g == 1))
                mm.then_inc(qk_done, 1)

            def score(s, i, par):
                t = NP * s + i
                tp = (par + i) % 2
                if i == 0:
                    pe.wait_ge(q_evac, 2 * s + 2)
                    pe.wait_ge(k_evac, 2 * s + 2)
                if not (isinstance(t, int)) or t >= 2:
                    pe.wait_ge(biased, (NP * s if i == 0 else t - 1) if i < 2 else t - 1)
                for h in range(HEADS):
                    kk = slice(0, G)
                    for k in range(2):
                        wi = 2 * i + k
                        mm = pe.matmul(pS[tp][64 * k:64 * k + 64, 64 * h:64 * h + 64], qs[par][kk, h // 3, h % 3, wi, :],
                                       patch(ks[par], kk, h // 3, wi), start=True, stop=True)
                mm.then_inc(scores, 1)

            def values(s, i, par):
                t = NP * s + i
                pe.wait_ge(v_evac, t)
                if i == 0:
                    pe.wait_ge(windowed, s + 1)
                for k in range(2):
                    for odd in range(2):
                        for g in range(2):
                            kk = slice(0, G + g)
                            rhs = w[kk, g, 2 * C:3 * C].rearrange("p (a o c) -> p a o c", o=2, c=32)[:, :, odd, :]
                            mm = pe.matmul(pV[64 * odd:64 * odd + 64, G * k:G * k + G], xw[par][kk, g, 2 * i + k, :], rhs,
                                           start=(g == 0), stop=(g == 1))
                mm.then_inc(v_done, 1)

            def turn(s, i, par):
                t = NP * s + i
                tp = (par + i) % 2
                pe.wait_ge(exp_done, t + 1)
                pe.wait_ge(et_evac, t)
                for a in range(3):
                    mm = pe.transpose(pT[:, 128 * a:128 * a + 128], sc[tp][:, 2 * a:2 * a + 2, :].rearrange("p a b -> p (a b)"), idf[:, :])
                mm.then_inc(turned, 1)

            def weigh(s, i, par):
                t = NP * s + i
                tp = (par + i) % 2
                pe.wait_ge(et_evac, t + 1)
                pe.wait_ge(v_evac, t + 1)
                pe.wait_ge(laid, 2 * t)
                pe.sem_inc(tick, 1)
                for k in range(2):
                    for a in range(3):
                        mm = pe.matmul(pO[:, 128 * a + 64 * k:128 * a + 64 * k + 64], vt[tp][:, k, a, :],
                                       et[:, a, 64 * k:64 * k + 64], start=True, stop=True)
                mm.then_inc(summed, 1)

            def project(s):
                pe.wait_ge(divided, 3 * s + 3)
                for m in range(2):
                    pe.wait_ge(p_evac, 2 * s + m)
                    for g in range(2):
                        mm = pe.matmul(pP[0:G, 0:ON], wp[:, g, G * m:G * m + G], att[:, g, :], start=(g == 0), stop=(g == 1))
                    mm.then_inc(projected, 1)

            def first(b):
                s = NR * b
                mean(s, 0)
                var(s)
                for m in range(4):
                    qk(s, 0, m)
                score(s, 0, 0)
                values(s, 0, 0)

            def strip(b, r, h, par, prev, nxt):
                s = NR * b + r
                for i in range(NP):
                    ahead = following(s, i, par, nxt)
                    if ahead:
                        score(*ahead)
                    if nxt and i == 0:
                        mean(s + 1, 1 - par)
                    if nxt and i == 3:
                        qk(s + 1, 1 - par, 2)
                        qk(s + 1, 1 - par, 3)
                    turn(s, i, par)
                    if ahead:
                        values(*ahead)
                    weigh(s, i, par)
                    if nxt and i == 0:
                        var(s + 1)
                    if nxt and i == 2:
                        qk(s + 1, 1 - par, 0)
                        qk(s + 1, 1 - par, 1)
                    if prev and i == NP - 1:
                        project(s - 1)
                if not nxt:
                    project(s)
            strips(pe, first, strip)

        @block.scalar
        def _(a):
            a.wait_ge(par_loaded, 160)

            def scale(b, before, par, s):
                a.wait_ge(in_loaded[par], 48 * (NP * b + before + 1))
                for g in range(2):
                    last = a.activation(xs[par][:, g, :], xs[par][:, g, :], ACT.Copy, scale=gt[par][:, g:g + 1])
                last.then_inc(scaled, 1)

            def square(s):
                a.wait_ge(centred, s + 1)
                a.activation(sq[:, :, :], ce[:, :, :], ACT.Square).then_inc(squared, 1)

            def root(s):
                a.wait_ge(var_done, s + 1)
                a.wait_ge(normed, s)
                a.activation(rstd[:, :], pa_[1][0:G, 0:SN], ACT.Sqrt, bias=EPS).then_inc(std_ready, 1)

            def evac(s, par, m):
                a.wait_ge(qk_done, 4 * s + m + 1)
                if m < 2:
                    for j in range(3):
                        kk = slice(32 * j, 32 * j + 32)
                        last = a.activation(qs[par][kk, m, j, :, :].rearrange("p n (h w) -> p n h w", w=WS),
                                            windows(pa_[m][kk, 0:SN]), ACT.Copy)
                    last.then_inc(k_evac if m else q_evac, 1)
                else:
                    a.activation(ks[par][:, 0, :, :].rearrange("p h w -> p (h w)"), pa_[0][0:G, 0:SN], ACT.Copy).then_inc(q_evac, 1)

            def values(s, i, par):
                t = NP * s + i
                a.wait_ge(v_done, t + 1)
                for odd in range(2):
                    kk = slice(64 * odd, 64 * odd + 64)
                    last = a.activation(vt[(par + i) % 2][kk, :, :, 64 * odd:64 * odd + 32],
                                        pV[kk, 0:2 * G].rearrange("p (k a c) -> p k a c", k=2, c=32), ACT.Copy)
                last.then_inc(v_evac, 1)

            def expo(s, i, par):
                t = NP * s + i
                a.wait_ge(shifted, t + 1)
                q = sc[(par + i) % 2]
                a.activation(q[:, :, :], q[:, :, :], ACT.Exp).then_inc(exp_done, 1)

            def turn(s, i):
                a.wait_ge(turned, NP * s + i + 1)
                a.activation(et[:, :, :], pT[:, 0:384].rearrange("p (a n) -> p a n", a=3), ACT.Copy).then_inc(et_evac, 1)

            def finish(s, par, before):
                a.wait_ge(stored[par], 16 * before)
                for m in range(2):
                    a.wait_ge(projected, 2 * s + m + 1)
                    a.activation(out[par][:, m, :], pP[0:G, 0:ON], ACT.Identity, bias=bp[:, m:m + 1]).then_inc(p_evac, 1)

            def first(b):
                s = NR * b
                scale(b, 0, 0, s)
                square(s)
                root(s)
                evac(s, 0, 0)
                evac(s, 0, 1)
                evac(s, 0, 2)
                values(s, 0, 0)
                expo(s, 0, 0)

            def strip(b, r, h, par, prev, nxt):
                s = NR * b + r
                if nxt:
                    scale(b, (h + 1 if par else h + 1 if prev else 0), 1 - par, s + 1)
                for i in range(NP):
                    ahead = following(s, i, par, nxt)
                    turn(s, i)
                    if nxt and i == 0:
                        square(s + 1)
                    if nxt and i == 3:
                        evac(s + 1, 1 - par, 2)
                    if ahead:
                        values(*ahead)
                        expo(*ahead)
                    if nxt and i == 0:
                        root(s + 1)
                    if nxt and i == 2:
                        evac(s + 1, 1 - par, 0)
                        evac(s + 1, 1 - par, 1)
                    if prev and i == NP - 1:
                        finish(s - 1, 1 - par, NP * b + h)
                if not nxt:
                    finish(s, par, NP * b + 4)
            strips(a, first, strip)

        @block.vector
        def _(v):
            v.memset(mean_w[:, :], 1.0 / C)
            v.memset(rec[:, :, :], 1.0)
            v.memset(nb[G:97, :], 1.0).then_inc(consts, 1)
            for k in range(2):
                v.memset(qs[k][:, :, :, :, :], 0.0)
                v.memset(vt[k][0:64, :, :, 64:128], 0.0)
                v.memset(vt[k][64:128, :, :, 0:64], 0.0)
                v.memset(vt[k][0:64, :, :, 32:64], 1.0)
                v.memset(vt[k][64:128, :, :, 96:128], 1.0).then_inc(consts, 1)
            v.wait_ge(par_loaded, 160)
            for g in range(2):
                last = v.tensor_scalar(w[0:G, g, :], w0[0:G, g, :], ng[:, g:g + 1], None, ALU.mult)
            last.then_inc(folding, 1)
            v.wait_ge(bias_sum, 1)
            v.tensor_copy(w[G:97, 1, 0:512], pS[0][0:1, 0:512])
            v.tensor_copy(w[G:97, 1, 512:576], pS[1][0:1, 0:64]).then_inc(folding, 1)
            v.wait_ge(folding, 2)
            for g in range(2):
                v.tensor_tensor(w[0:G + g, g, 0:C], w[0:G + g, g, 0:C], tmp[0:G + g, :], ALU.mult).then_inc(folding, 1)

            def centre(s, par):
                v.wait_ge(mean_done, s + 1)
                v.wait_ge(squared, s)
                v.tensor_tensor(ce[:, :, :], xs[par][:, :, :],
                                pa_[0][0:G, 0:SN].rearrange("p (o n) -> p o n", o=1).broadcast_to([G, 2, SN]), ALU.subtract).then_inc(centred, 1)

            def norm(s, par):
                v.wait_ge(std_ready, s + 1)
                v.reciprocal(rstd[:, :], rstd[:, :]).then_inc(rstd_ready, 1)
                v.wait_ge(rstd_ready, s + 1)
                v.tensor_tensor(xn[par][0:G, :, :, :].rearrange("p g h w -> p g (h w)"), ce[:, :, :],
                                rstd[:, :].rearrange("p (o n) -> p o n", o=1).broadcast_to([G, 2, SN]), ALU.mult).then_inc(normed, 1)

            def evac(s, par, m):
                v.wait_ge(qk_done, 4 * s + m + 1)
                v.tensor_copy(ks[par][:, 1, :, :].rearrange("p h w -> p (h w)"), pa_[1][0:G, 0:SN]).then_inc(k_evac, 1)

            def soft(s, i, par):
                t = NP * s + i
                tp = (par + i) % 2
                v.wait_ge(scores, t + 1)
                v.tensor_tensor(sc[tp][:, :, :], pS[tp][:, 0:384].rearrange("p (h j) -> p h j", j=64), bt[:, :, :], ALU.add).then_inc(biased, 1)
                v.wait_ge(biased, t + 1)
                v.tensor_reduce(mx[tp][:, :], sc[tp][:, :, :], AX.X, ALU.max).then_inc(max_found, 1)
                v.wait_ge(max_found, t + 1)
                v.tensor_tensor(sc[tp][:, :, :], sc[tp][:, :, :],
                                mx[tp][:, :].rearrange("p (h o) -> p h o", o=1).broadcast_to([128, HEADS, 64]), ALU.subtract).then_inc(shifted, 1)

            def lay(s, i, par):
                t = NP * s + i
                if i == 0:
                    v.wait_ge(acc_ready, s + 1)
                v.wait_ge(summed, t + 1)
                for k in range(2):
                    dst = acc[par][:, :, :, STEP * (2 * i + k):STEP * (2 * i + k) + WS]
                    v.wait_ge(laid, 2 * t + k)
                    v.tensor_tensor(dst, dst, pO[:, 0:384].rearrange("p (a k h w) -> p a k h w", a=3, k=2, h=8)[:, :, k, :, :],
                                    ALU.add).then_inc(laid, 1)

            def divide(s, par, a):
                v.wait_ge(sums_moved, 32 * (s + 1))
                v.wait_ge(laid, 10 * s + 10)
                v.wait_ge(projected, 2 * s)
                v.reciprocal(rec[0:96, a, :], rec[0:96, a, :]).then_inc(rec_ready, 1)
                v.wait_ge(rec_ready, 3 * s + a + 1)
                for odd in range(2):
                    h = 2 * a + odd
                    last = v.tensor_tensor(att[32 * (h % 3):32 * (h % 3) + 32, h // 3, :],
                                           acc[par][64 * odd:64 * odd + 32, a, 0:STEP, :].rearrange("p h w -> p (h w)"),
                                           rec[64 * odd:64 * odd + 32, a, :], ALU.mult)
                last.then_inc(divided, 1)

            def first(b):
                s = NR * b
                centre(s, 0)
                norm(s, 0)
                evac(s, 0, 3)
                soft(s, 0, 0)

            def strip(b, r, h, par, prev, nxt):
                s = NR * b + r
                for i in range(NP):
                    ahead = following(s, i, par, nxt)
                    if ahead:
                        soft(*ahead)
                    if nxt and i == 0:
                        centre(s + 1, 1 - par)
                    if nxt and i == 3:
                        evac(s + 1, 1 - par, 3)
                    lay(s, i, par)
                    if nxt and i == 1:
                        norm(s + 1, 1 - par)
                    if prev and i in (0, 2, 3):
                        divide(s - 1, 1 - par, (0, 2, 3).index(i))
                if not nxt:
                    for i in range(3):
                        divide(s, par, i)
            strips(v, first, strip)

        @block.gpsimd
        def _(p):
            def store(b, r, s, par):
                p.wait_ge(p_evac, 2 * s + 2)
                p.dma_start(ov[b, :, :, bass.ds(ON * r, ON)], out[par][:, :, :]).then_inc(stored[par], 16)

            def window(s, par):
                p.wait_ge(normed, s + 1)
                p.wait_ge(in_loaded[par], 48)
                p.sem_inc(tick, 1)
                for g in range(2):
                    last = p.tensor_copy(xw[par][0:G + g, g, :, :].rearrange("p n (h w) -> p n h w", w=WS),
                                         windows(xn[par][0:G + g, g, :, :].rearrange("p h w -> p (h w)")))
                last.then_inc(windowed, 1)

            def first(b):
                window(NR * b, 0)
                p.wait_ge(divided, 3 * NR * b)
                p.sem_inc(tick, 1)
                p.memset(acc[0][:, :, :, :], 0.0).then_inc(acc_ready, 1)

            def strip(b, r, h, par, prev, nxt):
                s = NR * b + r
                if nxt:
                    window(s + 1, 1 - par)
                    p.wait_ge(divided, 3 * s)
                    p.sem_inc(tick, 1)
                    p.memset(acc[1 - par][:, :, 2:, :], 0.0)
                    p.wait_ge(laid, 10 * s + 10)
                    p.sem_inc(tick, 1)
                    p.tensor_copy(acc[1 - par][:, :, 0:2, :], acc[par][:, :, STEP:WS, :]).then_inc(acc_ready, 1)
                if prev:
                    store(b, r - 1, s - 1, 1 - par)
                if not nxt:
                    store(b, r, s, par)
            strips(p, first, strip)
            p.wait_ge(stored[0], 16 * NP * B)
            p.wait_ge(stored[1], 16 * NP * B)


def inside():
    import numpy as np
    m = np.zeros((PW, PW), np.float32)
    m[3:59, 3:59] = 1
    return m.reshape(-1)


def relative(rpb):
    import numpy as np
    c = np.stack(np.meshgrid(np.arange(WS), np.arange(WS), indexing="ij"), 0).reshape(2, -1)
    d = c[:, :, None] - c[:, None, :] + WS - 1
    return np.ascontiguousarray(np.asarray(rpb)[d[0] * (2 * WS - 1) + d[1]].transpose(0, 2, 1))


def forward_block(nc, x1p, gate, pout, hft_w, hft_b, n2g, n2b, fc1_wT, fc1_b, sgn_g, sgn_b, sg_w, sg_b, fc2_wT, fc2_b, ident, x3):
    with ExitStack() as ctx:
        sb = lambda name, shape, dt=F32: ctx.enter_context(nc.sbuf_tensor(name, shape, dt))
        pt = lambda name, p=G: ctx.enter_context(nc.psum_tensor(name, [p, 512], F32))
        sem = ctx.enter_context(stage_semaphores(nc))
        w1 = sb("e_w1", [G, 2, HID])
        w2 = sb("e_w2", [G, 4, C])
        hw = sb("e_hw", [G, 2, 9])
        gw = sb("e_gw", [G, 4, 9])
        hb = sb("e_hb", [G, 2])
        ng = sb("e_ng", [G, 2])
        nb = sb("e_nb", [G, 2])
        b1o = sb("e_b1o", [G, 8])
        b1v = sb("e_b1", [G, 8])
        sgg = sb("e_sgg", [G, 4])
        sgb = sb("e_sgb", [G, 4])
        gb = sb("e_gb", [G, 4])
        b2v = sb("e_b2", [G, 2])
        idf = sb("e_idf", [128, 128])
        diag = sb("e_diag", [G, 2, 9, G])
        m192 = sb("e_m192", [G, G])
        m384 = sb("e_m384", [G, G])
        gt = [sb(f"e_gt{i}", [G, 2]) for i in range(4)]
        pin = [sb(f"e_pin{i}", [G, 2, 8, PW]) for i in range(4)]
        xin = [sb(f"e_xin{i}", [G, 2, 8, PW]) for i in range(4)]
        at = [sb(f"e_at{i}", [G, 2, 10, AW]) for i in range(4)]
        zt = [sb(f"e_zt{i}", [G, 4, 10, AW]) for i in range(4)]
        z1 = [sb(f"e_z1{i}", [G, 4, CH]) for i in range(4)]
        x1 = [sb(f"e_x1{i}", [G, 2, CH]) for i in range(NCH)]
        rows2, s2 = sb("e_rows2", [G, 2, 4, W]), sb("e_s2", [G, 2, 4, 28])
        rows4, s4 = sb("e_rows4", [G, 2, 2, 28]), sb("e_s4", [G, 2, 2, 14])
        rows8, s8 = sb("e_rows8", [G, 2, 14]), sb("e_s8", [G, 2, 7])
        sig = sb("e_sig", [G, 2, CH])
        ce = sb("e_ce", [G, 2, CH])
        sq = sb("e_sq", [G, 2, CH])
        rs = sb("e_rs", [G, CH])
        xn = sb("e_xn", [G, 2, CH])
        z2 = sb("e_z2", [G, 4, CH])
        sq2 = sb("e_sq2", [G, 4, CH])
        rs2 = sb("e_rs2", [G, CH])
        zc = sb("e_zc", [G, 4, CH])
        w1o = zc[:, :, :].rearrange("p a b -> p (a b)")[:, 0:2 * HID].rearrange("p (g o) -> p g o", g=2)
        out = [sb(f"e_out{i}", [G, 2, CH]) for i in range(2)]
        pC = [pt(f"e_pc{i}") for i in range(2)]
        pM, pV = pt("e_pm"), pt("e_pv")
        p1 = [pt(f"e_p1{i}") for i in range(2)]
        p2 = [pt(f"e_p2{i}") for i in range(2)]
        par_loaded = sem("e_par_loaded")
        in_loaded = [sem(f"e_in_loaded{i}") for i in range(4)]
        cleared = sem("e_cleared")
        folded = sem("e_folded")
        bias_sum = sem("e_bias_sum")
        tripled = sem("e_tripled")
        pool_step = sem("e_pool_step")
        high_ready = sem("e_high_ready")
        conv_done = sem("e_conv_done")
        sig_done = sem("e_sig_done")
        sig_mul = sem("e_sig_mul")
        x1_ready = sem("e_x1_ready")
        mean1 = sem("e_mean1")
        centred1 = sem("e_centred1")
        squared1 = sem("e_squared1")
        var1 = sem("e_var1")
        std1 = sem("e_std1")
        rstd1 = sem("e_rstd1")
        normed1 = sem("e_normed1")
        hidden = sem("e_hidden")
        gelu_done = sem("e_gelu_done")
        mean2 = sem("e_mean2")
        centred2 = sem("e_centred2")
        squared2 = sem("e_squared2")
        var2 = sem("e_var2")
        std2 = sem("e_std2")
        rstd2 = sem("e_rstd2")
        normed2 = sem("e_normed2")
        affine2 = sem("e_affine2")
        halo_ready = sem("e_halo_ready")
        dw_step = sem("e_dw_step")
        gated = sem("e_gated")
        mixed = sem("e_mixed")
        finished = sem("e_finished")
        stored = [sem(f"e_stored{i}") for i in range(2)]
        tick = sem("e_tick")
        block = ctx.enter_context(nc.Block())
        xv = x1p.rearrange("(b g p) h w -> b p g (h w)", b=B, g=2)
        pv = pout.rearrange("(b g p) h w -> b p g (h w)", b=B, g=2)
        ov = x3.rearrange("(b g p) n -> b p g n", b=B, g=2)
        gv = gate.rearrange("p (g b) -> b p g", g=2)

        def img(ap):
            return ap.rearrange("p (h w) -> p h w", w=W)

        def spread(ap, n):
            return ap.rearrange("p (o m) -> p o m", o=1).broadcast_to([G, n, CH])

        @block.sync
        def _(sp):
            with nc.allow_non_contiguous_dma(reason="small vectors, once"):
                sp.dma_start(w1o[:, :, :], fc1_wT.rearrange("(g p) o -> p g o", p=G)).then_inc(par_loaded, 16)
                sp.dma_start(w2[:, :, :], fc2_wT.rearrange("(g p) o -> p g o", p=G)).then_inc(par_loaded, 16)
                sp.dma_start(hw[:, :, :], hft_w.rearrange("(g p) k -> p g k", p=G)).then_inc(par_loaded, 16)
                sp.dma_start(gw[:, :, :], sg_w.rearrange("(g p) k -> p g k", p=G)).then_inc(par_loaded, 16)
                for dst, src in ((hb, hft_b), (ng, n2g), (nb, n2b), (b1o, fc1_b), (sgg, sgn_g), (sgb, sgn_b), (gb, sg_b), (b2v, fc2_b)):
                    sp.dma_start(dst[:, :], src.rearrange("(g p) -> p g", p=G)).then_inc(par_loaded, 16)
                sp.dma_start(idf[:, :], ident).then_inc(par_loaded, 16)

            def store(b, c):
                sp.wait_ge(finished, 2 * NCH * b + 2 * c + 2)
                sp.sem_inc(tick, 1)
                sp.dma_start(ov[b, :, :, c * CH:(c + 1) * CH], out[c % 2][:, :, :]).then_inc(stored[c % 2], 16)

            def step(b, k):
                now, old = chunk(b, k, 0), chunk(b, k, LAG)
                if now:
                    b, c = now
                    o = PLACE[c]
                    sp.wait_ge(x1_ready, before(b, c, 3, 2))
                    sp.sem_inc(tick, 1)
                    sp.dma_start(pin[o][:, :, :, :].rearrange("p g h w -> p g (h w)"), pv[b, :, :, (3 + 8 * c) * PW:(11 + 8 * c) * PW])\
                        .then_inc(in_loaded[o], 16)
                    sp.dma_start(xin[o][:, :, :, :].rearrange("p g h w -> p g (h w)"), xv[b, :, :, (3 + 8 * c) * PW:(11 + 8 * c) * PW])\
                        .then_inc(in_loaded[o], 16)
                    with nc.allow_non_contiguous_dma(reason="one gate per channel"):
                        sp.dma_start(gt[o][:, :], gv[b]).then_inc(in_loaded[o], 16)
                if old:
                    store(*old)
            pipeline(sp, step, LAG)
            sp.wait_ge(stored[0], 16 * 4 * B)
            sp.wait_ge(stored[1], 16 * 3 * B)

        @block.gpsimd
        def _(p):
            for i in range(4):
                p.memset(at[i][:, :, :, :], 0.0)
                p.memset(zt[i][:, :, :, :], 0.0).then_inc(cleared, 1)

            def high(b, c):
                q = NCH * b + c
                o = PLACE[c]
                n = 21 * c - (c > 0)

                def link(ins):
                    nonlocal n
                    n += 1
                    ins.then_inc(pool_step, 1)
                    p.wait_ge(pool_step, 21 * NCH * b + n)
                    p.sem_inc(tick, 1)
                p.wait_ge(tripled, q + 1)
                src = pin[o][:, :, :, 3:3 + W]
                link(p.tensor_tensor(rows2[:, :, :, :], src[:, :, 0::2, :], src[:, :, 1::2, :], ALU.add))
                link(p.tensor_tensor(s2[:, :, :, :], rows2[:, :, :, 0::2], rows2[:, :, :, 1::2], ALU.add))
                link(p.tensor_tensor(rows4[:, :, :, :], s2[:, :, 0::2, :], s2[:, :, 1::2, :], ALU.add))
                link(p.tensor_tensor(s4[:, :, :, :], rows4[:, :, :, 0::2], rows4[:, :, :, 1::2], ALU.add))
                link(p.tensor_tensor(rows8[:, :, :], s4[:, :, 0, :], s4[:, :, 1, :], ALU.add))
                link(p.tensor_tensor(s8[:, :, :], rows8[:, :, 0::2], rows8[:, :, 1::2], ALU.add))
                link(p.tensor_scalar(s8[:, :, :], s8[:, :, :], 1.0 / 64, None, ALU.mult))
                link(p.tensor_scalar(s4[:, :, :, :], s4[:, :, :, :], 1.0 / 16, None, ALU.mult))
                link(p.tensor_scalar(s2[:, :, :, :], s2[:, :, :, :], 1.0 / 4, None, ALU.mult))
                for g in range(2):
                    t = s4[:, g, :, :].rearrange("p r (a w) -> p r a w", w=2)
                    link(p.tensor_tensor(t, t, s8[:, g, :].rearrange("p (o a i) -> p o a i", o=1, i=1).broadcast_to([G, 2, 7, 2]), ALU.add))
                for g in range(2):
                    for w in range(2):
                        t = s2[:, g, :, w::2].rearrange("p (a r) w -> p a r w", r=2)
                        link(p.tensor_tensor(t, t, s4[:, g, :, :].rearrange("p a (o w) -> p a o w", o=1).broadcast_to([G, 2, 2, 14]), ALU.add))
                for g in range(2):
                    for r in range(2):
                        t = at[o][:, g, 1 + r:9:2, 1:1 + W].rearrange("p h (a w) -> p h a w", w=2)
                        link(p.tensor_tensor(t, t, s2[:, g, :, :].rearrange("p h (w o) -> p h w o", o=1).broadcast_to([G, 4, 28, 2]), ALU.subtract))
                if c == 0:
                    link(p.memset(at[o][:, :, 0, :], 0.0))
                else:
                    link(p.tensor_copy(at[o][:, :, 0, :], at[PLACE[c - 1]][:, :, 8, :]))
                    link(p.tensor_copy(at[PLACE[c - 1]][:, :, 9, :], at[o][:, :, 1, :]))
                if c == NCH - 1:
                    link(p.memset(at[o][:, :, 9, :], 0.0))
                p.sem_inc(high_ready, 1)

            def halo(b, c):
                q = NCH * b + c
                o = PLACE[c]
                p.wait_ge(affine2, q + 1)
                p.sem_inc(tick, 1)
                if c == 0:
                    p.memset(zt[o][:, :, 0, :], 0.0)
                else:
                    p.tensor_copy(zt[o][:, :, 0, :], zt[PLACE[c - 1]][:, :, 8, :])
                    p.tensor_copy(zt[PLACE[c - 1]][:, :, 9, :], zt[o][:, :, 1, :])
                if c == NCH - 1:
                    p.memset(zt[o][:, :, 9, :], 0.0)
                p.drain().then_inc(halo_ready, 1)

            def step(b, k):
                if chunk(b, k, 1):
                    high(*chunk(b, k, 1))
                if chunk(b, k, 4):
                    halo(*chunk(b, k, 4))
            pipeline(p, step, LAG)

        @block.tensor
        def _(pe):
            pe.wait_ge(par_loaded, 16 * 13)
            pe.wait_ge(cleared, 4 + 2)
            for m in range(8):
                for g in range(2):
                    mm = pe.matmul(pM[:, m:m + 1], w1o[:, g, G * m:G * m + G], nb[:, g:g + 1], start=(g == 0), stop=(g == 1))
            mm.then_inc(bias_sum, 1)
            pe.wait_ge(folded, 3)

            def moment(bank, weights, src, n, done):
                for g in range(n):
                    mm = pe.matmul(bank[:, 0:CH], weights[:, :], src[:, g, :], start=(g == 0), stop=(g == n - 1))
                mm.then_inc(done, 1)

            def conv(b, c, g):
                q = NCH * b + c
                if g == 0:
                    pe.wait_ge(high_ready, q + 2 if c + 1 < NCH else q + 1)
                pe.wait_ge(sig_done, 2 * q + g - (1 if g else 0))
                for k in range(9):
                    dy, dx = divmod(k, 3)
                    mm = pe.matmul(pC[g][:, 0:CH], diag[:, g, k, :], at[PLACE[c]][:, g, dy:dy + 8, dx:dx + W], start=(k == 0), stop=(k == 8))
                mm.then_inc(conv_done, 1)

            def expand(qm, m0):
                if m0 == 0:
                    pe.wait_ge(normed1, qm + 1)
                for m in range(m0, m0 + 4):
                    pe.wait_ge(gelu_done, 8 * qm + (m - 1 if m >= 2 else 0))
                    for g in range(2):
                        mm = pe.matmul(p1[m % 2][:, 0:CH], w1[:, g, G * m:G * m + G], xn[:, g, :], start=(g == 0), stop=(g == 1))
                    mm.then_inc(hidden, 1)

            def step(b, k):
                on1, on2, onm, on3 = (chunk(b, k, lag) for lag in (2, 3, 4, LAG))
                b1, c1 = on1 or (0, 0)
                b2, c2 = on2 or (0, 0)
                bm, cm = onm or (0, 0)
                b3, c3 = on3 or (0, 0)
                q1, q2, qm, q3 = NCH * b1 + c1, NCH * b2 + c2, NCH * bm + cm, NCH * b3 + c3
                if onm:
                    expand(qm, 0)
                if on2:
                    pe.wait_ge(x1_ready, 2 * q2 + 2)
                    pe.wait_ge(centred2, q2 - 1 if onm else 0)
                    moment(pM, m192, x1[c2], 2, mean1)
                if onm:
                    expand(qm, 4)
                if on1:
                    conv(b1, c1, 0)
                if on2:
                    pe.wait_ge(squared1, q2 + 1)
                    pe.wait_ge(std2, q2 - 1 if onm else 0)
                    moment(pV, m192, sq, 2, var1)
                if onm:
                    pe.wait_ge(gelu_done, 8 * qm + 8)
                    pe.wait_ge(centred1, q2 + 1 if on2 else qm + 1)
                    moment(pM, m384, z2, 4, mean2)
                if on1:
                    conv(b1, c1, 1)
                if onm:
                    pe.wait_ge(squared2, qm + 1)
                    pe.wait_ge(std1, q2 + 1 if on2 else qm + 1)
                    moment(pV, m384, sq2, 4, var2)
                if on3:
                    pe.wait_ge(gated, q3 + 1)
                    pe.wait_ge(finished, 2 * q3)
                    for m in range(2):
                        for g in range(4):
                            mm = pe.matmul(p2[m][:, 0:CH], w2[:, g, G * m:G * m + G], zc[:, g, :], start=(g == 0), stop=(g == 3))
                        mm.then_inc(mixed, 1)
            pipeline(pe, step, LAG)

        @block.scalar
        def _(a):
            a.wait_ge(par_loaded, 16 * 13)
            a.wait_ge(folded, 3)
            a.wait_ge(cleared, 4 + 2)
            def step(b, k):
                on1, on2, onm, on3 = (chunk(b, k, lag) for lag in (2, 3, 4, LAG))
                b1, c1 = on1 or (0, 0)
                b2, c2 = on2 or (0, 0)
                bm, cm = onm or (0, 0)
                b3, c3 = on3 or (0, 0)
                q1, q2, qm, q3 = NCH * b1 + c1, NCH * b2 + c2, NCH * bm + cm, NCH * b3 + c3
                if chunk(b, k, 1):
                    b0, c0 = chunk(b, k, 1)
                    o = PLACE[c0]
                    a.wait_ge(in_loaded[o], 48 * (turns(b0, c0) + 1))
                    a.wait_ge(conv_done, before(b0, c0, 3, 2))
                    a.activation(at[o][:, :, 1:9, 1:1 + W], pin[o][:, :, :, 3:3 + W], ACT.Copy, scale=3.0).then_inc(tripled, 1)
                if onm:
                    for m in range(8):
                        a.wait_ge(hidden, 8 * qm + m + 1)
                        if m == 0:
                            a.wait_ge(gated, before(bm, cm, 3))
                            a.wait_ge(normed2, qm)
                        dst = z1[PLACE[cm]][:, m, :] if m < 4 else z2[:, m - 4, :]
                        a.activation(dst, p1[m % 2][:, 0:CH], ACT.Gelu, bias=b1v[:, m:m + 1]).then_inc(gelu_done, 1)
                if on2:
                    a.wait_ge(centred1, q2 + 1)
                    a.activation(sq[:, :, :], ce[:, :, :], ACT.Square).then_inc(squared1, 1)
                    a.wait_ge(var1, q2 + 1)
                    a.wait_ge(normed1, q2)
                    a.activation(rs[:, :], pV[:, 0:CH], ACT.Sqrt, bias=EPS).then_inc(std1, 1)
                if onm:
                    a.wait_ge(centred2, qm + 1)
                    a.activation(sq2[:, :, :], z2[:, :, :], ACT.Square).then_inc(squared2, 1)
                    a.wait_ge(var2, qm + 1)
                    a.activation(rs2[:, :], pV[:, 0:CH], ACT.Sqrt, bias=EPS).then_inc(std2, 1)
                if on1:
                    a.wait_ge(x1_ready, 2 * q1)
                    for g in range(2):
                        a.wait_ge(conv_done, 2 * q1 + g + 1)
                        a.activation(sig[:, g, :], pC[g][:, 0:CH], ACT.Sigmoid, bias=hb[:, g:g + 1]).then_inc(sig_done, 1)
                if onm:
                    a.wait_ge(normed2, qm + 1)
                    a.wait_ge(gated, before(bm, cm, 3))
                    for g in range(4):
                        last = a.activation(zt[PLACE[cm]][:, g, 1:9, 1:1 + W], img(z2[:, g, :]), ACT.Identity,
                                            bias=sgb[:, g:g + 1], scale=sgg[:, g:g + 1])
                    last.then_inc(affine2, 1)
            pipeline(a, step, LAG)

        @block.vector
        def _(v):
            v.memset(m192[:, :], 1.0 / C).then_inc(cleared, 1)
            v.memset(m384[:, :], 1.0 / (2 * C)).then_inc(cleared, 1)
            v.wait_ge(par_loaded, 16 * 13)
            for g in range(2):
                for k in range(9):
                    v.tensor_scalar(diag[:, g, k, :], idf[0:G, 0:G], hw[:, g, k:k + 1], None, ALU.mult)
                v.tensor_scalar(w1[:, g, :], w1o[:, g, :], ng[:, g:g + 1], None, ALU.mult).then_inc(folded, 1)
            v.wait_ge(bias_sum, 1)
            v.tensor_tensor(b1v[:, :], pM[:, 0:8], b1o[:, :], ALU.add).then_inc(folded, 1)

            def depthwise(b, c, g0):
                q = NCH * b + c
                base = 36 * q + 9 * g0
                for k in range(9):
                    dy, dx = divmod(k, 3)
                    for i in range(2):
                        g = g0 + i
                        src = zt[PLACE[c]][:, g, dy:dy + 8, dx:dx + W]
                        dst = img(zc[:, g, :])
                        if k == 0:
                            v.tensor_scalar(dst, src, gw[:, g, 0:1], gb[:, g:g + 1], ALU.mult, ALU.add).then_inc(dw_step, 1)
                        else:
                            v.wait_ge(dw_step, base + 2 * (k - 1) + i + 1)
                            v.scalar_tensor_tensor(dst, src, gw[:, g, k:k + 1], dst, ALU.mult, ALU.add).then_inc(dw_step, 1)

            def norm(ready, done, rdone, q, rs_, src, dst, n):
                v.wait_ge(ready, q + 1)
                v.reciprocal(rs_[:, :], rs_[:, :]).then_inc(rdone, 1)
                v.wait_ge(rdone, q + 1)
                v.tensor_tensor(dst[:, :, :], src[:, :, :], spread(rs_[:, :], n), ALU.mult).then_inc(done, 1)

            def step(b, k):
                on1, on2, onm, on3 = (chunk(b, k, lag) for lag in (2, 3, 4, LAG))
                b1, c1 = on1 or (0, 0)
                b2, c2 = on2 or (0, 0)
                bm, cm = onm or (0, 0)
                b3, c3 = on3 or (0, 0)
                q1, q2, qm, q3 = NCH * b1 + c1, NCH * b2 + c2, NCH * bm + cm, NCH * b3 + c3
                if on3:
                    v.wait_ge(halo_ready, q3 + 2 if c3 + 1 < NCH else q3 + 1)
                    v.wait_ge(mixed, 2 * q3)
                    depthwise(b3, c3, 0)
                if on2:
                    v.wait_ge(mean1, q2 + 1)
                    v.wait_ge(squared1, q2)
                    v.tensor_tensor(ce[:, :, :], x1[c2][:, :, :], spread(pM[:, 0:CH], 2), ALU.subtract).then_inc(centred1, 1)
                if on3:
                    depthwise(b3, c3, 2)
                    v.wait_ge(dw_step, 36 * q3 + 36)
                    v.tensor_tensor(zc[:, :, :], zc[:, :, :], z1[PLACE[c3]][:, :, :], ALU.mult).then_inc(gated, 1)
                if onm:
                    v.wait_ge(mean2, qm + 1)
                    v.wait_ge(squared2, qm)
                    v.tensor_tensor(z2[:, :, :], z2[:, :, :], spread(pM[:, 0:CH], 4), ALU.subtract).then_inc(centred2, 1)
                if on2:
                    v.wait_ge(hidden, 8 * q2)
                    norm(std1, normed1, rstd1, q2, rs, ce, xn, 2)
                if onm:
                    norm(std2, normed2, rstd2, qm, rs2, z2, z2, 4)
                if on1:
                    o = PLACE[c1]
                    v.wait_ge(in_loaded[o], 48 * (turns(b1, c1) + 1))
                    for g in range(2):
                        v.wait_ge(sig_done, 2 * q1 + g + 1)
                        v.tensor_tensor(img(sig[:, g, :]), img(sig[:, g, :]), pin[o][:, g, :, 3:3 + W], ALU.mult).then_inc(sig_mul, 1)
                    for g in range(2):
                        v.wait_ge(sig_mul, 2 * q1 + g + 1)
                        v.scalar_tensor_tensor(img(x1[c1][:, g, :]), xin[o][:, g, :, 3:3 + W], gt[o][:, g:g + 1], img(sig[:, g, :]),
                                               ALU.mult, ALU.add).then_inc(x1_ready, 1)
                if on3:
                    o = c3 % 2
                    v.wait_ge(stored[o], 16 * ((3 if o else 4) * b3 + c3 // 2))
                    for m in range(2):
                        v.wait_ge(mixed, 2 * q3 + m + 1)
                        v.scalar_tensor_tensor(out[o][:, m, :], p2[m][:, 0:CH], b2v[:, m:m + 1], x1[c3][:, m, :],
                                               ALU.add, ALU.add).then_inc(finished, 1)
            pipeline(v, step, LAG)


def scan_inputs(nc, x3, ln_w, ln_b, in_wT, conv_w, conv_b, dts_wT, bc_wT, xc, zs, dts, bcs):
    with ExitStack() as ctx:
        sb = lambda name, shape, dt=F32: ctx.enter_context(nc.sbuf_tensor(name, shape, dt))
        pt = lambda name: ctx.enter_context(nc.psum_tensor(name, [G, 512], F32))
        sem = ctx.enter_context(stage_semaphores(nc))
        wo = sb("f_wo", [G, 2, 2 * C])
        w = sb("f_w", [G, 2, 2 * C])
        wd = sb("f_wd", [G, 2, KD * RANK])
        wb = sb("f_wb", [G, 2, NBC])
        wb3 = sb("f_wb3", [G, 2, 3, NBC])
        cw = sb("f_cw", [G, 2, 9])
        cb = sb("f_cb", [G, 2])
        lg = sb("f_lg", [G, 2])
        lb = sb("f_lb", [G, 2])
        bi = sb("f_bi", [G, 4])
        m192 = sb("f_m192", [G, G])
        xin = [sb(f"f_xin{i}", [G, 2, CH]) for i in range(4)]
        ce = sb("f_ce", [G, 2, CH])
        sq = sb("f_sq", [G, 2, CH])
        rs = sb("f_rs", [G, CH])
        xn = sb("f_xn", [G, 2, CH])
        ct = [sb(f"f_ct{i}", [G, 2, 10, AW]) for i in range(4)]
        cv = sb("f_cv", [G, 2, CH])
        xo = [sb(f"f_xo{i}", [G, 2, CH]) for i in range(4)]
        zo = [sb(f"f_zo{i}", [G, 2, CH]) for i in range(4)]
        do = [sb(f"f_do{i}", [KD * RANK, CH]) for i in range(4)]
        hi = sb("f_hi", [G, CH], BF16)
        r1 = sb("f_r1", [G, CH])
        mid = sb("f_mid", [G, CH], BF16)
        bo = [sb(f"f_bo{i}", [G, CH], BF16) for i in range(4)]
        pM, pV, pD, pB = pt("f_pm"), pt("f_pv"), pt("f_pd"), pt("f_pb")
        pI = [pt(f"f_pi{i}") for i in range(4)]
        par_loaded = sem("f_par_loaded")
        consts = sem("f_consts")
        bias_sum = sem("f_bias_sum")
        folded = sem("f_folded")
        in_loaded = [sem(f"f_in_loaded{i}") for i in range(4)]
        mean_done = sem("f_mean")
        centred = sem("f_centred")
        squared = sem("f_squared")
        var_done = sem("f_var")
        std_done = sem("f_std")
        rstd_done = sem("f_rstd")
        normed = sem("f_normed")
        projected = sem("f_projected")
        xc_evac = sem("f_xc_evac")
        z_evac = sem("f_z_evac")
        halo_ready = sem("f_halo_ready")
        conv_step = sem("f_conv_step")
        silu_done = sem("f_silu_done")
        dts_done = sem("f_dts_done")
        bc_done = sem("f_bc_done")
        dts_evac = sem("f_dts_evac")
        hi_done = sem("f_hi_done")
        rest_done = sem("f_rest_done")
        mid_done = sem("f_mid_done")
        lo_done = sem("f_lo_done")
        z_stored = [sem(f"f_z_stored{i}") for i in range(4)]
        x_stored = [sem(f"f_x_stored{i}") for i in range(4)]
        tick = sem("f_tick")
        block = ctx.enter_context(nc.Block())
        v3 = lambda t: t.rearrange("(b g p) n -> b p g n", b=B, g=2)


        def img(ap):
            return ap.rearrange("p (h w) -> p h w", w=W)

        @block.sync
        def _(sp):
            with nc.allow_non_contiguous_dma(reason="small vectors, once"):
                sp.dma_start(wo[:, :, :], in_wT.rearrange("(g p) o -> p g o", p=G)).then_inc(par_loaded, 16)
                sp.dma_start(wd[:, :, :], dts_wT.rearrange("(g p) o -> p g o", p=G)).then_inc(par_loaded, 16)
                sp.dma_start(wb[:, :, :], bc_wT.rearrange("(g p) o -> p g o", p=G)).then_inc(par_loaded, 16)
                sp.dma_start(cw[:, :, :], conv_w.rearrange("(g p) k -> p g k", p=G)).then_inc(par_loaded, 16)
                for dst, src in ((cb, conv_b), (lg, ln_w), (lb, ln_b)):
                    sp.dma_start(dst[:, :], src.rearrange("(g p) -> p g", p=G)).then_inc(par_loaded, 16)

            def step(b, k):
                now, expanded, finished = chunk(b, k, 0), chunk(b, k, 2), chunk(b, k, SLAG)
                if now:
                    b, c = now
                    sp.wait_ge(centred, before(b, c, 3))
                    sp.sem_inc(tick, 1)
                    sp.dma_start(xin[PLACE[c]][:, :, :], v3(x3)[b, :, :, c * CH:(c + 1) * CH]).then_inc(in_loaded[PLACE[c]], 16)
                if expanded:
                    b, c = expanded
                    o = PLACE[c]
                    sp.wait_ge(z_evac, NCH * b + c + 1)
                    sp.sem_inc(tick, 1)
                    sp.dma_start(v3(zs)[b, :, :, c * CH:(c + 1) * CH], zo[o][:, :, :]).then_inc(z_stored[o], 16)
                if finished:
                    b, c = finished
                    o = PLACE[c]
                    sl = slice(c * CH, (c + 1) * CH)
                    sp.wait_ge(lo_done, NCH * b + c + 1)
                    sp.sem_inc(tick, 1)
                    sp.wait_ge(dts_evac, NCH * b + c + 1)
                    sp.sem_inc(tick, 1)
                    sp.dma_start(v3(xc)[b, :, :, sl], xo[o][:, :, :]).then_inc(x_stored[o], 16)
                    sp.dma_start(dts[b, :, sl], do[o][:, :]).then_inc(x_stored[o], 16)
                    sp.dma_start(bcs[b, :, sl], bo[o][:, :]).then_inc(x_stored[o], 16)
            pipeline(sp, step, SLAG)
            for o in range(4):
                sp.wait_ge(z_stored[o], 16 * USES[o] * B)
                sp.wait_ge(x_stored[o], 48 * USES[o] * B)

        @block.gpsimd
        def _(p):
            for i in range(4):
                p.memset(ct[i][:, :, :, :], 0.0).then_inc(consts, 1)
            def step(b, k):
                if chunk(b, k, 2):
                    b, c = chunk(b, k, 2)
                    o = PLACE[c]
                    p.wait_ge(xc_evac, NCH * b + c + 1)
                    p.sem_inc(tick, 1)
                    if c == 0:
                        p.memset(ct[o][:, :, 0, :], 0.0)
                    else:
                        p.tensor_copy(ct[o][:, :, 0, :], ct[PLACE[c - 1]][:, :, 8, :])
                        p.tensor_copy(ct[PLACE[c - 1]][:, :, 9, :], ct[o][:, :, 1, :])
                    if c == NCH - 1:
                        p.memset(ct[o][:, :, 9, :], 0.0)
                    p.drain().then_inc(halo_ready, 1)
            pipeline(p, step, SLAG)

        @block.tensor
        def _(pe):
            pe.wait_ge(par_loaded, 16 * 7)
            pe.wait_ge(consts, 4 + 1)
            for m in range(4):
                for g in range(2):
                    mm = pe.matmul(pD[:, m:m + 1], wo[:, g, G * m:G * m + G], lb[:, g:g + 1], start=(g == 0), stop=(g == 1))
            mm.then_inc(bias_sum, 1)
            pe.wait_ge(folded, 3)

            def moment(bank, src, done):
                for g in range(2):
                    mm = pe.matmul(bank[:, 0:CH], m192[:, :], src[:, g, :], start=(g == 0), stop=(g == 1))
                mm.then_inc(done, 1)

            def step(b, k):
                on0, on1, on4 = (chunk(b, k, lag) for lag in (1, 2, SLAG))
                if on0:
                    b0, c0 = on0
                    q = NCH * b0 + c0
                    pe.wait_ge(in_loaded[PLACE[c0]], 16 * (turns(b0, c0) + 1))
                    pe.wait_ge(centred, q)
                    moment(pM, xin[PLACE[c0]], mean_done)
                if on4:
                    b4, c4 = on4
                    q4, o = NCH * b4 + c4, PLACE[c4]
                    pe.wait_ge(silu_done, q4 + 1)
                    pe.wait_ge(dts_evac, q4)
                    for g in range(2):
                        mm = pe.matmul(pD[0:KD * RANK, 0:CH], wd[:, g, :], xo[o][:, g, :], start=(g == 0), stop=(g == 1))
                    mm.then_inc(dts_done, 1)
                    pe.wait_ge(rest_done, q4)
                    for g in range(2):
                        mm = pe.matmul(pB[:, 0:CH], wb3[:, g, :, :].rearrange("p a b -> p (a b)"), xo[o][:, g, :], start=(g == 0), stop=(g == 1))
                    mm.then_inc(bc_done, 1)
                if on1:
                    b1, c1 = on1
                    q1 = NCH * b1 + c1
                    pe.wait_ge(normed, q1 + 1)
                    pe.wait_ge(xc_evac, q1)
                    pe.wait_ge(z_evac, q1)
                    for m in range(2):
                        for g in range(2):
                            mm = pe.matmul(pI[m][:, 0:CH], w[:, g, G * m:G * m + G], xn[:, g, :], start=(g == 0), stop=(g == 1))
                        mm.then_inc(projected, 1)
                if on0:
                    pe.wait_ge(squared, q + 1)
                    pe.wait_ge(std_done, q)
                    moment(pV, sq, var_done)
                if on1:
                    for m in range(2, 4):
                        for g in range(2):
                            mm = pe.matmul(pI[m][:, 0:CH], w[:, g, G * m:G * m + G], xn[:, g, :], start=(g == 0), stop=(g == 1))
                        mm.then_inc(projected, 1)
            pipeline(pe, step, SLAG)

        @block.scalar
        def _(a):
            a.wait_ge(par_loaded, 16 * 7)
            a.wait_ge(folded, 3)
            a.wait_ge(consts, 4 + 1)
            def step(b, k):
                on0, on1, on3, on4 = (chunk(b, k, lag) for lag in (1, 2, 4, SLAG))
                if on4:
                    b4, c4 = on4
                    q4, o = NCH * b4 + c4, PLACE[c4]
                    a.wait_ge(x_stored[o], 48 * turns(b4, c4))
                    a.wait_ge(dts_done, q4 + 1)
                    a.activation(do[o][:, :], pD[0:KD * RANK, 0:CH], ACT.Copy).then_inc(dts_evac, 1)
                    a.wait_ge(bc_done, q4 + 1)
                    a.wait_ge(lo_done, q4)
                    a.activation(hi[:, :], pB[:, 0:CH], ACT.Copy).then_inc(hi_done, 1)
                if on1:
                    b1, c1 = on1
                    q1, o = NCH * b1 + c1, PLACE[c1]
                    a.wait_ge(conv_step, before(b1, c1, 3, 18))
                    for g in range(2):
                        a.wait_ge(projected, 4 * q1 + g + 1)
                        last = a.activation(ct[o][:, g, 1:9, 1:1 + W], img(pI[g][:, 0:CH]), ACT.Identity, bias=bi[:, g:g + 1])
                    last.then_inc(xc_evac, 1)
                if on4:
                    a.wait_ge(rest_done, q4 + 1)
                    a.activation(mid[:, :], r1[:, :], ACT.Copy).then_inc(mid_done, 1)
                if on0:
                    b0, c0 = on0
                    q = NCH * b0 + c0
                    a.wait_ge(centred, q + 1)
                    a.activation(sq[:, :, :], ce[:, :, :], ACT.Square).then_inc(squared, 1)
                    a.wait_ge(var_done, q + 1)
                    a.wait_ge(normed, q)
                    a.activation(rs[:, :], pV[:, 0:CH], ACT.Sqrt, bias=EPS).then_inc(std_done, 1)
                if on1:
                    o = PLACE[c1]
                    a.wait_ge(z_stored[o], 16 * turns(b1, c1))
                    for g in range(2):
                        a.wait_ge(projected, 4 * q1 + g + 3)
                        last = a.activation(zo[o][:, g, :], pI[2 + g][:, 0:CH], ACT.Silu, bias=bi[:, 2 + g:3 + g])
                    last.then_inc(z_evac, 1)
                if on3:
                    b3, c3 = on3
                    q3, o = NCH * b3 + c3, PLACE[c3]
                    a.wait_ge(conv_step, 18 * q3 + 18)
                    a.wait_ge(x_stored[o], 48 * turns(b3, c3))
                    a.activation(xo[o][:, :, :], cv[:, :, :], ACT.Silu).then_inc(silu_done, 1)
            pipeline(a, step, SLAG)

        @block.vector
        def _(v):
            v.memset(m192[:, :], 1.0 / C).then_inc(consts, 1)
            v.wait_ge(par_loaded, 16 * 7)
            for g in range(2):
                for i in range(3):
                    v.tensor_copy(wb3[:, g, i, :], wb[:, g, :])
                v.tensor_scalar(w[:, g, :], wo[:, g, :], lg[:, g:g + 1], None, ALU.mult).then_inc(folded, 1)
            v.wait_ge(bias_sum, 1)
            v.tensor_copy(bi[:, :], pD[:, 0:4]).then_inc(folded, 1)
            def step(b, k):
                on0, on3, on4 = (chunk(b, k, lag) for lag in (1, 4, SLAG))
                if on3:
                    b3, c3 = on3
                    q3 = NCH * b3 + c3
                    v.wait_ge(halo_ready, q3 + 2 if c3 + 1 < NCH else q3 + 1)
                    v.wait_ge(silu_done, q3)

                def taps(first, last):
                    for t in range(first, last):
                        dy, dx = divmod(t, 3)
                        for g in range(2):
                            src = ct[PLACE[c3]][:, g, dy:dy + 8, dx:dx + W]
                            dst = img(cv[:, g, :])
                            if t == 0:
                                v.tensor_scalar(dst, src, cw[:, g, 0:1], cb[:, g:g + 1], ALU.mult, ALU.add).then_inc(conv_step, 1)
                            else:
                                v.wait_ge(conv_step, 18 * q3 + 2 * (t - 1) + g + 1)
                                v.scalar_tensor_tensor(dst, src, cw[:, g, t:t + 1], dst, ALU.mult, ALU.add).then_inc(conv_step, 1)
                if on3:
                    taps(0, 3)
                if on0:
                    b0, c0 = on0
                    q, o = NCH * b0 + c0, PLACE[c0]
                    v.wait_ge(mean_done, q + 1)
                    v.wait_ge(squared, q)
                    v.wait_ge(normed, q)
                    v.tensor_tensor(ce[:, :, :], xin[o][:, :, :],
                                    pM[:, 0:CH].rearrange("p (o m) -> p o m", o=1).broadcast_to([G, 2, CH]), ALU.subtract).then_inc(centred, 1)
                if on4:
                    b4, c4 = on4
                    q4, o = NCH * b4 + c4, PLACE[c4]
                    v.wait_ge(hi_done, q4 + 1)
                    v.wait_ge(mid_done, q4)
                    v.tensor_tensor(r1[:, :], pB[:, 0:CH], hi[:, :], ALU.subtract).then_inc(rest_done, 1)
                if on3:
                    taps(3, 9)
                if on4:
                    v.wait_ge(x_stored[PLACE[c4]], 48 * turns(b4, c4))
                    o = PLACE[c4]
                    v.tensor_copy(bo[o][0:32, :], hi[0:32, :])
                    v.wait_ge(mid_done, q4 + 1)
                    v.tensor_copy(bo[o][32:64, :], mid[32:64, :])
                    v.tensor_tensor(bo[o][64:96, :], r1[64:96, :], mid[64:96, :], ALU.subtract).then_inc(lo_done, 1)
                if on0:
                    v.wait_ge(std_done, q + 1)
                    v.reciprocal(rs[:, :], rs[:, :]).then_inc(rstd_done, 1)
                    v.wait_ge(rstd_done, q + 1)
                    v.wait_ge(projected, 4 * q)
                    v.tensor_tensor(xn[:, :, :], ce[:, :, :],
                                    rs[:, :].rearrange("p (o m) -> p o m", o=1).broadcast_to([G, 2, CH]), ALU.mult).then_inc(normed, 1)
            pipeline(v, step, SLAG)


def scan_outputs(nc, x3, ys, zs, on_w, on_b, out_wT, out):
    with ExitStack() as ctx:
        sb = lambda name, shape, dt=F32: ctx.enter_context(nc.sbuf_tensor(name, shape, dt))
        pt = lambda name: ctx.enter_context(nc.psum_tensor(name, [G, 512], F32))
        sem = ctx.enter_context(stage_semaphores(nc))
        w = sb("h_w", [G, 2, C])
        og = sb("h_og", [G, 2])
        ob = sb("h_ob", [G, 2])
        m192 = sb("h_m192", [G, G])
        yin = [sb(f"h_yin{i}", [G, 2, CH]) for i in range(4)]
        zin = [sb(f"h_zin{i}", [G, 2, CH]) for i in range(NCH)]
        xin = [sb(f"h_xin{i}", [G, 2, CH]) for i in range(NCH)]
        ce = [sb(f"h_ce{i}", [G, 2, CH]) for i in range(4)]
        sq = sb("h_sq", [G, 2, CH])
        rs = [sb(f"h_rs{i}", [G, CH]) for i in range(4)]
        yn = [sb(f"h_yn{i}", [G, 2, CH]) for i in range(4)]
        ot = [sb(f"h_ot{i}", [G, 2, CH]) for i in range(4)]
        pM = pt("h_pm")
        pV = pt("h_pv")
        pO = [pt(f"h_po{i}") for i in range(2)]
        par_loaded = sem("h_par_loaded")
        consts = sem("h_consts")
        y_loaded = [sem(f"h_y_loaded{i}") for i in range(4)]
        zx_loaded = [sem(f"h_zx_loaded{i}") for i in range(NCH)]
        mean_done = sem("h_mean")
        centred = sem("h_centred")
        squared = sem("h_squared")
        var_done = sem("h_var")
        std_done = sem("h_std")
        rstd_done = sem("h_rstd")
        normed = sem("h_normed")
        affine = sem("h_affine")
        gated = sem("h_gated")
        projected = sem("h_projected")
        finished = sem("h_finished")
        stored = [sem(f"h_stored{i}") for i in range(4)]
        tick = sem("h_tick")
        block = ctx.enter_context(nc.Block())
        v3 = lambda t: t.rearrange("(b g p) n -> b p g n", b=B, g=2)
        xo = out.rearrange("b (g p) h w -> b p g (h w)", g=2)
        LAGS = 4

        @block.sync
        def _(sp):
            with nc.allow_non_contiguous_dma(reason="small vectors, once"):
                sp.dma_start(w[:, :, :], out_wT.rearrange("(g p) o -> p g o", p=G)).then_inc(par_loaded, 16)
                sp.dma_start(og[:, :], on_w.rearrange("(g p) -> p g", p=G)).then_inc(par_loaded, 16)
                sp.dma_start(ob[:, :], on_b.rearrange("(g p) -> p g", p=G)).then_inc(par_loaded, 16)

            def step(b, k):
                if chunk(b, k, 0):
                    o = PLACE[k]
                    sl = slice(k * CH, (k + 1) * CH)
                    sp.wait_ge(centred, before(b, k, 3))
                    sp.sem_inc(tick, 1)
                    sp.dma_start(yin[o][:, :, :], v3(ys)[b, :, :, sl]).then_inc(y_loaded[o], 16)
                    sp.wait_ge(finished, before(b, k, NCH, 2))
                    sp.sem_inc(tick, 1)
                    sp.dma_start(zin[k][:, :, :], v3(zs)[b, :, :, sl]).then_inc(zx_loaded[k], 16)
                    sp.dma_start(xin[k][:, :, :], v3(x3)[b, :, :, sl]).then_inc(zx_loaded[k], 16)
            pipeline(sp, step, 0)

        @block.gpsimd
        def _(p):
            def step(b, k):
                if chunk(b, k, LAGS):
                    b, c = chunk(b, k, LAGS)
                    p.wait_ge(finished, 2 * (NCH * b + c + 1))
                    p.sem_inc(tick, 1)
                    p.dma_start(xo[b, :, :, c * CH:(c + 1) * CH], ot[PLACE[c]][:, :, :]).then_inc(stored[PLACE[c]], 16)
            pipeline(p, step, LAGS)
            for o in range(4):
                p.wait_ge(stored[o], 16 * USES[o] * B)

        @block.tensor
        def _(pe):
            pe.wait_ge(par_loaded, 48)
            pe.wait_ge(consts, 1)

            def step(b, k):
                on1, on2, on3 = (chunk(b, k, lag) for lag in (1, 3, LAGS))
                if on1:
                    b1, c1 = on1
                    q1, o = NCH * b1 + c1, PLACE[c1]
                    pe.wait_ge(y_loaded[o], 16 * (turns(b1, c1) + 1))
                    pe.wait_ge(centred, before(b1, c1, 1))
                    for g in range(2):
                        mm = pe.matmul(pM[:, 0:CH], m192[:, :], yin[o][:, g, :], start=(g == 0), stop=(g == 1))
                    mm.then_inc(mean_done, 1)
                if on3:
                    b3, c3 = on3
                    q3, o = NCH * b3 + c3, PLACE[c3]
                    pe.wait_ge(gated, q3 + 1)
                    pe.wait_ge(finished, 2 * q3)
                    for m in range(2):
                        for g in range(2):
                            mm = pe.matmul(pO[m][:, 0:CH], w[:, g, G * m:G * m + G], yn[o][:, g, :], start=(g == 0), stop=(g == 1))
                        mm.then_inc(projected, 1)
                if on1:
                    pe.wait_ge(squared, q1 + 1)
                    pe.wait_ge(std_done, q1)
                    for g in range(2):
                        mm = pe.matmul(pV[:, 0:CH], m192[:, :], sq[:, g, :], start=(g == 0), stop=(g == 1))
                    mm.then_inc(var_done, 1)
            pipeline(pe, step, LAGS)

        @block.scalar
        def _(a):
            a.wait_ge(par_loaded, 48)

            def step(b, k):
                on1, on2 = chunk(b, k, 1), chunk(b, k, 3)
                if on2:
                    b2, c2 = on2
                    o = PLACE[c2]
                    a.wait_ge(normed, NCH * b2 + c2 + 1)
                    for g in range(2):
                        last = a.activation(yn[o][:, g, :], yn[o][:, g, :], ACT.Identity, bias=ob[:, g:g + 1], scale=og[:, g:g + 1])
                    last.then_inc(affine, 1)
                if on1:
                    b1, c1 = on1
                    q1, o = NCH * b1 + c1, PLACE[c1]
                    a.wait_ge(centred, q1 + 1)
                    a.wait_ge(var_done, q1)
                    a.activation(sq[:, :, :], ce[o][:, :, :], ACT.Square).then_inc(squared, 1)
                    a.wait_ge(var_done, q1 + 1)
                    a.wait_ge(normed, before(b1, c1, 3))
                    a.activation(rs[o][:, :], pV[:, 0:CH], ACT.Sqrt, bias=EPS).then_inc(std_done, 1)
            pipeline(a, step, LAGS)

        @block.vector
        def _(v):
            v.memset(m192[:, :], 1.0 / C).then_inc(consts, 1)
            bc = lambda t: t.rearrange("p (o m) -> p o m", o=1).broadcast_to([G, 2, CH])

            def step(b, k):
                on1, onr, on2, on3 = (chunk(b, k, lag) for lag in (1, 2, 3, LAGS))
                if onr:
                    br, cr = onr
                    qr, o = NCH * br + cr, PLACE[cr]
                    v.wait_ge(std_done, qr + 1)
                    v.reciprocal(rs[o][:, :], rs[o][:, :]).then_inc(rstd_done, 1)
                if on1:
                    b1, c1 = on1
                    q1, o = NCH * b1 + c1, PLACE[c1]
                    v.wait_ge(mean_done, q1 + 1)
                    v.wait_ge(squared, before(b1, c1, 3))
                    v.wait_ge(normed, before(b1, c1, 3))
                    v.tensor_tensor(ce[o][:, :, :], yin[o][:, :, :], bc(pM[:, 0:CH]), ALU.subtract).then_inc(centred, 1)
                if onr:
                    o = PLACE[cr]
                    v.wait_ge(rstd_done, qr + 1)
                    v.wait_ge(projected, before(br, cr, 3, 2))
                    v.tensor_tensor(yn[o][:, :, :], ce[o][:, :, :], bc(rs[o][:, :]), ALU.mult).then_inc(normed, 1)
                if on2:
                    b2, c2 = on2
                    q2, o = NCH * b2 + c2, PLACE[c2]
                    v.wait_ge(zx_loaded[c2], 32 * (b2 + 1))
                    v.wait_ge(affine, q2 + 1)
                    v.tensor_tensor(yn[o][:, :, :], yn[o][:, :, :], zin[c2][:, :, :], ALU.mult).then_inc(gated, 1)
                if on3:
                    b3, c3 = on3
                    q3, o = NCH * b3 + c3, PLACE[c3]
                    v.wait_ge(stored[o], 16 * turns(b3, c3))
                    for m in range(2):
                        v.wait_ge(projected, 2 * q3 + m + 1)
                        v.tensor_tensor(ot[o][:, m, :], pO[m][:, 0:CH], xin[c3][:, m, :], ALU.add).then_inc(finished, 1)
            pipeline(v, step, LAGS)


def scans(nc, xc, dts, bcs, dt_wT, dt_b, a_log, ds, sel, ys):
    with ExitStack() as ctx:
        sb = lambda name, shape, dt=F32: ctx.enter_context(nc.sbuf_tensor(name, shape, dt))
        pt = lambda name: ctx.enter_context(nc.psum_tensor(name, [128, 512], F32))
        sem = ctx.enter_context(stage_semaphores(nc))
        wd = sb("s_wd", [RANK, KD, C])
        db = sb("s_db", [128, 3, KD])
        al = sb("s_al", [128, 3, KD * NST])
        dsk = sb("s_dsk", [128, 3, KD])
        dsum = sb("s_dsum", [128, 3])
        selt = sb("s_sel", [G, NBC], BF16)
        bct = [sb(f"s_bct{i}", [G, N], BF16) for i in range(2)]
        dtt = [sb(f"s_dtt{i}", [RANK, 2, CH]) for i in range(SR)]
        xt = [sb(f"s_xt{i}", [128, N]) for i in range(3)]
        yt = [sb(f"s_yt{i}", [128, N]) for i in range(2)]
        dt = [sb(f"s_dt{i}", [128, N]) for i in range(2)]
        dtu = [sb(f"s_dtu{i}", [128, N]) for i in range(2)]
        tmp = sb("s_tmp", [128, N])
        da = [sb(f"s_da{i}", [128, N]) for i in range(2)]
        dbu = sb("s_dbu", [128, N])
        prod = sb("s_prod", [128, RP, CH])
        pB = [pt(f"s_pb{i}") for i in range(3)]
        pC = [pt(f"s_pc{i}") for i in range(3)]
        pD = [pt(f"s_pd{i}") for i in range(2)]
        par_loaded = sem("s_par_loaded")
        a_exp = sem("s_a_exp")
        a_ready = sem("s_a_ready")
        bc_loaded = sem("s_bc_loaded")
        x_loaded = [sem(f"s_x_loaded{i}") for i in range(3)]
        dts_loaded = [sem(f"s_dts_loaded{i}") for i in range(SR)]
        step_done = sem("s_step_done")
        step_evac = sem("s_step_evac")
        exp_taken = sem("s_exp_taken")
        log_taken = sem("s_log_taken")
        dt_ready = sem("s_dt_ready")
        dtu_ready = sem("s_dtu_ready")
        b_spread = sem("s_b_spread")
        c_spread = sem("s_c_spread")
        b_used = sem("s_b_used")
        c_used = sem("s_c_used")
        decay_ready = sem("s_decay_ready")
        scanned = sem("s_scanned")
        y_begun = sem("s_y_begun")
        y_added = sem("s_y_added")
        stored = [sem(f"s_stored{i}") for i in range(2)]
        tick = sem("s_tick")
        block = ctx.enter_context(nc.Block())
        NP2 = B // 2
        NB = NIT * NCH
        xv = xc.rearrange("(q u p) n -> q u p n", u=3, p=128)
        yv = ys.rearrange("(q u p) n -> q u p n", u=3, p=128)
        dv = dts.rearrange("(q i) (k r) n -> q k r i n", i=2, k=KD)
        bv = bcs.rearrange("(q i) r n -> q i r n", i=2)

        def chunk(t, c, k):
            if k % 2:
                return t.rearrange("p (w h) -> p h w", h=H)[:, 8 * c:8 * c + 8, :]
            return t[:, c * CH:(c + 1) * CH].rearrange("p (h w) -> p h w", w=W)

        def img(t):
            return t.rearrange("p (h w) -> p h w", w=W)

        def along(t, k):
            return t[:, ::-1] if k >= 2 else t[:, :]

        @block.sync
        def _(sp):
            with nc.allow_non_contiguous_dma(reason="small vectors, once"):
                sp.dma_start(wd[:, :, :], dt_wT.rearrange("k r d -> r k d")).then_inc(par_loaded, 16)
                sp.dma_start(db[:, :, :], dt_b.rearrange("(u p) k -> p u k", p=128)).then_inc(par_loaded, 16)
                sp.dma_start(al[:, :, :], a_log.rearrange("(u p) k -> p u k", p=128)).then_inc(par_loaded, 16)
                sp.dma_start(dsk[:, :, :], ds.rearrange("(u p) k -> p u k", p=128)).then_inc(par_loaded, 16)
                sp.dma_start(selt[:, :], sel).then_inc(par_loaded, 16)
            with sp.Fori(0, NP2) as q:
                sp.wait_ge(b_spread, NB * q)
                sp.sem_inc(tick, 1)
                sp.wait_ge(c_spread, NB * q)
                sp.sem_inc(tick, 1)
                for i in range(2):
                    sp.dma_start(bct[i][:, :], bv[q, i]).then_inc(bc_loaded, 16)
                for u in range(3):
                    sp.wait_ge(dtu_ready, NSEC * q)
                    sp.sem_inc(tick, 1)
                    sp.wait_ge(y_begun, 3 * q)
                    sp.sem_inc(tick, 1)
                    sp.dma_start(xt[u][:, :], xv[q, u]).then_inc(x_loaded[u], 16)
                for s in range(NSEC):
                    for c in range(NCH):
                        n = NCH * s + c
                        sp.wait_ge(step_done, NSEC * NCH * q + max(n - SR + 1, 0))
                        sp.sem_inc(tick, 1)
                        sp.dma_start(dtt[n % SR][:, :, :], dv[q, s % KD, :, :, c * CH:(c + 1) * CH]).then_inc(dts_loaded[n % SR], 16)

        @block.tensor
        def _(pe):
            pe.wait_ge(par_loaded, 80)

            def steps(q, s, c):
                u, k = divmod(s, KD)
                n = NCH * s + c
                pe.wait_ge(dts_loaded[n % SR], 16 * (NSEC * NCH // SR * q + n // SR + 1))
                pe.wait_ge(step_evac, NSEC * NCH * q + max(n - 1, 0))
                pe.sem_inc(tick, 1)
                for i, d0, p0, m in PIECES[u]:
                    mm = pe.matmul(pD[n % 2][p0:p0 + m, 0:CH], wd[:, k, d0:d0 + m], dtt[n % SR][:, i, :], start=True, stop=True)
                mm.then_inc(step_done, 1)

            def rows(q, e, banks, used, done, bc):
                s, n = divmod(e, NST)
                u, k = divmod(s, KD)
                row = (2 * k + bc) * NST + n
                for c in range(NCH):
                    j = NCH * e + c
                    pe.wait_ge(used, NB * q + max(j - 2, 0))
                    pe.sem_inc(tick, 1)
                    for i, d0, p0, m in PIECES[u]:
                        mm = pe.matmul(banks[j % 3][p0:p0 + m, 0:CH], selt[:, row:row + 1].broadcast_to([G, m]),
                                       bct[i][:, c * CH:(c + 1) * CH], start=True, stop=True)
                    mm.then_inc(done, 1)
                    if s + 1 < NSEC and c == 2:
                        for m in AMONG.get((n, bc), ()):
                            steps(q, s + 1, m)

            with pe.Fori(0, NP2) as q:
                for c in range(NCH):
                    steps(q, 0, c)
                pe.wait_ge(bc_loaded, 32 * (q + 1))
                for e in range(NIT):
                    rows(q, e, pB, b_used, b_spread, 0)
                    rows(q, e, pC, c_used, c_spread, 1)

        @block.scalar
        def _(a):
            a.wait_ge(par_loaded, 80)
            a.activation(al[:, :, :], al[:, :, :], ACT.Exp).then_inc(a_exp, 1)
            a.wait_ge(a_ready, 2)

            def begin(q, u):
                a.wait_ge(x_loaded[u], 16 * (q + 1))
                a.wait_ge(stored[u % 2], 16 * ((1 if u % 2 else 2) * q + u // 2))
                a.activation(yt[u % 2][:, :], xt[u][:, :], ACT.Copy, scale=dsum[:, u:u + 1]).then_inc(y_begun, 1)

            def softplus(q, s):
                u, k = divmod(s, KD)
                o = s % 2
                a.wait_ge(dtu_ready, NSEC * q + max(s, 0))
                for c in range(NCH):
                    n = NCH * s + c
                    sl = slice(c * CH, (c + 1) * CH)
                    a.wait_ge(step_done, NSEC * NCH * q + n + 1)
                    a.activation(dt[o][:, sl], pD[n % 2][:, 0:CH], ACT.Relu, bias=db[:, u, k:k + 1])
                    a.activation(tmp[:, sl], pD[n % 2][:, 0:CH], ACT.Abs, bias=db[:, u, k:k + 1]).then_inc(step_evac, 1)
                a.wait_ge(step_evac, NSEC * NCH * q + NCH * (s + 1))
                a.activation(tmp[:, :], tmp[:, :], ACT.Exp, scale=-1.0).then_inc(exp_taken, 1)
                a.wait_ge(exp_taken, NSEC * q + s + 1)
                a.activation(tmp[:, :], tmp[:, :], ACT.Ln, bias=1.0).then_inc(log_taken, 1)

            def decay(q, e):
                s, n = divmod(e, NST)
                u, k = divmod(s, KD)
                if n == 0:
                    a.wait_ge(dt_ready, NSEC * q + s + 1)
                a.wait_ge(scanned, NIT * q + max(e - 1, 0))
                src = dt[s % 2][:, :]
                dst = da[e % 2][:, :]
                if k % 2:
                    src = src.rearrange("p (h w) -> p w h", w=W)
                    dst = dst.rearrange("p (w h) -> p w h", h=H)
                a.activation(dst, src, ACT.Exp, scale=al[:, u, NST * k + n:NST * k + n + 1]).then_inc(decay_ready, 1)

            with a.Fori(0, NP2) as q:
                softplus(q, 0)
                for s in range(NSEC):
                    if s % KD == 0:
                        begin(q, s // KD)
                    decay(q, NST * s)
                    decay(q, NST * s + 1)
                    if s + 1 < NSEC:
                        softplus(q, s + 1)
                    decay(q, NST * s + 2)
                    decay(q, NST * s + 3)

        @block.vector
        def _(v):
            v.wait_ge(par_loaded, 80)
            v.tensor_reduce(dsum[:, :], dsk[:, :, :], AX.X, ALU.add).then_inc(a_ready, 1)
            v.wait_ge(a_exp, 1)
            v.tensor_scalar(al[:, :, :], al[:, :, :], -1.0, None, ALU.mult).then_inc(a_ready, 1)
            with v.Fori(0, NP2) as q:
                for e in range(NIT):
                    s, n = divmod(e, NST)
                    k = s % KD
                    if n == 0:
                        v.wait_ge(dtu_ready, NSEC * q + s + 1)
                    v.wait_ge(c_used, NB * q + NCH * e)
                    for c in range(NCH):
                        j = NCH * e + c
                        v.wait_ge(b_spread, NB * q + j + 1)
                        v.tensor_tensor(chunk(dbu[:, :], c, k), img(dtu[s % 2][:, c * CH:(c + 1) * CH]), img(pB[j % 3][:, 0:CH]),
                                        ALU.mult).then_inc(b_used, 1)
                    v.wait_ge(decay_ready, NIT * q + e + 1)
                    v.wait_ge(b_used, NB * q + NCH * (e + 1))
                    v.tensor_tensor_scan(along(dbu, k), along(da[e % 2], k), along(dbu, k), 0.0, ALU.mult, ALU.add).then_inc(scanned, 1)
                    v.wait_ge(scanned, NIT * q + e + 1)
                    for c in range(NCH):
                        j = NCH * e + c
                        v.wait_ge(c_spread, NB * q + j + 1)
                        v.wait_ge(y_added, NB * q + max(j - RP + 1, 0))
                        v.tensor_tensor(img(prod[:, j % RP, :]), chunk(dbu[:, :], c, k), img(pC[j % 3][:, 0:CH]), ALU.mult).then_inc(c_used, 1)

        @block.gpsimd
        def _(p):
            def step_size(q, s):
                p.wait_ge(log_taken, NSEC * q + s + 1)
                p.tensor_tensor(dt[s % 2][:, :], dt[s % 2][:, :], tmp[:, :], ALU.add).then_inc(dt_ready, 1)

            def step_input(q, s):
                p.wait_ge(dt_ready, NSEC * q + s + 1)
                p.wait_ge(x_loaded[s // KD], 16 * (q + 1))
                p.wait_ge(b_used, NB * q + NCH * NST * max(s - 1, 0))
                p.tensor_tensor(dtu[s % 2][:, :], dt[s % 2][:, :], xt[s // KD][:, :], ALU.mult).then_inc(dtu_ready, 1)

            with p.Fori(0, NP2) as q:
                step_size(q, 0)
                step_input(q, 0)
                for e in range(NIT):
                    s, n = divmod(e, NST)
                    u, k = divmod(s, KD)
                    if k == 0 and n == 0:
                        p.wait_ge(y_begun, 3 * q + u + 1)
                    for c in range(NCH):
                        j = NCH * e + c
                        p.wait_ge(c_used, NB * q + j + 1)
                        p.wait_ge(y_added, NB * q + max(j - NCH + 1, 0))
                        y = yt[u % 2][:, c * CH:(c + 1) * CH]
                        p.tensor_tensor(y, y, prod[:, j % RP, :], ALU.add).then_inc(y_added, 1)
                    if n == 1 and s + 1 < NSEC:
                        step_size(q, s + 1)
                    if n == 1 and s + 1 < NSEC:
                        step_input(q, s + 1)
                    if k == KD - 1 and n == NST - 1:
                        p.wait_ge(y_added, NB * q + NCH * (e + 1))
                        p.sem_inc(tick, 1)
                        p.dma_start(yv[q, u], yt[u % 2][:, :]).then_inc(stored[u % 2], 16)
            p.wait_ge(stored[0], 16 * 2 * NP2)
            p.wait_ge(stored[1], 16 * NP2)


def bc_selector():
    import numpy as np
    return np.tile(np.eye(NBC, dtype=mybir.dt.np(BF16)), (3, 1))


def network(nc, a, s, out):
    batchnorm_qkv(nc, a["x"], a["bn_gamma"], a["bn_beta"], a["qkv1_wT"], a["qkv1_b"], s["qkvp"])
    window_attention(nc, s["qkvp"], a["dm_wT"], a["dm_b"], a["rel_bias"], a["tap_sel"], a["ident"], s["att"])
    mixer(nc, a["x"], s["att"], a["proj1_wT"], a["proj1_b"], a["c1_wT"], a["c1_b"], a["c2_wT"], a["c2_b"], s["x1p"], s["xp"])
    channel_gate(nc, s["x1p"], s["xp"], a["wg1T"], a["bn2"], a["wg2T"], a["bg2"], a["beta"], a["w1T"], a["bn1"],
                 a["basis"], a["chan"], a["ident"], s["gate"])
    window_strips(nc, s["x1p"], s["gate"], a["inside"], a["n1g"], a["n1b"], a["qkv2_wT"], a["qkv2_b"], a["tempr"],
                  a["biasT"], a["proj2_wT"], a["proj2_b"], a["ident"], s["pout"])
    forward_block(nc, s["x1p"], s["gate"], s["pout"], a["hft_w"], a["hft_b"], a["n2g"], a["n2b"], a["fc1_wT"], a["fc1_b"],
                  a["sgn_g"], a["sgn_b"], a["sg_w"], a["sg_b"], a["fc2_wT"], a["fc2_b"], a["ident"], s["x3"])
    scan_inputs(nc, s["x3"], a["ln_w"], a["ln_b"], a["in_wT"], a["conv_w"], a["conv_b"], a["dts_wT"], a["bc_wT"],
                s["xc"], s["zs"], s["dts"], s["bcs"])
    scans(nc, s["xc"], s["dts"], s["bcs"], a["dt_wT"], a["dt_b"], a["a_log"], a["ds"], a["bc_sel"], s["ys"])
    scan_outputs(nc, s["x3"], s["ys"], s["zs"], a["on_w"], a["on_b"], a["out_wT"], out)


def kernel(**inputs):
    import numpy as np
    import concourse.bacc as bacc
    from concourse.bass_utils import run_bass_kernel_spmd

    v = {name: np.asarray(value) for name, value in inputs.items()}
    l0 = {name[8:]: a for name, a in v.items() if name.startswith("L0_conv_")}
    l1 = {name[8:]: a for name, a in v.items() if name.startswith("L1_conv_")}
    l2 = {name[8:]: a for name, a in v.items() if name.startswith("L2_conv_")}
    l3 = {name[8:]: a for name, a in v.items() if name.startswith("L3_conv_")}
    two = lambda a: np.tile(a, (2, 1))
    laid = dict(
        x=v["x"],
        bn_gamma=l0["bn_gamma"], bn_beta=l0["bn_beta"], qkv1_wT=l0["qkv_w"].T, qkv1_b=l0["qkv_b"],
        dm_wT=l0["dm_w"].transpose(1, 2, 3, 0), dm_b=l0["dm_b"], rel_bias=l0["rel_bias"], tap_sel=selector(),
        proj1_wT=l0["proj_w"].T, proj1_b=l0["proj_b"], c1_wT=l0["c1_w"].T, c1_b=l0["c1_b"],
        c2_wT=l0["c2_w"].T, c2_b=l0["c2_b"],
        wg1T=l1["wg1"].T, bn2=np.stack([l1["bn2_g"], l1["bn2_b"], l1["bn2_m"], l1["bn2_v"]]), wg2T=l1["wg2"].T,
        bg2=l1["bg2"], beta=l1["beta"], w1T=l1["w1d"][:, :, 1].T,
        bn1=np.stack([l1["bn1_g"], l1["bn1_b"], l1["bn1_m"], l1["bn1_v"], l1["b1d"]]),
        basis=dct_basis(), chan=channels(), ident=np.eye(128, dtype=np.float32), inside=inside(),
        n1g=l2["n1g"], n1b=l2["n1b"], qkv2_wT=l2["qkv_w"].T, qkv2_b=l2["qkv_b"],
        tempr=np.repeat(l2["temp"].reshape(HEADS), HD), biasT=relative(l2["rpb"]),
        proj2_wT=l2["proj_w"].T, proj2_b=l2["proj_b"],
        hft_w=l2["hft_w"].reshape(C, 9), hft_b=l2["hft_b"], n2g=l2["n2g"], n2b=l2["n2b"],
        fc1_wT=l2["fc1_w"].T, fc1_b=l2["fc1_b"], sgn_g=l2["sgn_g"], sgn_b=l2["sgn_b"],
        sg_w=l2["sg_w"].reshape(HID // 2, 9), sg_b=l2["sg_b"], fc2_wT=l2["fc2_w"].T, fc2_b=l2["fc2_b"],
        ln_w=l3["ln_w"], ln_b=l3["ln_b"], in_wT=l3["in_proj_w"].T, conv_w=l3["conv_w"].reshape(C, 9), conv_b=l3["conv_b"],
        dts_wT=l3["x_proj_w"][:, :RANK].reshape(KD * RANK, C).T, bc_wT=l3["x_proj_w"][:, RANK:].reshape(NBC, C).T,
        dt_wT=l3["dt_proj_w"].transpose(0, 2, 1), dt_b=two(l3["dt_proj_b"].T),
        a_log=two(l3["A_log"].transpose(1, 0, 2).reshape(C, KD * NST)), ds=two(l3["Ds"].T), bc_sel=bc_selector(),
        on_w=l3["out_norm_w"], on_b=l3["out_norm_b"], out_wT=l3["out_proj_w"].T,
    )
    between = dict(
        qkvp=((3, B * C, PW, PW), F32), att=((B * C, N), F32), x1p=((B * C, PW, PW), F32), xp=((B * C, DCT * DCT), F32),
        gate=((G, 2 * B), F32), pout=((B * C, NR * STEP, PW), F32), x3=((B * C, N), F32),
        xc=((B * C, N), F32), zs=((B * C, N), F32), dts=((B, KD * RANK, N), F32), bcs=((B, 3 * NBC, N), BF16),
        ys=((B * C, N), F32),
    )
    nc = bacc.Bacc("TRN2", target_bir_lowering=False, num_devices=1)
    arrays, args = {}, {}
    for name, a in laid.items():
        arrays[f"in_{name}"] = np.ascontiguousarray(a)
        args[name] = nc.dram_tensor(f"in_{name}", a.shape, mybir.dt.from_np(a.dtype), kind="ExternalInput").ap()
    scratch = {name: nc.dram_tensor(f"mid_{name}", shape, dt, kind="Internal").ap() for name, (shape, dt) in between.items()}
    out = nc.dram_tensor("out_y", (B, C, H, W), F32, kind="ExternalOutput").ap()
    network(nc, args, scratch, out)
    r = run_bass_kernel_spmd(nc, [arrays], core_ids=[0])
    return r.results[0]["out_y"]
```
